# Optimizing a Trainium2 kernel written in Bass

```python
import numpy as np
import jax
import jax.numpy as jnp

def _softmax(x, axis=-1):
    return jax.nn.softmax(x, axis=axis)

def _gelu(x):
    return jax.nn.gelu(x, approximate=True)

def _silu(x):
    return jax.nn.silu(x)

def _sigmoid(x):
    return jax.nn.sigmoid(x)

def _layernorm(x, axis=-1, eps=1e-05):
    m = jnp.mean(x, axis=axis, keepdims=True)
    v = jnp.var(x, axis=axis, keepdims=True)
    return (x - m) / jnp.sqrt(v + eps)

def _scatter_add(tgt, idx, src, axis=0):
    return tgt.at[idx].add(src)

def _segment_sum(src, seg, n):
    return jax.ops.segment_sum(src, seg, n)
kernel_name = 'mk_hybrid_d2_jaxref_r8_324cd5'

def setup_inputs(seed: int=0):
    np.random.seed(seed)
    _w = jnp.asarray

    def _L0_attn_a_setup():
        import jax, jax.numpy as jnp
        import numpy as np
        N_HEAD = 16
        BUCKET = 64
        HIDDEN = 128
        EPS = 1e-05

        def _ln(x, g, b):
            m = x.mean(-1, keepdims=True)
            v = x.var(-1, keepdims=True)
            return (x - m) * jax.lax.rsqrt(v + EPS) * g + b
        key = jax.random.key(seed)
        ks = jax.random.split(key, 6)

        def w(k, shape, s=0.02):
            return jax.random.normal(k, shape, jnp.float32) * s
        C = HIDDEN
        return {'x': jax.random.normal(ks[0], (4, 1024, C), jnp.float32), 'ln1_g': jnp.ones((C,), jnp.float32), 'ln1_b': jnp.zeros((C,), jnp.float32), 'w_qkv': w(ks[1], (C, 3 * C)), 'b_qkv': jnp.zeros((3 * C,), jnp.float32), 'w_out': w(ks[2], (C, C)), 'b_out': jnp.zeros((C,), jnp.float32), 'ln2_g': jnp.ones((C,), jnp.float32), 'ln2_b': jnp.zeros((C,), jnp.float32), 'w1': w(ks[3], (C, 4 * C)), 'b1': jnp.zeros((4 * C,), jnp.float32), 'w2': w(ks[4], (4 * C, C)), 'b2': jnp.zeros((C,), jnp.float32)}
    _L0_attn_a_in = _L0_attn_a_setup()

    def _L0_attn_b_setup():
        import jax, jax.numpy as jnp
        import numpy as np
        D_MODEL = 128
        D_INNER = 256
        D_STATE = 16
        D_CONV = 4
        DT_RANK = 64
        N_EXPERTS = 8
        TOP_K = 2
        FFN = 512
        EPS = 1e-05

        def rmsnorm(x, w):
            return x * jax.lax.rsqrt(jnp.mean(x * x, axis=-1, keepdims=True) + EPS) * w

        def mamba_block(x, in_proj_w, conv_w, conv_b, x_proj_w, dt_proj_w, dt_proj_b, A_log, D_skip, out_proj_w):
            B, L, _ = x.shape
            xz = x @ in_proj_w
            xi, z = jnp.split(xz, 2, axis=-1)
            xc = jax.lax.conv_general_dilated(xi.transpose(0, 2, 1), conv_w, window_strides=(1,), padding=[(D_CONV - 1, 0)], feature_group_count=D_INNER, dimension_numbers=('NCH', 'OIH', 'NCH'))
            xi = jax.nn.silu(xc.transpose(0, 2, 1) + conv_b)
            dbc = xi @ x_proj_w
            delta = jax.nn.softplus(dbc[..., :DT_RANK] @ dt_proj_w + dt_proj_b)
            Bm = dbc[..., DT_RANK:DT_RANK + D_STATE]
            Cm = dbc[..., DT_RANK + D_STATE:]
            A = -jnp.exp(A_log)

            def step(h, inp):
                d_t, B_t, C_t, x_t = inp
                dA = jnp.exp(d_t[..., None] * A)
                h = dA * h + (d_t * x_t)[..., None] * B_t[:, None, :]
                y = jnp.einsum('ben,bn->be', h, C_t)
                return (h, y)
            h0 = jnp.zeros((B, D_INNER, D_STATE), dtype=x.dtype)
            xs = (delta.transpose(1, 0, 2), Bm.transpose(1, 0, 2), Cm.transpose(1, 0, 2), xi.transpose(1, 0, 2))
            _, ys = jax.lax.scan(step, h0, xs)
            y = ys.transpose(1, 0, 2) + D_skip * xi
            y = y * jax.nn.silu(z)
            return y @ out_proj_w

        def moe_block(x, router_w, Wg, Wu, Wd):
            B, L, D = x.shape
            hs = x.reshape(-1, D)
            router_logits = hs @ router_w
            rw = jax.nn.softmax(router_logits.astype(jnp.float32), axis=-1)
            top_w, sel = jax.lax.top_k(rw, TOP_K)
            top_w = top_w.astype(hs.dtype)
            out = jnp.zeros_like(hs)
            for e in range(N_EXPERTS):
                w_e = jnp.where(sel == e, top_w, 0.0).sum(axis=-1)
                ye = jax.nn.silu(hs @ Wg[e]) * (hs @ Wu[e]) @ Wd[e]
                out = out + w_e[:, None] * ye
            return (out.reshape(B, L, D), router_logits)
        key = jax.random.key(seed)
        ks = jax.random.split(key, 16)
        s = 0.02
        inp = {'hidden_states': jax.random.normal(ks[0], (2, 256, D_MODEL), jnp.float32), 'rms1_w': jnp.ones((D_MODEL,), jnp.float32), 'rms2_w': jnp.ones((D_MODEL,), jnp.float32), 'in_proj_w': jax.random.normal(ks[1], (D_MODEL, 2 * D_INNER), jnp.float32) * s, 'conv_w': jax.random.normal(ks[2], (D_INNER, 1, D_CONV), jnp.float32) * s, 'conv_b': jnp.zeros((D_INNER,), jnp.float32), 'x_proj_w': jax.random.normal(ks[3], (D_INNER, DT_RANK + 2 * D_STATE), jnp.float32) * s, 'dt_proj_w': jax.random.normal(ks[4], (DT_RANK, D_INNER), jnp.float32) * s, 'dt_proj_b': jnp.zeros((D_INNER,), jnp.float32), 'A_log': jnp.log(jnp.tile(jnp.arange(1, D_STATE + 1, dtype=jnp.float32), (D_INNER, 1))), 'D_skip': jnp.ones((D_INNER,), jnp.float32), 'out_proj_w': jax.random.normal(ks[5], (D_INNER, D_MODEL), jnp.float32) * s, 'router_w': jax.random.normal(ks[6], (D_MODEL, N_EXPERTS), jnp.float32) * s, 'Wg': jax.random.normal(ks[7], (N_EXPERTS, D_MODEL, FFN), jnp.float32) * s, 'Wu': jax.random.normal(ks[8], (N_EXPERTS, D_MODEL, FFN), jnp.float32) * s, 'Wd': jax.random.normal(ks[9], (N_EXPERTS, FFN, D_MODEL), jnp.float32) * s}
        return inp
    _L0_attn_b_in = _L0_attn_b_setup()

    def _L0_ffn_setup():
        import jax, jax.numpy as jnp
        import numpy as np
        DIM = 128
        DEPTH = 2
        HEADS = 8
        DIM_HEAD = 64
        WINDOW = 64
        INNER = HEADS * DIM_HEAD
        HID = int(DIM * 4 * 2 / 3)
        B, N = (2, 1024)
        QK_SCALE = 8.0

        def shift_token(t):
            t1, t2 = jnp.split(t, 2, axis=-1)
            t2 = jnp.pad(t2, ((0, 0), (1, 0), (0, 0)))[:, :-1]
            return jnp.concatenate([t1, t2], axis=-1)

        def l2norm(t):
            return t / jnp.clip(jnp.linalg.norm(t, axis=-1, keepdims=True), 1e-12)

        def rotate_half(x):
            x1, x2 = jnp.split(x, 2, axis=-1)
            return jnp.concatenate([-x2, x1], axis=-1)

        def rotary_xpos(q, k):
            n = q.shape[-2]
            half_idx = jnp.arange(0, DIM_HEAD, 2, dtype=jnp.float32)
            inv_freq = 1.0 / 10000.0 ** (half_idx / DIM_HEAD)
            t = jnp.arange(n, dtype=jnp.float32)
            freqs = t[:, None] * inv_freq[None, :]
            freqs = jnp.concatenate([freqs, freqs], axis=-1)
            base = (half_idx + 0.4 * DIM_HEAD) / (1.4 * DIM_HEAD)
            power = (t - n // 2) / float(WINDOW // 2)
            scale = base[None, :] ** power[:, None]
            scale = jnp.concatenate([scale, scale], axis=-1)
            cos, sin = (jnp.cos(freqs), jnp.sin(freqs))
            q = q * cos * scale + rotate_half(q) * sin * scale
            k = k * cos / scale + rotate_half(k) * sin / scale
            return (q, k)

        def local_attention(q, k, v):
            b, h, n, d = q.shape
            w = n // WINDOW
            bq = q.reshape(b, h, w, WINDOW, d) * QK_SCALE
            bk = k.reshape(b, h, w, WINDOW, d)
            bv = v.reshape(b, h, w, WINDOW, d)

            def look_around(t):
                p = jnp.pad(t, ((0, 0), (0, 0), (1, 0), (0, 0), (0, 0)))
                return jnp.concatenate([p[:, :, :w], p[:, :, 1:]], axis=3)
            bk, bv = (look_around(bk), look_around(bv))
            bt = jnp.arange(n).reshape(w, WINDOW)
            btp = jnp.pad(bt, ((1, 0), (0, 0)), constant_values=-1)
            btk = jnp.concatenate([btp[:w], btp[1:]], axis=1)
            sim = jnp.einsum('bhwid,bhwjd->bhwij', bq, bk)
            i = bt[:, :, None]
            j = btk[:, None, :]
            mask = (i < j) | (i > j + WINDOW) | (j == -1)
            sim = jnp.where(mask, -jnp.finfo(sim.dtype).max, sim)
            attn = jax.nn.softmax(sim, axis=-1)
            out = jnp.einsum('bhwij,bhwjd->bhwid', attn, bv)
            return out.reshape(b, h, n, d)

        def _layer(x, wqkv, qs, ksc, wo, lg, lb, w1, b1, w2, b2):
            b, n, _ = x.shape
            h = shift_token(x)
            qkv = h @ wqkv
            q, k, v = jnp.split(qkv, 3, axis=-1)
            to_heads = lambda t: t.reshape(b, n, HEADS, DIM_HEAD).transpose(0, 2, 1, 3)
            q, k, v = (to_heads(q), to_heads(k), to_heads(v))
            q = l2norm(q) * qs
            k = l2norm(k) * ksc
            q, k = rotary_xpos(q, k)
            o = local_attention(q, k, v)
            o = o.transpose(0, 2, 1, 3).reshape(b, n, INNER)
            x = x + o @ wo
            h = shift_token(x)
            mu = h.mean(-1, keepdims=True)
            var = h.var(-1, keepdims=True)
            h = (h - mu) / jnp.sqrt(var + 1e-05) * lg + lb
            h = h @ w1 + b1
            a, g = jnp.split(h, 2, axis=-1)
            h = a * jax.nn.gelu(g, approximate=False)
            x = x + h @ w2 + b2
            return x
        key = jax.random.key(seed)
        ks = jax.random.split(key, 6)
        return {'x': jax.random.normal(ks[0], (B, N, DIM), jnp.float32), 'wqkv': jax.random.normal(ks[1], (DEPTH, DIM, 3 * INNER), jnp.float32) * 0.02, 'q_scale': jnp.ones((DEPTH, DIM_HEAD), jnp.float32), 'k_scale': jnp.ones((DEPTH, DIM_HEAD), jnp.float32), 'wo': jax.random.normal(ks[2], (DEPTH, INNER, DIM), jnp.float32) * 0.02, 'ln_g': jnp.ones((DEPTH, DIM), jnp.float32), 'ln_b': jnp.zeros((DEPTH, DIM), jnp.float32), 'w1': jax.random.normal(ks[3], (DEPTH, DIM, 2 * HID), jnp.float32) * 0.02, 'b1': jnp.zeros((DEPTH, 2 * HID), jnp.float32), 'w2': jax.random.normal(ks[4], (DEPTH, HID, DIM), jnp.float32) * 0.02, 'b2': jnp.zeros((DEPTH, DIM), jnp.float32)}
    _L0_ffn_in = _L0_ffn_setup()

    def _L1_attn_a_setup():
        import jax, jax.numpy as jnp
        import numpy as np
        E = 128
        H = 16
        D = E // H
        WIN = 32
        STRIDE = 128
        G = 1
        B = 2
        L = 4097
        key = jax.random.key(seed)
        ks = jax.random.split(key, 9)
        s = 0.02
        return {'hidden_states': jax.random.normal(ks[0], (B, L, E), jnp.float32), 'Wq': jax.random.normal(ks[1], (E, E), jnp.float32) * s, 'bq': jnp.zeros((E,), jnp.float32), 'Wk': jax.random.normal(ks[2], (E, E), jnp.float32) * s, 'bk': jnp.zeros((E,), jnp.float32), 'Wv': jax.random.normal(ks[3], (E, E), jnp.float32) * s, 'bv': jnp.zeros((E,), jnp.float32), 'Wo': jax.random.normal(ks[4], (E, E), jnp.float32) * s, 'bo': jnp.zeros((E,), jnp.float32)}
    _L1_attn_a_in = _L1_attn_a_setup()

    def _L1_attn_b_setup():
        import jax, jax.numpy as jnp
        import numpy as np
        N_HEADS = 16
        D_MODEL = 128
        D_HEAD = 64
        BATCH = 4
        SEQ = 256
        IGNORE = -100000.0
        key = jax.random.key(seed)
        ks = jax.random.split(key, 10)
        s = 1.0 / np.sqrt(D_MODEL)
        return {'x': jax.random.normal(ks[0], (BATCH, SEQ, D_MODEL), jnp.float32), 'pos_embed': jax.random.normal(ks[1], (BATCH, SEQ, D_MODEL), jnp.float32), 'W_Q': jax.random.normal(ks[2], (N_HEADS, D_MODEL, D_HEAD), jnp.float32) * s, 'b_Q': jnp.zeros((N_HEADS, D_HEAD), jnp.float32), 'W_K': jax.random.normal(ks[3], (N_HEADS, D_MODEL, D_HEAD), jnp.float32) * s, 'b_K': jnp.zeros((N_HEADS, D_HEAD), jnp.float32), 'W_V': jax.random.normal(ks[4], (N_HEADS, D_MODEL, D_HEAD), jnp.float32) * s, 'b_V': jnp.zeros((N_HEADS, D_HEAD), jnp.float32), 'W_O': jax.random.normal(ks[5], (N_HEADS, D_HEAD, D_MODEL), jnp.float32) * (1.0 / np.sqrt(D_HEAD)), 'b_O': jnp.zeros((D_MODEL,), jnp.float32)}
    _L1_attn_b_in = _L1_attn_b_setup()

    def _L1_ffn_setup():
        import jax, jax.numpy as jnp
        import numpy as np
        E = 16
        K = 4
        G = 4
        TG = 2
        NS = 2
        H = 128
        I = 176
        SCALE = 1.0

        def _gate(x2d, gate_w, gate_bias):
            T = x2d.shape[0]
            logits = x2d.astype(jnp.float32) @ gate_w.astype(jnp.float32).T
            scores = jax.nn.sigmoid(logits)
            sfc = scores + gate_bias[None, :]
            grp = sfc.reshape(T, G, E // G)
            top2, _ = jax.lax.top_k(grp, 2)
            group_scores = top2.sum(-1)
            _, gidx = jax.lax.top_k(group_scores, TG)
            gmask = jnp.zeros((T, G), sfc.dtype).at[jnp.arange(T)[:, None], gidx].set(1.0)
            smask = jnp.repeat(gmask, E // G, axis=1) > 0
            tmp = jnp.where(smask, sfc, 0.0)
            _, topk_idx = jax.lax.top_k(tmp, K)
            topk_w = jnp.take_along_axis(scores, topk_idx, axis=1)
            topk_w = topk_w / (topk_w.sum(-1, keepdims=True) + 1e-20)
            return (topk_idx, topk_w * SCALE)
        key = jax.random.key(seed)
        ks = jax.random.split(key, 8)
        bound = 1.0 / np.sqrt(H)
        return {'hidden_states': jax.random.normal(ks[0], (1, 128, H), jnp.float32), 'gate_w': jax.random.uniform(ks[1], (E, H), jnp.float32, -bound, bound), 'gate_bias': jnp.zeros((E,), jnp.float32), 'gate_proj': jax.random.normal(ks[2], (E, I, H), jnp.float32) * 0.02, 'up_proj': jax.random.normal(ks[3], (E, I, H), jnp.float32) * 0.02, 'down_proj': jax.random.normal(ks[4], (E, H, I), jnp.float32) * 0.02, 'shared_gate_w': jax.random.normal(ks[5], (I * NS, H), jnp.float32) * 0.02, 'shared_up_w': jax.random.normal(ks[6], (I * NS, H), jnp.float32) * 0.02, 'shared_down_w': jax.random.normal(ks[7], (H, I * NS), jnp.float32) * 0.02}
    _L1_ffn_in = _L1_ffn_setup()
    _d = {'L0_attn_a_x': _L0_attn_a_in['x'], 'L0_attn_a_ln1_g': _L0_attn_a_in['ln1_g'], 'L0_attn_a_ln1_b': _L0_attn_a_in['ln1_b'], 'L0_attn_a_w_qkv': _L0_attn_a_in['w_qkv'], 'L0_attn_a_b_qkv': _L0_attn_a_in['b_qkv'], 'L0_attn_a_w_out': _L0_attn_a_in['w_out'], 'L0_attn_a_b_out': _L0_attn_a_in['b_out'], 'L0_attn_a_ln2_g': _L0_attn_a_in['ln2_g'], 'L0_attn_a_ln2_b': _L0_attn_a_in['ln2_b'], 'L0_attn_a_w1': _L0_attn_a_in['w1'], 'L0_attn_a_b1': _L0_attn_a_in['b1'], 'L0_attn_a_w2': _L0_attn_a_in['w2'], 'L0_attn_a_b2': _L0_attn_a_in['b2'], 'L0_attn_b_rms1_w': _L0_attn_b_in['rms1_w'], 'L0_attn_b_rms2_w': _L0_attn_b_in['rms2_w'], 'L0_attn_b_in_proj_w': _L0_attn_b_in['in_proj_w'], 'L0_attn_b_conv_w': _L0_attn_b_in['conv_w'], 'L0_attn_b_conv_b': _L0_attn_b_in['conv_b'], 'L0_attn_b_x_proj_w': _L0_attn_b_in['x_proj_w'], 'L0_attn_b_dt_proj_w': _L0_attn_b_in['dt_proj_w'], 'L0_attn_b_dt_proj_b': _L0_attn_b_in['dt_proj_b'], 'L0_attn_b_A_log': _L0_attn_b_in['A_log'], 'L0_attn_b_D_skip': _L0_attn_b_in['D_skip'], 'L0_attn_b_out_proj_w': _L0_attn_b_in['out_proj_w'], 'L0_attn_b_router_w': _L0_attn_b_in['router_w'], 'L0_attn_b_Wg': _L0_attn_b_in['Wg'], 'L0_attn_b_Wu': _L0_attn_b_in['Wu'], 'L0_attn_b_Wd': _L0_attn_b_in['Wd'], 'L0_ffn_wqkv': _L0_ffn_in['wqkv'], 'L0_ffn_q_scale': _L0_ffn_in['q_scale'], 'L0_ffn_k_scale': _L0_ffn_in['k_scale'], 'L0_ffn_wo': _L0_ffn_in['wo'], 'L0_ffn_ln_g': _L0_ffn_in['ln_g'], 'L0_ffn_ln_b': _L0_ffn_in['ln_b'], 'L0_ffn_w1': _L0_ffn_in['w1'], 'L0_ffn_b1': _L0_ffn_in['b1'], 'L0_ffn_w2': _L0_ffn_in['w2'], 'L0_ffn_b2': _L0_ffn_in['b2'], 'L1_attn_a_Wq': _L1_attn_a_in['Wq'], 'L1_attn_a_bq': _L1_attn_a_in['bq'], 'L1_attn_a_Wk': _L1_attn_a_in['Wk'], 'L1_attn_a_bk': _L1_attn_a_in['bk'], 'L1_attn_a_Wv': _L1_attn_a_in['Wv'], 'L1_attn_a_bv': _L1_attn_a_in['bv'], 'L1_attn_a_Wo': _L1_attn_a_in['Wo'], 'L1_attn_a_bo': _L1_attn_a_in['bo'], 'L1_attn_b_pos_embed': _L1_attn_b_in['pos_embed'], 'L1_attn_b_W_Q': _L1_attn_b_in['W_Q'], 'L1_attn_b_b_Q': _L1_attn_b_in['b_Q'], 'L1_attn_b_W_K': _L1_attn_b_in['W_K'], 'L1_attn_b_b_K': _L1_attn_b_in['b_K'], 'L1_attn_b_W_V': _L1_attn_b_in['W_V'], 'L1_attn_b_b_V': _L1_attn_b_in['b_V'], 'L1_attn_b_W_O': _L1_attn_b_in['W_O'], 'L1_attn_b_b_O': _L1_attn_b_in['b_O'], 'L1_ffn_gate_w': _L1_ffn_in['gate_w'], 'L1_ffn_gate_bias': _L1_ffn_in['gate_bias'], 'L1_ffn_gate_proj': _L1_ffn_in['gate_proj'], 'L1_ffn_up_proj': _L1_ffn_in['up_proj'], 'L1_ffn_down_proj': _L1_ffn_in['down_proj'], 'L1_ffn_shared_gate_w': _L1_ffn_in['shared_gate_w'], 'L1_ffn_shared_up_w': _L1_ffn_in['shared_up_w'], 'L1_ffn_shared_down_w': _L1_ffn_in['shared_down_w']}
    _x0 = _d['L0_attn_a_x']
    _d['L0_attn_a_x'] = jax.random.normal(jax.random.fold_in(jax.random.key(seed), 1), (8, 256, 128), dtype=_x0.dtype)
    del _x0
    return _d

def reference(L0_attn_a_x, L0_attn_a_ln1_g, L0_attn_a_ln1_b, L0_attn_a_w_qkv, L0_attn_a_b_qkv, L0_attn_a_w_out, L0_attn_a_b_out, L0_attn_a_ln2_g, L0_attn_a_ln2_b, L0_attn_a_w1, L0_attn_a_b1, L0_attn_a_w2, L0_attn_a_b2, L0_attn_b_rms1_w, L0_attn_b_rms2_w, L0_attn_b_in_proj_w, L0_attn_b_conv_w, L0_attn_b_conv_b, L0_attn_b_x_proj_w, L0_attn_b_dt_proj_w, L0_attn_b_dt_proj_b, L0_attn_b_A_log, L0_attn_b_D_skip, L0_attn_b_out_proj_w, L0_attn_b_router_w, L0_attn_b_Wg, L0_attn_b_Wu, L0_attn_b_Wd, L0_ffn_wqkv, L0_ffn_q_scale, L0_ffn_k_scale, L0_ffn_wo, L0_ffn_ln_g, L0_ffn_ln_b, L0_ffn_w1, L0_ffn_b1, L0_ffn_w2, L0_ffn_b2, L1_attn_a_Wq, L1_attn_a_bq, L1_attn_a_Wk, L1_attn_a_bk, L1_attn_a_Wv, L1_attn_a_bv, L1_attn_a_Wo, L1_attn_a_bo, L1_attn_b_pos_embed, L1_attn_b_W_Q, L1_attn_b_b_Q, L1_attn_b_W_K, L1_attn_b_b_K, L1_attn_b_W_V, L1_attn_b_b_V, L1_attn_b_W_O, L1_attn_b_b_O, L1_ffn_gate_w, L1_ffn_gate_bias, L1_ffn_gate_proj, L1_ffn_up_proj, L1_ffn_down_proj, L1_ffn_shared_gate_w, L1_ffn_shared_up_w, L1_ffn_shared_down_w):

    def _L0_attn_a_ref(x, ln1_g, ln1_b, w_qkv, b_qkv, w_out, b_out, ln2_g, ln2_b, w1, b1, w2, b2):
        import jax, jax.numpy as jnp
        import numpy as np
        N_HEAD = 16
        BUCKET = 64
        HIDDEN = 128
        EPS = 1e-05

        def _ln(x, g, b):
            m = x.mean(-1, keepdims=True)
            v = x.var(-1, keepdims=True)
            return (x - m) * jax.lax.rsqrt(v + EPS) * g + b
        B, T, C = x.shape
        nb = T // BUCKET
        hd = C // N_HEAD
        scale = 1.0 / np.sqrt(hd)
        h = _ln(x, ln1_g, ln1_b)
        qkv = h @ w_qkv + b_qkv
        q, k, v = jnp.split(qkv, 3, axis=-1)

        def buck(t):
            return t.reshape(B, nb, BUCKET, N_HEAD, hd)
        qb, kb, vb = (buck(q), buck(k), buck(v))
        kp = jnp.concatenate([jnp.zeros_like(kb[:, :1]), kb[:, :-1]], axis=1)
        vp = jnp.concatenate([jnp.zeros_like(vb[:, :1]), vb[:, :-1]], axis=1)
        kc = jnp.concatenate([kp, kb], axis=2)
        vc = jnp.concatenate([vp, vb], axis=2)
        scores = jnp.einsum('bnihd,bnjhd->bnhij', qb, kc) * scale
        i = jnp.arange(BUCKET)[:, None]
        j = jnp.arange(2 * BUCKET)[None, :]
        mask = (j < BUCKET) | (j - BUCKET <= i)
        scores = jnp.where(mask, scores, -jnp.inf)
        attn = jax.nn.softmax(scores, axis=-1)
        ob = jnp.einsum('bnhij,bnjhd->bnihd', attn, vc).reshape(B, T, C)
        x = x + ob @ w_out + b_out
        h2 = _ln(x, ln2_g, ln2_b)
        m = jax.nn.gelu(h2 @ w1 + b1, approximate=False) @ w2 + b2
        return x + m

    def _L0_attn_b_ref(hidden_states, rms1_w, rms2_w, in_proj_w, conv_w, conv_b, x_proj_w, dt_proj_w, dt_proj_b, A_log, D_skip, out_proj_w, router_w, Wg, Wu, Wd):
        import jax, jax.numpy as jnp
        import numpy as np
        D_MODEL = 128
        D_INNER = 256
        D_STATE = 16
        D_CONV = 4
        DT_RANK = 64
        N_EXPERTS = 8
        TOP_K = 2
        FFN = 512
        EPS = 1e-05

        def rmsnorm(x, w):
            return x * jax.lax.rsqrt(jnp.mean(x * x, axis=-1, keepdims=True) + EPS) * w

        def mamba_block(x, in_proj_w, conv_w, conv_b, x_proj_w, dt_proj_w, dt_proj_b, A_log, D_skip, out_proj_w):
            B, L, _ = x.shape
            xz = x @ in_proj_w
            xi, z = jnp.split(xz, 2, axis=-1)
            xc = jax.lax.conv_general_dilated(xi.transpose(0, 2, 1), conv_w, window_strides=(1,), padding=[(D_CONV - 1, 0)], feature_group_count=D_INNER, dimension_numbers=('NCH', 'OIH', 'NCH'))
            xi = jax.nn.silu(xc.transpose(0, 2, 1) + conv_b)
            dbc = xi @ x_proj_w
            delta = jax.nn.softplus(dbc[..., :DT_RANK] @ dt_proj_w + dt_proj_b)
            Bm = dbc[..., DT_RANK:DT_RANK + D_STATE]
            Cm = dbc[..., DT_RANK + D_STATE:]
            A = -jnp.exp(A_log)

            def step(h, inp):
                d_t, B_t, C_t, x_t = inp
                dA = jnp.exp(d_t[..., None] * A)
                h = dA * h + (d_t * x_t)[..., None] * B_t[:, None, :]
                y = jnp.einsum('ben,bn->be', h, C_t)
                return (h, y)
            h0 = jnp.zeros((B, D_INNER, D_STATE), dtype=x.dtype)
            xs = (delta.transpose(1, 0, 2), Bm.transpose(1, 0, 2), Cm.transpose(1, 0, 2), xi.transpose(1, 0, 2))
            _, ys = jax.lax.scan(step, h0, xs)
            y = ys.transpose(1, 0, 2) + D_skip * xi
            y = y * jax.nn.silu(z)
            return y @ out_proj_w

        def moe_block(x, router_w, Wg, Wu, Wd):
            B, L, D = x.shape
            hs = x.reshape(-1, D)
            router_logits = hs @ router_w
            rw = jax.nn.softmax(router_logits.astype(jnp.float32), axis=-1)
            top_w, sel = jax.lax.top_k(rw, TOP_K)
            top_w = top_w.astype(hs.dtype)
            out = jnp.zeros_like(hs)
            for e in range(N_EXPERTS):
                w_e = jnp.where(sel == e, top_w, 0.0).sum(axis=-1)
                ye = jax.nn.silu(hs @ Wg[e]) * (hs @ Wu[e]) @ Wd[e]
                out = out + w_e[:, None] * ye
            return (out.reshape(B, L, D), router_logits)
        residual = hidden_states
        h = rmsnorm(hidden_states, rms1_w)
        h = mamba_block(h, in_proj_w, conv_w, conv_b, x_proj_w, dt_proj_w, dt_proj_b, A_log, D_skip, out_proj_w)
        h = residual + h
        residual = h
        h = rmsnorm(h, rms2_w)
        h, router_logits = moe_block(h, router_w, Wg, Wu, Wd)
        h = residual + h
        return h

    def _L0_ffn_ref(x, wqkv, q_scale, k_scale, wo, ln_g, ln_b, w1, b1, w2, b2):
        import jax, jax.numpy as jnp
        import numpy as np
        DIM = 128
        DEPTH = 2
        HEADS = 8
        DIM_HEAD = 64
        WINDOW = 64
        INNER = HEADS * DIM_HEAD
        HID = int(DIM * 4 * 2 / 3)
        B, N = (2, 1024)
        QK_SCALE = 8.0

        def shift_token(t):
            t1, t2 = jnp.split(t, 2, axis=-1)
            t2 = jnp.pad(t2, ((0, 0), (1, 0), (0, 0)))[:, :-1]
            return jnp.concatenate([t1, t2], axis=-1)

        def l2norm(t):
            return t / jnp.clip(jnp.linalg.norm(t, axis=-1, keepdims=True), 1e-12)

        def rotate_half(x):
            x1, x2 = jnp.split(x, 2, axis=-1)
            return jnp.concatenate([-x2, x1], axis=-1)

        def rotary_xpos(q, k):
            n = q.shape[-2]
            half_idx = jnp.arange(0, DIM_HEAD, 2, dtype=jnp.float32)
            inv_freq = 1.0 / 10000.0 ** (half_idx / DIM_HEAD)
            t = jnp.arange(n, dtype=jnp.float32)
            freqs = t[:, None] * inv_freq[None, :]
            freqs = jnp.concatenate([freqs, freqs], axis=-1)
            base = (half_idx + 0.4 * DIM_HEAD) / (1.4 * DIM_HEAD)
            power = (t - n // 2) / float(WINDOW // 2)
            scale = base[None, :] ** power[:, None]
            scale = jnp.concatenate([scale, scale], axis=-1)
            cos, sin = (jnp.cos(freqs), jnp.sin(freqs))
            q = q * cos * scale + rotate_half(q) * sin * scale
            k = k * cos / scale + rotate_half(k) * sin / scale
            return (q, k)

        def local_attention(q, k, v):
            b, h, n, d = q.shape
            w = n // WINDOW
            bq = q.reshape(b, h, w, WINDOW, d) * QK_SCALE
            bk = k.reshape(b, h, w, WINDOW, d)
            bv = v.reshape(b, h, w, WINDOW, d)

            def look_around(t):
                p = jnp.pad(t, ((0, 0), (0, 0), (1, 0), (0, 0), (0, 0)))
                return jnp.concatenate([p[:, :, :w], p[:, :, 1:]], axis=3)
            bk, bv = (look_around(bk), look_around(bv))
            bt = jnp.arange(n).reshape(w, WINDOW)
            btp = jnp.pad(bt, ((1, 0), (0, 0)), constant_values=-1)
            btk = jnp.concatenate([btp[:w], btp[1:]], axis=1)
            sim = jnp.einsum('bhwid,bhwjd->bhwij', bq, bk)
            i = bt[:, :, None]
            j = btk[:, None, :]
            mask = (i < j) | (i > j + WINDOW) | (j == -1)
            sim = jnp.where(mask, -jnp.finfo(sim.dtype).max, sim)
            attn = jax.nn.softmax(sim, axis=-1)
            out = jnp.einsum('bhwij,bhwjd->bhwid', attn, bv)
            return out.reshape(b, h, n, d)

        def _layer(x, wqkv, qs, ksc, wo, lg, lb, w1, b1, w2, b2):
            b, n, _ = x.shape
            h = shift_token(x)
            qkv = h @ wqkv
            q, k, v = jnp.split(qkv, 3, axis=-1)
            to_heads = lambda t: t.reshape(b, n, HEADS, DIM_HEAD).transpose(0, 2, 1, 3)
            q, k, v = (to_heads(q), to_heads(k), to_heads(v))
            q = l2norm(q) * qs
            k = l2norm(k) * ksc
            q, k = rotary_xpos(q, k)
            o = local_attention(q, k, v)
            o = o.transpose(0, 2, 1, 3).reshape(b, n, INNER)
            x = x + o @ wo
            h = shift_token(x)
            mu = h.mean(-1, keepdims=True)
            var = h.var(-1, keepdims=True)
            h = (h - mu) / jnp.sqrt(var + 1e-05) * lg + lb
            h = h @ w1 + b1
            a, g = jnp.split(h, 2, axis=-1)
            h = a * jax.nn.gelu(g, approximate=False)
            x = x + h @ w2 + b2
            return x
        for l in range(DEPTH):
            x = _layer(x, wqkv[l], q_scale[l], k_scale[l], wo[l], ln_g[l], ln_b[l], w1[l], b1[l], w2[l], b2[l])
        return x

    def _L1_attn_a_ref(hidden_states, Wq, bq, Wk, bk, Wv, bv, Wo, bo):
        import jax, jax.numpy as jnp
        import numpy as np
        E = 128
        H = 16
        D = E // H
        WIN = 32
        STRIDE = 128
        G = 1
        B = 2
        L = 4097
        b, seq_len, e = hidden_states.shape
        scale = 1.0 / jnp.sqrt(jnp.asarray(D, hidden_states.dtype))
        q = (hidden_states @ Wq + bq).reshape(b, seq_len, H, D)
        k = (hidden_states @ Wk + bk).reshape(b, seq_len, H, D)
        v = (hidden_states @ Wv + bv).reshape(b, seq_len, H, D)
        qg = q[:, :G]
        gw = jnp.einsum('bghd,bshd->bhgs', qg, k) * scale
        gp = jax.nn.softmax(gw, axis=-1)
        gctx = jnp.einsum('bhgs,bshd->bghd', gp, v).reshape(b, G, e)
        ql, kl, vl = (q[:, G:], k[:, G:], v[:, G:])
        Lc = seq_len - G
        num_windows = max(1, (Lc - WIN) // STRIDE + 1)
        starts = jnp.arange(num_windows) * STRIDE
        widx = starts[:, None] + jnp.arange(WIN)
        qw = ql[:, widx]
        kw = kl[:, widx]
        vw = vl[:, widx]
        aw = jnp.einsum('bwqhd,bwkhd->bwhqk', qw, kw) * scale
        ap = jax.nn.softmax(aw, axis=-1)
        ctx = jnp.einsum('bwhqk,bwkhd->bwqhd', ap, vw)
        ctx = ctx.reshape(b, num_windows * WIN, e)
        flat = widx.reshape(-1)
        local = jnp.zeros((b, Lc, e), hidden_states.dtype).at[:, flat].add(ctx)
        counts = jnp.zeros((Lc,), hidden_states.dtype).at[flat].add(1.0)
        counts = jnp.maximum(counts, 1.0)
        local = local / counts[None, :, None]
        out = jnp.concatenate([gctx, local], axis=1)
        return out @ Wo + bo

    def _L1_attn_b_ref(x, pos_embed, W_Q, b_Q, W_K, b_K, W_V, b_V, W_O, b_O):
        import jax, jax.numpy as jnp
        import numpy as np
        N_HEADS = 16
        D_MODEL = 128
        D_HEAD = 64
        BATCH = 4
        SEQ = 256
        IGNORE = -100000.0
        q = jnp.einsum('bpm,imh->bpih', x, W_Q) + b_Q
        k = jnp.einsum('bpm,imh->bpih', x, W_K) + b_K
        v = jnp.einsum('bpm,imh->bpih', x, W_V) + b_V
        attn_scale = np.sqrt(D_HEAD).astype(np.float32)
        scores = jnp.einsum('bpih,bqih->bipq', q, k) / attn_scale
        S = x.shape[1]
        causal = jnp.tril(jnp.ones((S, S), dtype=bool))
        scores = jnp.where(causal, scores, jnp.float32(IGNORE))
        attn = jax.nn.softmax(scores, axis=-1)
        z = jnp.einsum('bpih,biqp->bqih', v, attn)
        out = jnp.einsum('bqih,ihm->bqm', z, W_O) + b_O
        return out

    def _L1_ffn_ref(hidden_states, gate_w, gate_bias, gate_proj, up_proj, down_proj, shared_gate_w, shared_up_w, shared_down_w):
        import jax, jax.numpy as jnp
        import numpy as np
        E = 16
        K = 4
        G = 4
        TG = 2
        NS = 2
        H = 128
        I = 176
        SCALE = 1.0

        def _gate(x2d, gate_w, gate_bias):
            T = x2d.shape[0]
            logits = x2d.astype(jnp.float32) @ gate_w.astype(jnp.float32).T
            scores = jax.nn.sigmoid(logits)
            sfc = scores + gate_bias[None, :]
            grp = sfc.reshape(T, G, E // G)
            top2, _ = jax.lax.top_k(grp, 2)
            group_scores = top2.sum(-1)
            _, gidx = jax.lax.top_k(group_scores, TG)
            gmask = jnp.zeros((T, G), sfc.dtype).at[jnp.arange(T)[:, None], gidx].set(1.0)
            smask = jnp.repeat(gmask, E // G, axis=1) > 0
            tmp = jnp.where(smask, sfc, 0.0)
            _, topk_idx = jax.lax.top_k(tmp, K)
            topk_w = jnp.take_along_axis(scores, topk_idx, axis=1)
            topk_w = topk_w / (topk_w.sum(-1, keepdims=True) + 1e-20)
            return (topk_idx, topk_w * SCALE)
        orig_shape = hidden_states.shape
        x = hidden_states.reshape(-1, H)
        topk_idx, topk_w = _gate(x, gate_w, gate_bias)
        combine_w = (jax.nn.one_hot(topk_idx, E, dtype=x.dtype) * topk_w[..., None]).sum(1)
        g = jnp.einsum('th,eih->tei', x, gate_proj)
        u = jnp.einsum('th,eih->tei', x, up_proj)
        act = jax.nn.silu(g) * u
        y = jnp.einsum('tei,ehi,te->th', act, down_proj, combine_w)
        sg = x @ shared_gate_w.T
        su = x @ shared_up_w.T
        y = y + jax.nn.silu(sg) * su @ shared_down_w.T
        return y.reshape(orig_shape)
    x = L0_attn_a_x
    x = x + _L0_attn_a_ref(_layernorm(x, axis=-1), L0_attn_a_ln1_g, L0_attn_a_ln1_b, L0_attn_a_w_qkv, L0_attn_a_b_qkv, L0_attn_a_w_out, L0_attn_a_b_out, L0_attn_a_ln2_g, L0_attn_a_ln2_b, L0_attn_a_w1, L0_attn_a_b1, L0_attn_a_w2, L0_attn_a_b2)
    x = x + _L0_ffn_ref(_layernorm(x, axis=-1), L0_ffn_wqkv, L0_ffn_q_scale, L0_ffn_k_scale, L0_ffn_wo, L0_ffn_ln_g, L0_ffn_ln_b, L0_ffn_w1, L0_ffn_b1, L0_ffn_w2, L0_ffn_b2)
    x = x + _L0_attn_b_ref(_layernorm(x, axis=-1), L0_attn_b_rms1_w, L0_attn_b_rms2_w, L0_attn_b_in_proj_w, L0_attn_b_conv_w, L0_attn_b_conv_b, L0_attn_b_x_proj_w, L0_attn_b_dt_proj_w, L0_attn_b_dt_proj_b, L0_attn_b_A_log, L0_attn_b_D_skip, L0_attn_b_out_proj_w, L0_attn_b_router_w, L0_attn_b_Wg, L0_attn_b_Wu, L0_attn_b_Wd)
    x = x + _L0_ffn_ref(_layernorm(x, axis=-1), L0_ffn_wqkv, L0_ffn_q_scale, L0_ffn_k_scale, L0_ffn_wo, L0_ffn_ln_g, L0_ffn_ln_b, L0_ffn_w1, L0_ffn_b1, L0_ffn_w2, L0_ffn_b2)
    x = x + _L1_attn_a_ref(_layernorm(x, axis=-1), L1_attn_a_Wq, L1_attn_a_bq, L1_attn_a_Wk, L1_attn_a_bk, L1_attn_a_Wv, L1_attn_a_bv, L1_attn_a_Wo, L1_attn_a_bo)
    x = x + _L1_ffn_ref(_layernorm(x, axis=-1), L1_ffn_gate_w, L1_ffn_gate_bias, L1_ffn_gate_proj, L1_ffn_up_proj, L1_ffn_down_proj, L1_ffn_shared_gate_w, L1_ffn_shared_up_w, L1_ffn_shared_down_w)
    x = x + _L1_attn_b_ref(_layernorm(x, axis=-1), L1_attn_b_pos_embed, L1_attn_b_W_Q, L1_attn_b_b_Q, L1_attn_b_W_K, L1_attn_b_b_K, L1_attn_b_W_V, L1_attn_b_b_V, L1_attn_b_W_O, L1_attn_b_b_O)
    x = x + _L1_ffn_ref(_layernorm(x, axis=-1), L1_ffn_gate_w, L1_ffn_gate_bias, L1_ffn_gate_proj, L1_ffn_up_proj, L1_ffn_down_proj, L1_ffn_shared_gate_w, L1_ffn_shared_up_w, L1_ffn_shared_down_w)
    return x

_drawn_inputs = setup_inputs


def setup_inputs(seed=0):
    import zlib

    import numpy as np

    out = dict(_drawn_inputs(seed))
    spreads = {'L0_attn_a_ln1_g': (1.0, 0.6),
     'L0_attn_a_ln1_b': (0.0, 0.8),
     'L0_attn_a_b_qkv': (0.0, 0.719),
     'L0_attn_a_b_out': (0.0, 0.1),
     'L0_attn_a_ln2_g': (1.0, 0.6),
     'L0_attn_a_ln2_b': (0.0, 0.8),
     'L0_attn_a_b1': (0.0, 0.584),
     'L0_attn_a_b2': (0.0, 0.1),
     'L0_attn_b_rms1_w': (1.0, 0.6),
     'L0_attn_b_rms2_w': (1.0, 0.6),
     'L0_attn_b_conv_b': (0.0, 0.8),
     'L0_attn_b_dt_proj_b': (0.0, 0.8),
     'L0_attn_b_D_skip': (1.0, 0.6),
     'L0_ffn_q_scale': (1.0, 0.6),
     'L0_ffn_k_scale': (1.0, 0.6),
     'L0_ffn_ln_g': (1.0, 0.6),
     'L0_ffn_ln_b': (0.0, 0.8),
     'L0_ffn_b1': (0.0, 0.8),
     'L0_ffn_b2': (0.0, 0.1),
     'L1_attn_a_bq': (0.0, 2.0),
     'L1_attn_a_bk': (0.0, 2.0),
     'L1_attn_a_bv': (0.0, 2.0),
     'L1_attn_a_bo': (0.0, 2.0),
     'L1_attn_b_b_Q': (0.0, 2.0),
     'L1_attn_b_b_K': (0.0, 2.0),
     'L1_attn_b_b_V': (0.0, 0.8),
     'L1_attn_b_b_O': (0.0, 2.0),
     'L1_ffn_gate_bias': (0.0, 0.8)}
    factors = {'L0_attn_a_w_qkv': 8.0,
     'L0_attn_a_w_out': 4.717,
     'L0_attn_b_in_proj_w': 8.0,
     'L0_attn_b_conv_w': 8.0,
     'L0_attn_b_x_proj_w': 8.0,
     'L0_attn_b_dt_proj_w': 8.0,
     'L0_attn_b_A_log': 8.0,
     'L0_attn_b_out_proj_w': 8.0,
     'L0_attn_b_router_w': 8.0,
     'L0_attn_b_Wg': 8.0,
     'L0_attn_b_Wu': 8.0,
     'L0_attn_b_Wd': 8.0,
     'L0_ffn_w1': 5.688,
     'L0_ffn_w2': 5.545,
     'L1_attn_a_Wq': 22.776,
     'L1_attn_a_Wk': 21.4,
     'L1_attn_a_Wv': 8.0,
     'L1_attn_a_Wo': 8.0,
     'L1_ffn_gate_w': 8.0,
     'L1_ffn_gate_proj': 8.0,
     'L1_ffn_up_proj': 8.0,
     'L1_ffn_down_proj': 8.0,
     'L1_ffn_shared_gate_w': 8.0,
     'L1_ffn_shared_up_w': 8.0,
     'L1_ffn_shared_down_w': 8.0,
     'L1_attn_b_W_Q': 3.904,
     'L1_attn_b_W_K': 3.406}
    for name, (base, spread) in spreads.items():
        noise = np.random.default_rng([zlib.crc32(name.encode()), seed]).standard_normal(out[name].shape)
        drawn = base * np.exp(spread * noise) if base else spread * noise
        out[name] = jnp.asarray(drawn.astype(out[name].dtype))
    for name, factor in factors.items():
        out[name] = (out[name] * factor).astype(out[name].dtype)
    return out
```

```python
from collections import namedtuple
from contextlib import ExitStack

import numpy as np
import concourse.bass as bass
from concourse import mybir

F32 = mybir.dt.float32
BF16 = mybir.dt.bfloat16
ALU = mybir.AluOpType
ACT = mybir.ActivationFunctionType
AX = mybir.AxisListType.X

P = 128
SEQS, LEN = 8, 256
TOK = SEQS * LEN
GROUP = 512
TILES = TOK // P
EPS = 1e-5
MASKED = -1e30

A_HEADS, A_DIM = 16, 8
F_HEADS, F_DIM = 8, 64
D_HEADS, D_DIM = 16, 64
HID_F, HIDP_F = 341, 384
N_EXP, FFN = 8, 512
E2, I2, SHARED = 16, 176, 352
ROUTED = E2 * I2
D_INNER, STATE, DT_RANK = 256, 16, 64

COLS = {
    "k": dict(ident=P, mean=P, pairs=P, rot=P, qcos=LEN, qsin=LEN, kcos=LEN, ksin=LEN,
              m_bucket=384, m_local=384, m_causal=384, m_window=384, heads8=16,
              floor=1, extra=1, seen=2, eps=1, one=1, back=1, before8=64, before16=256),
    "a": dict(g1=1, c1=1, wqkv=384, bq=1, bk=1, bv=P, wo=P, bo=1, g2=1, c2=1, w1=512, b1=4, w2=512, b2=1),
    "f": dict(wqkv0=1536, qs0=1, ks0=1, wo0=512, g0=1, c0=1, w10=682, ba0=3, bg0=3, w20=384, b20=1,
              wqkv1=1536, qs1=1, ks1=1, wo1=512, g1=1, c1=1, w11=682, ba1=3, bg1=3, w21=384, b21=1),
    "m": dict(r1=1, r2=1, win=512, cw=8, cb=2, wx=192, wdt=256, bdt=2, alog=32, dskip=2, wout=256, router=8),
    "e": dict(wg=4096, wu=4096, wd=4096),
    "h": dict(wg=ROUTED + SHARED, wu=ROUTED + SHARED, wd=25 * P, expert=ROUTED),
    "g": dict(gate=E2, bias=E2),
    "c": dict(wq=P, wk=P, wv=P, wo=P, bq=1, bk=1, bv=P, bo=1),
    "d": dict(wq=1024, wk=1024, wv=1024, wo=1024, bq=8, bk=8, bv=1024, bo=1),
}


def starts(group):
    at, out = 0, {}
    for name, width in COLS[group].items():
        out[name] = at
        at += width
    return out, at


def span(signals):
    return range(signals[0].num, signals[-1].num + 1)


class Order:

    def __init__(self, eng, sem):
        self.eng, self.sem, self.n = eng, sem, 0

    def step(self, ins):
        self.n += 1
        ins.then_inc(self.sem, 1)
        self.eng.wait_ge(self.sem, self.n)


class Net:

    def __init__(self, nc, ctx):
        self.nc, self.ctx, self.sets, self.tensors = nc, ctx, {}, 0

    def sbuf(self, name, shape, dt=F32, ctx=None):
        self.tensors += 1
        return (ctx or self.ctx).enter_context(self.nc.sbuf_tensor(f"{name}_{self.tensors}", shape, dt))

    def psum(self, name, shape, ctx):
        self.tensors += 1
        return ctx.enter_context(self.nc.psum_tensor(f"{name}_{self.tensors}", shape, F32))

    def signals(self, kind, names):
        if kind not in self.sets:
            got = [self.ctx.enter_context(self.nc.semaphore(f"{kind}_{n}")) for n in names]
            nums = [s.num for s in got]
            assert nums == list(range(nums[0], nums[0] + len(nums))), nums
            self.sets[kind] = namedtuple(f"Signals_{kind}", names)(*got)
        return self.sets[kind]

    def w(self, group, name, a=0, b=None, rows=P):
        at, _ = starts(group)
        lo = at[name]
        hi = lo + (COLS[group][name] if b is None else b)
        return self.weights[group][0:rows, lo + a:hi]


def norm(net, tag, src, dst, root_mean_square=False, gain=None, bias=None, shift=False):
    nc = net.nc
    chunks = TOK // GROUP
    s = net.signals("norm", ["shifted", "mean_ready", "centred", "squared", "var_ready", "std_ready", "steps", "act_steps"])
    with ExitStack() as ctx:
        moved = net.sbuf("n_moved", [P, TOK], ctx=ctx) if shift else src
        centred = net.sbuf("n_centred", [P, TOK], ctx=ctx) if not root_mean_square else src
        squared = net.sbuf("n_squared", [P, TOK], ctx=ctx)
        std = net.sbuf("n_std", [P, TOK], ctx=ctx)
        mean_ps = net.psum("n_mean", [P, chunks, GROUP], ctx)
        var_ps = net.psum("n_var", [P, chunks, GROUP], ctx)
        ones = net.w("k", "mean")

        def cut(t, c):
            return t[:, c * GROUP:(c + 1) * GROUP]

        with nc.Block(no_gpsimd_drain=True) as block:
            @block.gpsimd
            def _(pool):
                if shift:
                    half = P // 2
                    by_seq = moved[half:P, :].rearrange("p (s t) -> p s t", s=SEQS)
                    src_seq = src[half:P, :].rearrange("p (s t) -> p s t", s=SEQS)
                    pool.tensor_copy(moved[0:half, :], src[0:half, :]).then_inc(s.shifted, 1)
                    pool.memset(by_seq[:, :, 0:1], 0.0).then_inc(s.shifted, 1)
                    pool.tensor_copy(by_seq[:, :, 1:LEN], src_seq[:, :, 0:LEN - 1]).then_inc(s.shifted, 1)

            @block.tensor
            def _(pe):
                if shift:
                    pe.wait_ge(s.shifted, 3)
                if not root_mean_square:
                    for c in range(chunks):
                        pe.matmul(mean_ps[:, c, :], ones, cut(moved, c), start=True, stop=True)\
                          .then_inc(s.mean_ready, 1)
                for c in range(chunks):
                    pe.wait_ge(s.squared, c + 1)
                    pe.matmul(var_ps[:, c, :], ones, cut(squared, c), start=True, stop=True)\
                      .then_inc(s.var_ready, 1)

            @block.scalar
            def _(act):
                order = Order(act, s.act_steps)
                for c in range(chunks):
                    if not root_mean_square:
                        act.wait_ge(s.centred, c + 1)
                    act.activation(cut(squared, c), cut(centred, c), ACT.Square).then_inc(s.squared, 1)
                for c in range(chunks):
                    act.wait_ge(s.var_ready, c + 1)
                    order.step(act.activation(cut(std, c), var_ps[:, c, :], ACT.Ln, bias=net.w("k", "eps")))
                    act.activation(cut(std, c), cut(std, c), ACT.Exp, scale=-0.5).then_inc(s.std_ready, 1)

            @block.vector
            def _(dve):
                if shift:
                    dve.wait_ge(s.shifted, 3)
                if not root_mean_square:
                    for c in range(chunks):
                        dve.wait_ge(s.mean_ready, c + 1)
                        dve.tensor_tensor(cut(centred, c), cut(moved, c), mean_ps[:, c, :], ALU.subtract)\
                           .then_inc(s.centred, 1)
                    dve.wait_ge(s.centred, chunks)
                order = Order(dve, s.steps)
                for c in range(chunks):
                    dve.wait_ge(s.std_ready, c + 1)
                    done = dve.tensor_tensor(cut(dst, c), cut(centred, c), cut(std, c), ALU.mult)
                    if gain is not None:
                        order.step(done)
                        if bias is None:
                            dve.tensor_scalar(cut(dst, c), cut(dst, c), gain, None, ALU.mult)
                        else:
                            dve.tensor_scalar(cut(dst, c), cut(dst, c), gain, bias, ALU.mult, ALU.add)
        nc.all_engine_barrier(sems_to_clear=span(s))


def mlp(net, src, dst, chunks, func, out_bias=None, also=None, shares=None):
    nc = net.nc
    s = net.signals("mlp", ["x_ready", "gate_ready", "up_ready", "act_done", "hidden_ready", "down_done", "steps"])
    n_chunks = len(chunks)
    gated = chunks[0]["up"] is not None
    numbers, matrices, last_use = [], [], {}
    for c, lot in enumerate(chunks):
        m = lot.get("share")
        if m is None:
            numbers.append(None)
            continue
        if lot["share_key"] not in last_use:
            matrices.append(m)
        last_use[lot["share_key"]] = c
        numbers.append(len(matrices) - 1)
    last_chunk = list(last_use.values())
    with ExitStack() as ctx:
        xin = net.sbuf("f_xin", [P, GROUP], ctx=ctx)
        acted = net.sbuf("f_acted", [P, 2, GROUP], ctx=ctx)
        shared = net.sbuf("f_shared", [P, 2, GROUP], ctx=ctx)
        hidden = net.sbuf("f_hidden", [P, 2, GROUP], ctx=ctx)
        total = net.sbuf("f_total", [P, GROUP], ctx=ctx)
        share_in = net.sbuf("f_share_in", [E2, GROUP], ctx=ctx)
        gate_ps = net.psum("f_gate", [P, 2, GROUP], ctx)
        up_ps = net.psum("f_up", [P, 2, GROUP], ctx)
        share_ps = net.psum("f_share", [P, 2, GROUP], ctx)
        out_ps = net.psum("f_out", [P, GROUP], ctx)
        n_share = shares.shape[0] if shares is not None else 0

        def down(pe, c):
            pe.wait_ge(s.hidden_ready, c + 1)
            rows = chunks[c]["rows"]
            pe.matmul(out_ps[:, :], chunks[c]["down"], hidden[0:rows, c % 2, :],
                      start=(c == 0), stop=(c == n_chunks - 1)).then_inc(s.down_done, 1)

        with nc.Fori(0, TOK // GROUP) as i:
            with nc.Block(no_gpsimd_drain=True) as block:
                @block.tensor
                def _(pe):
                    pe.wait_ge(s.x_ready, 1)
                    for c, lot in enumerate(chunks):
                        rows, b = lot["rows"], c % 2
                        if c >= 2:
                            pe.wait_ge(s.act_done if gated else s.hidden_ready, c - 1)
                        pe.matmul(gate_ps[0:rows, b, :], lot["gate"], xin[:, :], start=True, stop=True)\
                          .then_inc(s.gate_ready, 1)
                        if gated:
                            if c >= 2:
                                pe.wait_ge(s.hidden_ready, c - 1)
                            k = numbers[c]
                            if k is not None and (c == 0 or numbers[c - 1] != k):
                                if k >= 2:
                                    pe.wait_ge(s.hidden_ready, last_chunk[k - 2] + 1)
                                pe.matmul(share_ps[:, k % 2, :], matrices[k], share_in[0:n_share, :],
                                          start=True, stop=True)
                            pe.matmul(up_ps[0:rows, b, :], lot["up"], xin[:, :], start=True, stop=True)\
                              .then_inc(s.up_ready, 1)
                        if c >= 1:
                            down(pe, c - 1)
                    down(pe, n_chunks - 1)

                @block.scalar
                def _(act):
                    for c, lot in enumerate(chunks):
                        rows, b = lot["rows"], c % 2
                        act.wait_ge(s.gate_ready, c + 1)
                        bias = lot.get("gate_bias")
                        more = {} if bias is None else {"bias": bias}
                        if gated:
                            if c >= 2:
                                act.wait_ge(s.hidden_ready, c - 1)
                            act.activation(acted[0:rows, b, :], gate_ps[0:rows, b, :], func, **more)\
                               .then_inc(s.act_done, 1)
                        else:
                            if c >= 2:
                                act.wait_ge(s.down_done, c - 1)
                            act.activation(hidden[0:rows, b, :], gate_ps[0:rows, b, :], func, **more)\
                               .then_inc(s.hidden_ready, 1)

                @block.vector
                def _(dve):
                    order = Order(dve, s.steps)
                    if shares is not None:
                        order.step(dve.tensor_copy(share_in[0:n_share, :], shares[:, bass.ds(i * GROUP, GROUP)]))
                    dve.tensor_copy(xin[:, :], src[:, bass.ds(i * GROUP, GROUP)]).then_inc(s.x_ready, 1)
                    if gated:
                        for c, lot in enumerate(chunks):
                            rows, b = lot["rows"], c % 2
                            dve.wait_ge(s.act_done, c + 1)
                            dve.wait_ge(s.up_ready, c + 1)
                            left = acted[0:rows, b, :]
                            if numbers[c] is not None:
                                left = shared[0:rows, b, :]
                                order.step(dve.tensor_tensor(left, acted[0:rows, b, :],
                                                             share_ps[0:rows, numbers[c] % 2, :], ALU.mult))
                            if c >= 2:
                                dve.wait_ge(s.down_done, c - 1)
                            out = hidden[0:rows, b, :]
                            if lot.get("up_bias") is not None:
                                dve.scalar_tensor_tensor(out=out, in0=up_ps[0:rows, b, :], scalar=lot["up_bias"],
                                                         in1=left, op0=ALU.add, op1=ALU.mult)\
                                   .then_inc(s.hidden_ready, 1)
                            else:
                                dve.tensor_tensor(out, left, up_ps[0:rows, b, :], ALU.mult)\
                                   .then_inc(s.hidden_ready, 1)
                    dve.wait_ge(s.down_done, n_chunks)
                    here = dst[:, bass.ds(i * GROUP, GROUP)]
                    if out_bias is not None:
                        order.step(dve.tensor_scalar(total[:, :], out_ps[:, :], out_bias, None, ALU.add))
                    else:
                        order.step(dve.tensor_copy(total[:, :], out_ps[:, :]))
                    if also is not None:
                        order.step(dve.tensor_tensor(total[:, :], total[:, :],
                                                     also[:, bass.ds(i * GROUP, GROUP)], ALU.add))
                    dve.tensor_tensor(here, here, total[:, :], ALU.add)
            nc.all_engine_barrier(sems_to_clear=span(s))


def gate(net, src, shares, experts):
    nc = net.nc
    E, T = experts, TILES
    s = net.signals("gate", ["logits_ready", "scored", "steps", "chosen", "turned", "copied", "act_steps"])
    weights = net.w("m", "router") if E == N_EXP else net.w("g", "gate")
    with ExitStack() as ctx:
        x = net.sbuf("g_x", [P, T, E], ctx=ctx)
        y = net.sbuf("g_y", [P, T, E], ctx=ctx)
        rank = net.sbuf("g_rank", [P, T, E], ctx=ctx)
        more = net.sbuf("g_more", [P, T, E, E], ctx=ctx)
        same = net.sbuf("g_same", [P, T, E, E], ctx=ctx)
        row = net.sbuf("g_row", [P, T], ctx=ctx)
        z = net.sbuf("g_z", [P, T, E], ctx=ctx)
        pairs = net.sbuf("g_pairs", [P, T * 4, 6], ctx=ctx)
        groups = net.sbuf("g_groups", [P, T, 4], ctx=ctx)
        group_rank = net.sbuf("g_grank", [P, T, 4], ctx=ctx)
        logits = net.psum("g_logits", [P, T, E], ctx)
        turned = net.psum("g_turned", [E, TOK], ctx)

        def ranks(order, dve, v, out, n, before):
            big = more[:, :, :, :].rearrange("p t a b -> p t (a b)")[:, :, 0:n * n]\
                .rearrange("p t (a b) -> p t a b", a=n)
            eq = same[:, :, :, :].rearrange("p t a b -> p t (a b)")[:, :, 0:n * n]\
                .rearrange("p t (a b) -> p t a b", a=n)
            shape = [P, T, n, n]
            other = v.unsqueeze(2).to_broadcast(shape)
            own = v.unsqueeze(3).to_broadcast(shape)
            order.step(dve.tensor_tensor(big, other, own, ALU.is_gt))
            order.step(dve.tensor_tensor(eq, other, own, ALU.is_equal))
            order.step(dve.tensor_tensor(eq, eq, before.unsqueeze(1).to_broadcast(shape), ALU.mult))
            order.step(dve.tensor_tensor(big, big, eq, ALU.add))
            order.step(dve.tensor_reduce(out, big, AX, ALU.add))

        with nc.Block(no_gpsimd_drain=True) as block:
            @block.tensor
            def _(pe):
                for t in range(T):
                    last = pe.matmul(logits[:, t, :], src[:, t * P:(t + 1) * P], weights, start=True, stop=True)
                last.then_inc(s.logits_ready, 1)
                pe.wait_ge(s.chosen, 1)
                for t in range(T):
                    last = pe.transpose(turned[:, t * P:(t + 1) * P], x[:, t, :], net.w("k", "ident"))
                last.then_inc(s.turned, 1)

            @block.scalar
            def _(act):
                if E == N_EXP:
                    act.wait_ge(s.steps, 2)
                    act.activation(y[:, :, :], x[:, :, :], ACT.Exp).then_inc(s.scored, 1)
                else:
                    act.wait_ge(s.logits_ready, 1)
                    act.activation(y[:, :, :], logits[:, :, :], ACT.Sigmoid).then_inc(s.scored, 1)

            @block.vector
            def _(dve):
                order = Order(dve, s.steps)
                shape = [P, T, E]

                def over(v):
                    return v.unsqueeze(2).to_broadcast(shape)

                dve.wait_ge(s.logits_ready, 1)
                if E == N_EXP:
                    order.step(dve.tensor_reduce(row[:, :], logits[:, :, :], AX, ALU.max))
                    order.step(dve.tensor_tensor(x[:, :, :], logits[:, :, :], over(row[:, :]), ALU.subtract))
                    dve.wait_ge(s.scored, 1)
                    order.step(dve.tensor_reduce(row[:, :], y[:, :, :], AX, ALU.add))
                    order.step(dve.reciprocal(row[:, :], row[:, :]))
                    order.step(dve.tensor_tensor(y[:, :, :], y[:, :, :], over(row[:, :]), ALU.mult))
                    ranks(order, dve, y[:, :, :], rank[:, :, :], E,
                          net.w("k", "before8").rearrange("p (a b) -> p a b", a=E))
                    order.step(dve.tensor_scalar(rank[:, :, :], rank[:, :, :], 2.0, None, ALU.is_lt))
                    dve.tensor_tensor(x[:, :, :], y[:, :, :], rank[:, :, :], ALU.mult).then_inc(s.chosen, 1)
                else:
                    dve.wait_ge(s.scored, 1)
                    order.step(dve.tensor_tensor(z[:, :, :], y[:, :, :],
                                                 net.w("g", "bias").unsqueeze(1).to_broadcast(shape), ALU.add))
                    four = z[:, :, :].rearrange("p t (g e) -> p (t g) e", g=4)
                    order.step(dve.tensor_tensor(pairs[:, :, 0:3], four[:, :, 0:3], four[:, :, 1:4], ALU.add))
                    order.step(dve.tensor_tensor(pairs[:, :, 3:5], four[:, :, 0:2], four[:, :, 2:4], ALU.add))
                    order.step(dve.tensor_tensor(pairs[:, :, 5:6], four[:, :, 0:1], four[:, :, 3:4], ALU.add))
                    order.step(dve.tensor_reduce(groups[:, :, :].rearrange("p t g -> p (t g)"),
                                                 pairs[:, :, :], AX, ALU.max))
                    before4 = net.w("k", "before16").rearrange("p (a b) -> p a b", a=16)[:, 0:4, 0:4]
                    ranks(order, dve, groups[:, :, :], group_rank[:, :, :], 4, before4)
                    order.step(dve.tensor_scalar(group_rank[:, :, :], group_rank[:, :, :], 2.0, None, ALU.is_lt))
                    spread = group_rank[:, :, :].rearrange("p t g -> p (t g)").unsqueeze(2)\
                        .to_broadcast([P, T * 4, 4])
                    order.step(dve.tensor_tensor(four, four, spread, ALU.mult))
                    ranks(order, dve, z[:, :, :], rank[:, :, :], E,
                          net.w("k", "before16").rearrange("p (a b) -> p a b", a=16))
                    order.step(dve.tensor_scalar(rank[:, :, :], rank[:, :, :], 4.0, None, ALU.is_lt))
                    order.step(dve.tensor_tensor(y[:, :, :], y[:, :, :], rank[:, :, :], ALU.mult))
                    order.step(dve.tensor_reduce(row[:, :], y[:, :, :], AX, ALU.add))
                    order.step(dve.tensor_scalar(row[:, :], row[:, :], 1e-20, None, ALU.add))
                    order.step(dve.reciprocal(row[:, :], row[:, :]))
                    dve.tensor_tensor(x[:, :, :], y[:, :, :], over(row[:, :]), ALU.mult).then_inc(s.chosen, 1)
                dve.wait_ge(s.turned, 1)
                dve.tensor_copy(shares, turned[:, :])
        nc.all_engine_barrier(sems_to_clear=span(s))


def attention(net, kind, src, dst, masks, scale, wq, wk, wv, wo, bq=None, bk=None, bv=None, bo=None,
              q_gain=None, k_gain=None):
    nc = net.nc
    small = kind in ("bucket", "window")
    rotary = kind == "local"
    heads = {"bucket": A_HEADS, "window": A_HEADS, "local": F_HEADS, "causal": D_HEADS}[kind]
    dim = A_DIM if small else D_DIM
    width = heads * dim
    parts = width // P
    lot = heads if small else 8
    lots = heads // lot
    lot_w = lot * dim
    lot_parts = lot_w // P
    v_w = min(width, GROUP)
    segs = [(0, [0, 1], 0), (1, [1], 256)] if kind == "window" else [(0, [0], 0), (1, [0, 1], 128)]
    places = [(q, k, at + P * n) for q, ks, at in segs for n, k in enumerate(ks)]
    s = net.signals("attn", [
        "x_ready", "q_ready", "q_read", "v_ready", "v_read", "k_spread", "qk_done", "scores_ready",
        "max_ready", "probs_ready", "turned", "turned_read", "out_ready", "out_scaled", "out_turned", "out_copied",
        "proj_ready", "vec_steps", "act_steps", "raw_ready", "rot_ready", "cos_done", "std_ready", "extra_ready", "norm_ready", "chain"])
    n_proj = 2 * parts
    n_v = 2 * (width // v_w)
    with ExitStack() as ctx:
        xs = net.sbuf("t_x", [P, LEN], ctx=ctx)
        qk = net.sbuf("t_qk", [P, n_proj, LEN], ctx=ctx)
        q_sb, k_sb = qk[:, 0:parts, :], qk[:, parts:, :]
        v_sb = net.sbuf("t_v", [P, 2, width], ctx=ctx)
        k_one = net.sbuf("t_kone", [P, heads, LEN], ctx=ctx) if small else None
        probs = net.sbuf("t_probs", [P, 2, 384], ctx=ctx)
        turned = net.sbuf("t_turned", [P, 2, 384], ctx=ctx)
        neg_max = net.sbuf("t_negmax", [P, heads, 2], ctx=ctx)
        sums = net.sbuf("t_sums", [P, heads, 2], ctx=ctx)
        zero_key = net.sbuf("t_zero", [P, heads], ctx=ctx)
        o_sb = net.sbuf("t_o", [P, 2, lot_w], ctx=ctx)
        o_t = net.sbuf("t_ot", [P, parts, LEN], ctx=ctx)
        if rotary:
            raw = net.sbuf("t_raw", [P, n_proj, LEN], ctx=ctx)
            sq = net.sbuf("t_sq", [P, n_proj, LEN], ctx=ctx)
            cosd = qk
            sind = net.sbuf("t_sin", [P, n_proj, LEN], ctx=ctx)
            std = sq
        pp = net.psum("t_pp", [P, 2, 512], ctx)
        sc = net.psum("t_sc", [P, 2, 512], ctx)
        tp = net.psum("t_tp", [P, 2, 512], ctx)
        op = net.psum("t_op", [P, 2, 512], ctx)
        otp = tp[:, :, :].rearrange("p a b -> p (a b)").rearrange("p (c t) -> p c t", c=4)
        ident = net.w("k", "ident")
        mask = masks

        def head_q(h, tile):
            if small:
                return q_sb[:, 0, tile * P:(tile + 1) * P]
            r = 64 * (h % 2)
            return q_sb[r:r + 64, h // 2, tile * P:(tile + 1) * P]

        def head_k(h, tiles):
            lo, hi = tiles[0] * P, (tiles[-1] + 1) * P
            if small:
                return k_one[:, h, lo:hi]
            r = 64 * (h % 2)
            return k_sb[r:r + 64, h // 2, lo:hi]

        with nc.Fori(0, SEQS) as i:
            with nc.Block(no_gpsimd_drain=True) as block:
                @block.tensor
                def _(pe):
                    pe.wait_ge(s.x_ready, 3 if rotary else 1)
                    for n in range(n_proj):
                        wt = (wq, wk)[n // parts]
                        if n >= 2:
                            pe.wait_ge(s.q_read, n - 1)
                        pe.matmul(pp[:, n % 2, 0:LEN], wt[:, (n % parts) * P:(n % parts + 1) * P], xs[:, :],
                                  start=True, stop=True).then_inc(s.q_ready, 1)
                    for n in range(n_v):
                        tile, c = n % 2, n // 2
                        if n < 2:
                            pe.wait_ge(s.q_read, n_proj - 1 + n)
                        else:
                            pe.wait_ge(s.v_read, n - 1)
                        pe.matmul(pp[:, n % 2, 0:v_w], xs[:, tile * P:(tile + 1) * P],
                                  wv[:, c * v_w:(c + 1) * v_w], start=True, stop=True).then_inc(s.v_ready, 1)
                    if rotary:
                        for n in range(n_proj):
                            pe.wait_ge(s.raw_ready, 2 * n + 2)
                            if n < 2:
                                pe.wait_ge(s.v_read, n + 1)
                            else:
                                pe.wait_ge(s.std_ready, n - 1)
                            pe.matmul(pp[:, n % 2, 0:LEN], net.w("k", "rot"), raw[:, n, :], start=True, stop=True)
                            pe.matmul(pp[:, n % 2, LEN:2 * LEN], net.w("k", "pairs"), sq[:, n, :],
                                      start=True, stop=True).then_inc(s.rot_ready, 1)
                    pe.wait_ge(s.v_read, n_v)
                    pe.wait_ge(s.qk_done, 1)

                    def scores(h):
                        if h >= 2:
                            pe.wait_ge(s.probs_ready, 2 * (h - 1))
                        pe.matmul(sc[:, h % 2, 0:384], net.ident16[:, :], mask[:, :], start=True, stop=False)
                        for q, ks, at in segs:
                            last = pe.matmul(sc[:, h % 2, at:at + P * len(ks)], head_q(h, q), head_k(h, ks),
                                             start=False, stop=(q == 1))
                        last.then_inc(s.scores_ready, 1)

                    def turn(h):
                        pe.wait_ge(s.probs_ready, 2 * (h + 1))
                        if h >= 2:
                            pe.wait_ge(s.turned_read, h - 1)
                        if h % lot < 2 and h >= lot:
                            pe.wait_ge(s.out_copied, h // lot)
                        for q, k, at in places:
                            last = pe.transpose(tp[:, h % 2, at:at + P], probs[:, h % 2, at:at + P], ident)
                        last.then_inc(s.turned, 1)

                    def mix(h):
                        pe.wait_ge(s.turned_read, h + 1)
                        j = h % lot
                        if j == 0 and h >= lot:
                            pe.wait_ge(s.out_scaled, 2 * (h // lot))
                        for q, ks, at0 in segs:
                            for n, k in enumerate(ks):
                                at = at0 + P * n
                                last = pe.matmul(op[:, q, j * dim:(j + 1) * dim], turned[:, h % 2, at:at + P],
                                                 v_sb[:, k, h * dim:(h + 1) * dim],
                                                 start=(n == 0), stop=(n == len(ks) - 1))
                        last.then_inc(s.out_ready, 1)

                    def turn_out(g):
                        pe.wait_ge(s.out_scaled, 2 * (g + 1))
                        pe.wait_ge(s.turned_read, min(heads, (g + 1) * lot))
                        for c in range(lot_parts):
                            for q in range(2):
                                last = pe.transpose(otp[:, c, q * P:(q + 1) * P],
                                                    o_sb[:, q, c * P:(c + 1) * P], ident)
                        last.then_inc(s.out_turned, 1)

                    for h in range(heads + 2):
                        if h >= lot and h % lot == 0:
                            turn(h - 1)
                            mix(h - 2)
                            mix(h - 1)
                            turn_out(h // lot - 1)
                            if h < heads:
                                scores(h)
                            continue
                        if h > heads:
                            continue
                        if h < heads:
                            scores(h)
                        if h >= 1 and (h - 1) // lot == h // lot:
                            turn(h - 1)
                        if h >= 2 and (h - 2) // lot == h // lot:
                            mix(h - 2)
                    pe.wait_ge(s.out_copied, lots)
                    for c in range(parts):
                        last = pe.matmul(pp[:, 0, 0:LEN], wo[:, c * P:(c + 1) * P], o_t[:, c, :],
                                         start=(c == 0), stop=(c == parts - 1))
                    last.then_inc(s.proj_ready, 1)

                @block.scalar
                def _(act):
                    if rotary:
                        for n in range(n_proj):
                            act.wait_ge(s.q_ready, n + 1)
                            act.activation(raw[:, n, :], pp[:, n % 2, 0:LEN], ACT.Copy,
                                           scale=(q_gain, k_gain)[n // parts]).then_inc(s.raw_ready, 1)
                            act.activation(sq[:, n, :], pp[:, n % 2, 0:LEN], ACT.Square)\
                               .then_inc(s.raw_ready, 1)
                        act.wait_ge(s.std_ready, n_proj)
                        flat = "p n t -> p (n t)"
                        order = Order(act, s.act_steps)
                        order.step(act.activation(std[:, :, :].rearrange(flat), std[:, :, :].rearrange(flat),
                                                  ACT.Ln, scale=float(2 ** 20)))
                        act.activation(std[:, :, :].rearrange(flat), std[:, :, :].rearrange(flat), ACT.Exp,
                                       scale=-0.5, bias=net.w("k", "back")).then_inc(s.norm_ready, 1)
                    for h in range(heads):
                        act.wait_ge(s.max_ready, h + 1)
                        if h >= 2:
                            act.wait_ge(s.turned, h - 1)
                        for n, (q, ks, at) in enumerate(segs):
                            w = P * len(ks)
                            act.activation(probs[:, h % 2, at:at + w], sc[:, h % 2, at:at + w], ACT.Exp,
                                           bias=neg_max[:, h, n:n + 1], accum_out=sums[:, h, n:n + 1])\
                               .then_inc(s.probs_ready, 1)
                    if kind == "bucket":
                        act.activation(zero_key[:, :], neg_max[:, :, 0], ACT.Exp).then_inc(s.extra_ready, 1)

                @block.gpsimd
                def _(pool):
                    if rotary:
                        for n in range(n_proj):
                            pool.wait_ge(s.raw_ready, 2 * n + 2)
                            pool.tensor_tensor(cosd[:, n, :], raw[:, n, :],
                                               net.w("k", ("qcos", "kcos")[n // parts]), ALU.mult)\
                                .then_inc(s.cos_done, 1)

                @block.vector
                def _(dve):
                    here = i * LEN
                    if rotary:
                        dve.tensor_copy(xs[0:64, :], src[0:64, bass.ds(here, LEN)]).then_inc(s.x_ready, 1)
                        dve.memset(xs[64:P, 0:1], 0.0).then_inc(s.x_ready, 1)
                        dve.tensor_copy(xs[64:P, 1:LEN], src[64:P, bass.ds(here, LEN - 1)]).then_inc(s.x_ready, 1)
                    else:
                        dve.tensor_copy(xs[:, :], src[:, bass.ds(here, LEN)]).then_inc(s.x_ready, 1)
                        for n in range(n_proj):
                            dve.wait_ge(s.q_ready, n + 1)
                            c = n % parts
                            if n < parts:
                                dve.tensor_scalar(q_sb[:, c, :], pp[:, n % 2, 0:LEN], bq[:, c:c + 1], scale,
                                                  ALU.add, ALU.mult).then_inc(s.q_read, 1)
                            else:
                                dve.tensor_scalar(k_sb[:, c, :], pp[:, n % 2, 0:LEN], bk[:, c:c + 1], None,
                                                  ALU.add).then_inc(s.q_read, 1)
                    if rotary:
                        for n in range(n_proj):
                            dve.wait_ge(s.raw_ready, 2 * n + 2)
                            dve.engine_nop().then_inc(s.q_read, 1)
                    for n in range(n_v):
                        tile, c = n % 2, n // 2
                        dve.wait_ge(s.v_ready, n + 1)
                        out = v_sb[:, tile, c * v_w:(c + 1) * v_w]
                        if bv is None:
                            dve.tensor_copy(out, pp[:, n % 2, 0:v_w]).then_inc(s.v_read, 1)
                        else:
                            dve.tensor_tensor(out, pp[:, n % 2, 0:v_w], bv[:, c * v_w:(c + 1) * v_w], ALU.add)\
                               .then_inc(s.v_read, 1)
                    if rotary:
                        for n in range(n_proj):
                            dve.wait_ge(s.rot_ready, n + 1)
                            dve.tensor_tensor(sind[:, n, :], pp[:, n % 2, 0:LEN],
                                              net.w("k", ("qsin", "ksin")[n // parts]), ALU.mult)\
                               .then_inc(s.vec_steps, 1)
                            dve.tensor_scalar(std[:, n, :], pp[:, n % 2, LEN:2 * LEN], 1e-24, None, ALU.max)\
                               .then_inc(s.std_ready, 1)
                        dve.wait_ge(s.vec_steps, n_proj)
                        dve.wait_ge(s.cos_done, n_proj)
                        flat = "p n t -> p (n t)"
                        al = [t[:, :, :].rearrange(flat) for t in (sind, cosd, std)]
                        order = Order(dve, s.k_spread)
                        order.step(dve.tensor_tensor(al[0], al[0], al[1], ALU.add))
                        dve.wait_ge(s.norm_ready, 1)
                        half = parts * LEN
                        order.step(dve.tensor_tensor(q_sb[:, :, :].rearrange(flat), al[0][:, 0:half],
                                                     al[2][:, 0:half], ALU.mult))
                        dve.tensor_tensor(k_sb[:, :, :].rearrange(flat), al[0][:, half:], al[2][:, half:],
                                          ALU.mult).then_inc(s.qk_done, 1)
                    elif small:
                        dve.wait_ge(s.q_read, n_proj)
                        shape = [P, heads, LEN]
                        dve.tensor_tensor(k_one[:, :, :], k_sb[:, 0, :].unsqueeze(1).to_broadcast(shape),
                                          net.w("k", "heads8").unsqueeze(2).to_broadcast(shape), ALU.mult)\
                           .then_inc(s.qk_done, 1)
                    else:
                        dve.wait_ge(s.q_read, n_proj)
                        dve.engine_nop().then_inc(s.qk_done, 1)
                    chain = Order(dve, s.chain)

                    def copy_turned(h):
                        dve.wait_ge(s.turned, h + 1)
                        if h >= 2:
                            dve.wait_ge(s.out_ready, h - 1)
                        dve.tensor_copy(turned[:, h % 2, :], tp[:, h % 2, 0:384]).then_inc(s.turned_read, 1)

                    def finish(g):
                        dve.wait_ge(s.out_ready, (g + 1) * lot)
                        if kind == "bucket":
                            dve.wait_ge(s.extra_ready, 1)
                            chain.step(dve.scalar_tensor_tensor(
                                out=sums[:, :, 0], in0=zero_key[:, :], scalar=net.w("k", "extra"),
                                in1=sums[:, :, 0], op0=ALU.mult, op1=ALU.add))
                        mine = sums[:, g * lot:(g + 1) * lot, :]
                        chain.step(dve.reciprocal(mine, mine))
                        for q in range(2):
                            shape = [P, lot, dim]
                            src_o = op[:, q, 0:lot_w].rearrange("p (h d) -> p h d", h=lot)
                            out_o = o_sb[:, q, :].rearrange("p (h d) -> p h d", h=lot)
                            below = sums[:, g * lot:(g + 1) * lot, q].unsqueeze(2).to_broadcast(shape)
                            if kind == "window":
                                chain.step(dve.tensor_tensor(out_o, src_o, below, ALU.mult))
                                dve.tensor_scalar(o_sb[:, q, :], o_sb[:, q, :],
                                                  net.w("k", "seen", q, q + 1), None, ALU.mult)\
                                   .then_inc(s.out_scaled, 1)
                            else:
                                dve.tensor_tensor(out_o, src_o, below, ALU.mult).then_inc(s.out_scaled, 1)
                        dve.wait_ge(s.out_turned, g + 1)
                        dve.tensor_copy(o_t[:, g * lot_parts:(g + 1) * lot_parts, :], otp[:, 0:lot_parts, :])\
                           .then_inc(s.out_copied, 1)

                    for h in range(heads):
                        dve.wait_ge(s.scores_ready, h + 1)
                        outs = [neg_max[:, h, n:n + 1] for n in range(2)]
                        ins = [sc[:, h % 2, at:at + P * len(ks)] for q, ks, at in segs]
                        if kind == "bucket":
                            chain.step(dve.tensor_reduce(outs[0], ins[0], AX, ALU.max, negate=True))
                            chain.step(dve.tensor_scalar(outs[0], outs[0], net.w("k", "floor"), None, ALU.min))
                        else:
                            chain.step(dve.tensor_reduce(outs[0], ins[0], AX, ALU.max, negate=True))
                        dve.tensor_reduce(outs[1], ins[1], AX, ALU.max, negate=True).then_inc(s.max_ready, 1)
                        if h % lot >= 1:
                            copy_turned(h - 1)
                        if h % lot == lot - 1:
                            copy_turned(h)
                            finish(h // lot)
                    dve.wait_ge(s.proj_ready, 1)
                    to = dst[:, bass.ds(here, LEN)]
                    if bo is None:
                        dve.tensor_tensor(to, to, pp[:, 0, 0:LEN], ALU.add)
                    else:
                        dve.scalar_tensor_tensor(out=to, in0=pp[:, 0, 0:LEN], scalar=bo, in1=to,
                                                 op0=ALU.add, op1=ALU.add)
            nc.all_engine_barrier(sems_to_clear=span(s))


def selective_scan(net, src, dst):
    nc = net.nc
    s = net.signals("scan", [
        "rates_ready", "x_ready", "in_ready", "padded", "z_done", "conv_done", "x_acted", "low_ready", "low_copied",
        "dt_ready", "dt_biased", "dt_steps", "delta_ready", "rows_ready", "decay_ready", "read_out", "hc_ready",
        "summed", "gated", "out_ready", "steps"])
    C = D_INNER // P
    with ExitStack() as ctx:
        xs = net.sbuf("m_x", [P, LEN], ctx=ctx)
        padded = net.sbuf("m_pad", [P, C, LEN + 4], ctx=ctx)
        conv = net.sbuf("m_conv", [P, C, LEN], ctx=ctx)
        xi = net.sbuf("m_xi", [P, C, LEN], ctx=ctx)
        z = net.sbuf("m_z", [P, C, LEN], ctx=ctx)
        low = net.sbuf("m_low", [DT_RANK, LEN], ctx=ctx)
        bc = net.sbuf("m_bc", [STATE, 2, LEN], ctx=ctx)
        pre = net.sbuf("m_pre", [P, C, LEN], ctx=ctx)
        soft = net.sbuf("m_soft", [P, C, LEN], ctx=ctx)
        delta = net.sbuf("m_delta", [P, C, LEN], ctx=ctx)
        dx = net.sbuf("m_dx", [P, C, LEN], ctx=ctx)
        decay = net.sbuf("m_decay", [P, 2, C, LEN], ctx=ctx)
        drive = net.sbuf("m_drive", [P, C, LEN], ctx=ctx)
        state = net.sbuf("m_state", [P, C, LEN], ctx=ctx)
        hc = net.sbuf("m_hc", [P, 2, C, LEN], ctx=ctx)
        y = net.sbuf("m_y", [P, C, LEN], ctx=ctx)
        rates = net.sbuf("m_rates", [P, C * STATE], ctx=ctx)
        x_ps = net.psum("m_xps", [P, C, LEN], ctx)
        z_ps = net.psum("m_zps", [P, C, LEN], ctx)
        low_ps = net.psum("m_lps", [P, 512], ctx)
        bc_ps = net.psum("m_bps", [STATE, 2, LEN], ctx)
        rows_ps = net.psum("m_rps", [P, 2, 2, LEN], ctx)
        y_ps = net.psum("m_yps", [P, C, LEN], ctx)
        flat = "p c t -> p (c t)"
        with nc.Block(no_gpsimd_drain=True) as block:
            @block.scalar
            def _(act):
                act.activation(rates[:, :], net.w("m", "alog"), ACT.Exp).then_inc(s.rates_ready, 1)

            @block.vector
            def _(dve):
                dve.wait_ge(s.rates_ready, 1)
                dve.tensor_scalar(rates[:, :], rates[:, :], -1.0, None, ALU.mult)
                dve.memset(decay[:, :, :, 0:1], 0.0)
                dve.memset(padded[:, :, 0:3], 0.0)
        nc.all_engine_barrier(sems_to_clear=span(s))

        with nc.Fori(0, SEQS) as i:
            with nc.Block(no_gpsimd_drain=True) as block:
                @block.tensor
                def _(pe):
                    pe.wait_ge(s.x_ready, 1)
                    for n in range(2 * C):
                        to = (x_ps, z_ps)[n // C]
                        last = pe.matmul(to[:, n % C, :], net.w("m", "win", n * P, (n + 1) * P), xs[:, :],
                                         start=True, stop=True)
                        if n % C == C - 1:
                            last.then_inc(s.in_ready, 1)
                    pe.wait_ge(s.x_acted, C)
                    wx = net.w("m", "wx").rearrange("p (c n) -> p c n", c=C)
                    for out, a, b in ((low_ps[0:DT_RANK, 0:LEN], 0, DT_RANK),
                                      (bc_ps[:, 0, :], DT_RANK, DT_RANK + STATE),
                                      (bc_ps[:, 1, :], DT_RANK + STATE, DT_RANK + 2 * STATE)):
                        for c in range(C):
                            last = pe.matmul(out, wx[:, c, a:b], xi[:, c, :], start=(c == 0), stop=(c == C - 1))
                    last.then_inc(s.low_ready, 1)
                    pe.wait_ge(s.low_copied, 1)
                    for c in range(C):
                        last = pe.matmul(x_ps[:, c, :], net.w("m", "wdt", c * P, (c + 1) * P, rows=DT_RANK),
                                         low[:, :], start=True, stop=True)
                    last.then_inc(s.dt_ready, 1)
                    pe.wait_ge(s.low_copied, 2)

                    def add_up(n):
                        pe.wait_ge(s.hc_ready, n + 1)
                        pe.matmul(y_ps[:, :, :].rearrange(flat), net.w("k", "ident"),
                                  hc[:, n % 2, :, :].rearrange(flat), start=(n == 0), stop=(n == STATE - 1))\
                          .then_inc(s.summed, 1)

                    for n in range(STATE):
                        if n >= 2:
                            pe.wait_ge(s.hc_ready, n - 1)
                        pe.matmul(rows_ps[:, n % 2, :, :].rearrange("p a t -> p (a t)"),
                                  net.w("k", "ident", n, n + 1, rows=STATE).to_broadcast([STATE, P]),
                                  bc[:, :, :].rearrange("p a t -> p (a t)"), start=True, stop=True)\
                          .then_inc(s.rows_ready, 1)
                        if n >= 1:
                            add_up(n - 1)
                    add_up(STATE - 1)
                    pe.wait_ge(s.gated, 1)
                    for c in range(C):
                        last = pe.matmul(low_ps[:, 0:LEN], net.w("m", "wout", c * P, (c + 1) * P), y[:, c, :],
                                         start=(c == 0), stop=(c == C - 1))
                    last.then_inc(s.out_ready, 1)

                @block.scalar
                def _(act):
                    act.wait_ge(s.in_ready, 2)
                    act.activation(z[:, :, :], z_ps[:, :, :], ACT.Silu).then_inc(s.z_done, 1)
                    for c in range(C):
                        act.wait_ge(s.conv_done, c + 1)
                        act.activation(xi[:, c, :], conv[:, c, :], ACT.Silu, bias=net.w("m", "cb", c, c + 1))\
                           .then_inc(s.x_acted, 1)
                    act.wait_ge(s.dt_biased, C)
                    order = Order(act, s.dt_steps)
                    order.step(act.activation(soft[:, :, :], pre[:, :, :], ACT.Abs))
                    order.step(act.activation(soft[:, :, :], soft[:, :, :], ACT.Exp, scale=-1.0))
                    order.step(act.activation(soft[:, :, :], soft[:, :, :], ACT.Ln, bias=net.w("k", "one")))
                    act.wait_ge(s.delta_ready, 1)
                    for n in range(STATE):
                        if n >= 2:
                            act.wait_ge(s.read_out, n - 1)
                        for c in range(C):
                            last = act.activation(decay[:, n % 2, c, 1:LEN], delta[:, c, 1:LEN], ACT.Exp,
                                                  scale=rates[:, c * STATE + n:c * STATE + n + 1])
                            last.then_inc(s.decay_ready, 1)

                @block.vector
                def _(dve):
                    here = i * LEN
                    order = Order(dve, s.steps)
                    dve.tensor_copy(xs[:, :], src[:, bass.ds(here, LEN)]).then_inc(s.x_ready, 1)
                    dve.wait_ge(s.in_ready, 1)
                    order.step(dve.tensor_copy(padded[:, :, 3:3 + LEN], x_ps[:, :, :]))
                    for c in range(C):
                        for j in range(4):
                            tap = net.w("m", "cw", c * 4 + j, c * 4 + j + 1)
                            there = padded[:, c, j:j + LEN]
                            if j == 0:
                                ins = dve.tensor_scalar(conv[:, c, :], there, tap, None, ALU.mult)
                            else:
                                ins = dve.scalar_tensor_tensor(out=conv[:, c, :], in0=there, scalar=tap,
                                                               in1=conv[:, c, :], op0=ALU.mult, op1=ALU.add)
                            if j < 3:
                                order.step(ins)
                            else:
                                ins.then_inc(s.conv_done, 1)
                    dve.wait_ge(s.low_ready, 1)
                    dve.tensor_copy(low[:, :], low_ps[0:DT_RANK, 0:LEN]).then_inc(s.low_copied, 1)
                    dve.tensor_copy(bc[:, :, :], bc_ps[:, :, :]).then_inc(s.low_copied, 1)
                    dve.wait_ge(s.dt_ready, 1)
                    for c in range(C):
                        dve.tensor_scalar(pre[:, c, :], x_ps[:, c, :], net.w("m", "bdt", c, c + 1), None, ALU.add)\
                           .then_inc(s.dt_biased, 1)
                    dve.wait_ge(s.dt_biased, C)
                    dve.wait_ge(s.dt_steps, 3)
                    dve.scalar_tensor_tensor(out=delta[:, :, :], in0=pre[:, :, :], scalar=0.0, in1=soft[:, :, :],
                                             op0=ALU.max, op1=ALU.add).then_inc(s.delta_ready, 1)
                    dve.wait_ge(s.delta_ready, 1)
                    dve.wait_ge(s.x_acted, C)
                    order.step(dve.tensor_tensor(dx[:, :, :], delta[:, :, :], xi[:, :, :], ALU.mult))
                    for n in range(STATE):
                        b = n % 2
                        dve.wait_ge(s.rows_ready, n + 1)
                        shape = [P, C, LEN]
                        order.step(dve.tensor_tensor(drive[:, :, :], dx[:, :, :],
                                                     rows_ps[:, b, 0, :].unsqueeze(1).to_broadcast(shape), ALU.mult))
                        dve.wait_ge(s.decay_ready, C * (n + 1))
                        dve.tensor_tensor_scan(state[:, :, :].rearrange(flat), decay[:, b, :, :].rearrange(flat),
                                               drive[:, :, :].rearrange(flat), 0.0, ALU.mult, ALU.add)\
                           .then_inc(s.read_out, 1)
                        dve.wait_ge(s.read_out, n + 1)
                        if n >= 2:
                            dve.wait_ge(s.summed, n - 1)
                        dve.tensor_tensor(hc[:, b, :, :], state[:, :, :],
                                          rows_ps[:, b, 1, :].unsqueeze(1).to_broadcast(shape), ALU.mult)\
                           .then_inc(s.hc_ready, 1)
                        dve.wait_ge(s.hc_ready, n + 1)
                    dve.wait_ge(s.summed, STATE)
                    for c in range(C):
                        order.step(dve.scalar_tensor_tensor(
                            out=y[:, c, :], in0=xi[:, c, :], scalar=net.w("m", "dskip", c, c + 1),
                            in1=y_ps[:, c, :], op0=ALU.mult, op1=ALU.add))
                    dve.wait_ge(s.z_done, 1)
                    dve.tensor_tensor(y[:, :, :], y[:, :, :], z[:, :, :], ALU.mult).then_inc(s.gated, 1)
                    dve.wait_ge(s.out_ready, 1)
                    to = dst[:, bass.ds(here, LEN)]
                    dve.tensor_tensor(to, to, low_ps[:, 0:LEN], ALU.add)
            nc.all_engine_barrier(sems_to_clear=span(s))


def model(nc, x_in, blobs, out, stages):
    with ExitStack() as ctx:
        net = Net(nc, ctx)
        X = net.sbuf("X", [P, TOK])
        H = net.sbuf("H", [P, TOK])
        G = net.sbuf("G", [P, TOK])
        shares = net.sbuf("shares", [E2, TOK])
        width = {g: starts(g)[1] for g in COLS}
        net.weights = {g: net.sbuf(f"w_{g}", [P, width[g]]) for g in COLS if g not in "eh"}
        region = net.sbuf("w_experts", [P, max(width["e"], width["h"])])
        net.weights["e"] = net.weights["h"] = region
        net.ident16 = net.sbuf("ident16", [P, P], BF16)
        masks = {m: net.sbuf(f"mask_{m}", [P, 384], BF16) for m in ("m_bucket", "m_local", "m_causal", "m_window")}
        loaded = ctx.enter_context(nc.semaphore("loaded"))
        experts_loaded = ctx.enter_context(nc.semaphore("experts_loaded"))
        stored = ctx.enter_context(nc.semaphore("stored"))

        def load(sp, g, sem):
            sp.dma_start(net.weights[g][:, 0:width[g]], blobs[g]).then_inc(sem, 16)

        early = ["k", "a", "f"]
        late = ["m", "g", "c", "d"]
        with nc.Block() as block:
            @block.sync
            def _(sp):
                sp.dma_start(X[:, :], x_in).then_inc(loaded, 16)
                for g in early:
                    load(sp, g, loaded)
                for g in late:
                    load(sp, g, experts_loaded)
                load(sp, "e" if "M" in stages else "h", experts_loaded)
                sp.wait_ge(loaded, 16 * (1 + len(early)))

            @block.vector
            def _(dve):
                dve.wait_ge(loaded, 16 * (1 + len(early)))
                dve.tensor_copy(net.ident16[:, :], net.w("k", "ident"))
                for m, t in masks.items():
                    dve.tensor_copy(t[:, :], net.w("k", m))

        def wait_experts(n):
            with nc.Block(no_gpsimd_drain=True) as block:
                @block.sync
                def _(sp):
                    sp.wait_ge(experts_loaded, n)

        def stage_a():
            norm(net, "a0", X, H)
            norm(net, "a1", H, G, gain=net.w("a", "g1"), bias=net.w("a", "c1"))
            w = net.w("a", "wqkv")
            attention(net, "bucket", G, H, masks["m_bucket"], A_DIM ** -0.5, w[:, 0:P], w[:, P:2 * P],
                      w[:, 2 * P:3 * P], net.w("a", "wo"), net.w("a", "bq"), net.w("a", "bk"),
                      net.w("a", "bv"), net.w("a", "bo"))
            norm(net, "a2", H, G, gain=net.w("a", "g2"), bias=net.w("a", "c2"))
            chunks = [dict(rows=P, gate=net.w("a", "w1", c * P, (c + 1) * P), up=None,
                           down=net.w("a", "w2", c * P, (c + 1) * P), gate_bias=net.w("a", "b1", c, c + 1))
                      for c in range(4)]
            mlp(net, G, X, chunks, ACT.Gelu, out_bias=net.w("a", "b2"), also=H)

        def stage_f():
            norm(net, "f0", X, H)
            for l in (0, 1):
                inner = F_HEADS * F_DIM
                w = net.w("f", f"wqkv{l}")
                attention(net, "local", H, H, masks["m_local"], None, w[:, 0:inner], w[:, inner:2 * inner],
                          w[:, 2 * inner:], net.w("f", f"wo{l}"), q_gain=net.w("f", f"qs{l}"),
                          k_gain=net.w("f", f"ks{l}"))
                norm(net, f"f{l}", H, G, gain=net.w("f", f"g{l}"), bias=net.w("f", f"c{l}"), shift=True)
                chunks = []
                for c in range(3):
                    rows = min(P, HID_F - c * P)
                    chunks.append(dict(
                        rows=rows, up=net.w("f", f"w1{l}", c * P, c * P + rows),
                        gate=net.w("f", f"w1{l}", HID_F + c * P, HID_F + c * P + rows),
                        down=net.w("f", f"w2{l}", c * P, (c + 1) * P, rows=rows),
                        up_bias=net.w("f", f"ba{l}", c, c + 1, rows=rows),
                        gate_bias=net.w("f", f"bg{l}", c, c + 1, rows=rows)))
                if l == 0:
                    mlp(net, G, H, chunks, ACT.Gelu, out_bias=net.w("f", "b20"))
                else:
                    mlp(net, G, X, chunks, ACT.Gelu, out_bias=net.w("f", "b21"), also=H)

        def stage_m():
            norm(net, "m0", X, H)
            norm(net, "m1", H, G, root_mean_square=True, gain=net.w("m", "r1"))
            selective_scan(net, G, H)
            norm(net, "m2", H, G, root_mean_square=True, gain=net.w("m", "r2"))
            gate(net, G, shares[0:N_EXP, :], N_EXP)
            chunks = []
            for e in range(N_EXP):
                for c in range(FFN // P):
                    at = e * FFN + c * P
                    chunks.append(dict(rows=P, gate=net.w("e", "wg", at, at + P), up=net.w("e", "wu", at, at + P),
                                       down=net.w("e", "wd", at, at + P), share_key=e,
                                       share=net.w("k", "ident", e, e + 1, rows=N_EXP).to_broadcast([N_EXP, P])))
            mlp(net, G, X, chunks, ACT.Silu, also=H, shares=shares[0:N_EXP, :])

        def stage_c():
            norm(net, "c0", X, H)
            attention(net, "window", H, X, masks["m_window"], A_DIM ** -0.5, net.w("c", "wq"), net.w("c", "wk"),
                      net.w("c", "wv"), net.w("c", "wo"), net.w("c", "bq"), net.w("c", "bk"),
                      net.w("c", "bv"), net.w("c", "bo"))

        def stage_h():
            norm(net, "h0", X, H)
            gate(net, H, shares[:, :], E2)
            chunks = []
            for c in range((ROUTED + SHARED + P - 1) // P):
                at = c * P
                rows = min(P, ROUTED + SHARED - at)
                lot = dict(rows=rows, gate=net.w("h", "wg", at, at + rows), up=net.w("h", "wu", at, at + rows),
                           down=net.w("h", "wd", at, at + P, rows=rows))
                if at < ROUTED:
                    lot.update(share_key=c, share=net.w("h", "expert", at, at + P, rows=E2))
                chunks.append(lot)
            mlp(net, H, X, chunks, ACT.Silu, shares=shares[:, :])

        def stage_d():
            norm(net, "d0", X, H)
            attention(net, "causal", H, X, masks["m_causal"], D_DIM ** -0.5, net.w("d", "wq"), net.w("d", "wk"),
                      net.w("d", "wv"), net.w("d", "wo"), net.w("d", "bq"), net.w("d", "bk"),
                      net.w("d", "bv"), net.w("d", "bo"))

        came = 16 * (len(late) + 1)
        for n, st in enumerate(stages):
            if n == min([stages.find(k) for k in "MCHD" if k in stages] or [99]):
                wait_experts(came)
            dict(A=stage_a, F=stage_f, M=stage_m, C=stage_c, H=stage_h, D=stage_d)[st]()
            if st == "M":
                with nc.Block(no_gpsimd_drain=True) as block:
                    @block.sync
                    def _(sp):
                        load(sp, "h", experts_loaded)
                came += 16
                second = came
            if "M" in stages[:n + 1] and stages[n + 1:n + 2] == "H":
                wait_experts(second)

        with nc.Block() as block:
            @block.sync
            def _(sp):
                sp.dma_start(out, X[:, :]).then_inc(stored, 16)
                sp.wait_ge(stored, 16)



def _rows(a, n=P):
    a = np.asarray(a, np.float32)
    return np.concatenate([a, np.zeros((n - a.shape[0],) + a.shape[1:], np.float32)]) if a.shape[0] < n else a


def _col(b):
    b = np.asarray(b, np.float32).reshape(-1)
    n = -(-b.size // P)
    return np.ascontiguousarray(_rows(b, n * P).reshape(n, P).T)


def _stack(w):
    w = np.asarray(w, np.float32)
    k = -(-w.shape[0] // P)
    return np.ascontiguousarray(_rows(w, k * P).reshape(k, P, -1).transpose(1, 0, 2)).reshape(P, -1)


def _wide(b):
    return np.ascontiguousarray(np.broadcast_to(np.asarray(b, np.float32).reshape(1, -1), (P, np.size(b))))


def _constants():
    f = np.float32
    ident = np.eye(P, dtype=f)
    blocks = np.kron(np.eye(2, dtype=f), np.ones((64, 64), f))
    half = np.zeros((64, 64), f)
    for d in range(32):
        half[d + 32, d] = -1.0
        half[d, d + 32] = 1.0
    rot = np.kron(np.eye(2, dtype=f), half)
    idx = np.arange(0, F_DIM, 2, dtype=f)
    inv_freq = (f(1.0) / np.power(f(10000.0), idx / f(F_DIM))).astype(f)
    t = np.arange(LEN, dtype=f)
    freqs = (t[:, None] * inv_freq[None, :]).astype(f)
    base = ((idx + f(0.4 * F_DIM)) / f(1.4 * F_DIM)).astype(f)
    power = ((t - LEN // 2) / f(32.0)).astype(f)
    sc = np.power(base[None, :], power[:, None]).astype(f)
    cos, sin = np.cos(freqs).astype(f), np.sin(freqs).astype(f)

    def table(a):
        return np.ascontiguousarray(np.tile(np.concatenate([a, a], 1), (1, 2)).T.astype(f))

    qs = f(8.0)
    q = np.arange(P)[:, None]
    k = np.arange(P)[None, :]

    def lay(rule, window=False):
        segs = [(0, 0), (0, 1), (1, 1)] if window else [(0, 0), (1, 0), (1, 1)]
        return np.concatenate([np.where(rule(q + P * a, k + P * b), 0.0, MASKED) for a, b in segs], 1).astype(f)

    def win(i, j):
        first = (i >= 1) & (i <= 32) & (j >= 1) & (j <= 32)
        second = (i >= 129) & (i <= 160) & (j >= 129) & (j <= 160)
        return (i == 0) | first | second | ((i == j) & (i > 0))

    tok = np.arange(LEN)
    seen = ((tok <= 32) | ((tok >= 129) & (tok <= 160))).astype(f).reshape(2, P).T
    in_first = np.arange(P) < 64

    def before(n):
        return np.tile((np.arange(n)[None, :] < np.arange(n)[:, None]).astype(f).reshape(1, -1), (P, 1))

    return dict(
        ident=ident, mean=np.full((P, P), 1.0 / P, f), pairs=blocks, rot=rot,
        qcos=table(cos * sc * qs), qsin=table(sin * sc * qs), kcos=table(cos / sc), ksin=table(sin / sc),
        m_bucket=lay(lambda i, j: (j <= i) & (j // 64 >= i // 64 - 1)),
        m_local=lay(lambda i, j: (j <= i) & (i <= j + 64)),
        m_causal=lay(lambda i, j: j <= i), m_window=lay(win, True),
        heads8=(np.arange(P)[:, None] // 8 == np.arange(16)[None, :]).astype(f),
        floor=np.where(in_first, 0.0, 3e38).astype(f)[:, None],
        extra=np.where(in_first, 64.0, 0.0).astype(f)[:, None],
        seen=seen, eps=np.full((P, 1), EPS, f), one=np.ones((P, 1), f), back=np.full((P, 1), 10 * np.log(2.0), f),
        before8=before(8), before16=before(16))


def _layout(v):
    out = {"k": _constants()}
    a = {n[len("L0_attn_a_"):]: x for n, x in v.items() if n.startswith("L0_attn_a_")}
    out["a"] = dict(g1=_col(a["ln1_g"]), c1=_col(a["ln1_b"]), wqkv=a["w_qkv"], bq=_col(a["b_qkv"][:P]),
                    bk=_col(a["b_qkv"][P:2 * P]), bv=_wide(a["b_qkv"][2 * P:]), wo=a["w_out"], bo=_col(a["b_out"]),
                    g2=_col(a["ln2_g"]), c2=_col(a["ln2_b"]), w1=a["w1"], b1=_col(a["b1"]), w2=_stack(a["w2"]),
                    b2=_col(a["b2"]))
    f = {n[len("L0_ffn_"):]: x for n, x in v.items() if n.startswith("L0_ffn_")}
    out["f"] = {}
    for l in (0, 1):
        twice = lambda g: _col(np.concatenate([g, g]))
        out["f"].update({
            f"wqkv{l}": f["wqkv"][l], f"qs{l}": twice(f["q_scale"][l]), f"ks{l}": twice(f["k_scale"][l]),
            f"wo{l}": _stack(f["wo"][l]), f"g{l}": _col(f["ln_g"][l]), f"c{l}": _col(f["ln_b"][l]),
            f"w1{l}": f["w1"][l], f"ba{l}": _col(f["b1"][l][:HID_F]), f"bg{l}": _col(f["b1"][l][HID_F:]),
            f"w2{l}": _stack(f["w2"][l]), f"b2{l}": _col(f["b2"][l])})
    m = {n[len("L0_attn_b_"):]: x for n, x in v.items() if n.startswith("L0_attn_b_")}
    out["m"] = dict(r1=_col(m["rms1_w"]), r2=_col(m["rms2_w"]), win=m["in_proj_w"],
                    cw=_stack(m["conv_w"].reshape(D_INNER, 4)), cb=_col(m["conv_b"]), wx=_stack(m["x_proj_w"]),
                    wdt=_rows(m["dt_proj_w"]), bdt=_col(m["dt_proj_b"]), alog=_stack(m["A_log"]),
                    dskip=_col(m["D_skip"]), wout=_stack(m["out_proj_w"]), router=m["router_w"])
    out["e"] = dict(wg=m["Wg"].transpose(1, 0, 2).reshape(P, -1), wu=m["Wu"].transpose(1, 0, 2).reshape(P, -1),
                    wd=_stack(m["Wd"].reshape(-1, P)))
    h = {n[len("L1_ffn_"):]: x for n, x in v.items() if n.startswith("L1_ffn_")}
    out["h"] = dict(
        wg=np.concatenate([h["gate_proj"].reshape(-1, P).T, h["shared_gate_w"].T], 1),
        wu=np.concatenate([h["up_proj"].reshape(-1, P).T, h["shared_up_w"].T], 1),
        wd=_stack(np.concatenate([h["down_proj"].transpose(0, 2, 1).reshape(-1, P), h["shared_down_w"].T], 0)),
        expert=_rows((np.arange(ROUTED)[None, :] // I2 == np.arange(E2)[:, None]).astype(np.float32)))
    out["g"] = dict(gate=h["gate_w"].T, bias=_wide(h["gate_bias"]))
    c = {n[len("L1_attn_a_"):]: x for n, x in v.items() if n.startswith("L1_attn_a_")}
    out["c"] = dict(wq=c["Wq"], wk=c["Wk"], wv=c["Wv"], wo=c["Wo"], bq=_col(c["bq"]), bk=_col(c["bk"]),
                    bv=_wide(c["bv"]), bo=_col(c["bo"]))
    d = {n[len("L1_attn_b_"):]: x for n, x in v.items() if n.startswith("L1_attn_b_")}
    flat = lambda w: w.transpose(1, 0, 2).reshape(P, -1)
    out["d"] = dict(wq=flat(d["W_Q"]), wk=flat(d["W_K"]), wv=flat(d["W_V"]),
                    wo=_stack(d["W_O"].reshape(-1, P)), bq=_col(d["b_Q"]), bk=_col(d["b_K"]), bv=_wide(d["b_V"]),
                    bo=_col(d["b_O"]))
    return out


def _arrays(inputs):
    v = {n: np.asarray(x) for n, x in inputs.items()}
    got = _layout(v)
    arrays = {"x_dram": np.ascontiguousarray(v["L0_attn_a_x"].reshape(TOK, P).T)}
    for g, parts in COLS.items():
        arrays[f"w_{g}_dram"] = np.ascontiguousarray(np.concatenate([got[g][n] for n in parts], 1))
        assert arrays[f"w_{g}_dram"].shape == (P, starts(g)[1]), g
    return arrays


STAGES = "AFMFCHDH"


def kernel(**inputs):
    import concourse.bacc as _bacc
    from concourse.bass_utils import run_bass_kernel_spmd as _launch

    arrays = _arrays(inputs)
    nc = _bacc.Bacc("TRN2", target_bir_lowering=False, num_devices=1)
    dram = {n: nc.dram_tensor(n, a.shape, F32, kind="ExternalInput").ap() for n, a in arrays.items()}
    out = nc.dram_tensor("out_dram", (P, TOK), F32, kind="ExternalOutput").ap()
    model(nc, dram["x_dram"], {g: dram[f"w_{g}_dram"] for g in COLS}, out, STAGES)
    r = _launch(nc, [arrays], core_ids=[0])
    return np.ascontiguousarray(r.results[0]["out_dram"].T).reshape(SEQS, LEN, P)
```

```python
from collections import namedtuple
from contextlib import ExitStack

import numpy as np
import concourse.bass as bass
from concourse import mybir

F32 = mybir.dt.float32
BF16 = mybir.dt.bfloat16
F32R = mybir.dt.float32r
ALU = mybir.AluOpType
ACT = mybir.ActivationFunctionType
AX = mybir.AxisListType.X

P = 128
SEQS, LEN = 8, 256
TOK = SEQS * LEN
GROUP = 512
TILES = TOK // P
EPS = 1e-5
MASKED = -1e30

A_HEADS, A_DIM = 16, 8
F_HEADS, F_DIM = 8, 64
D_HEADS, D_DIM = 16, 64
HID_F, HIDP_F = 341, 384
N_EXP, FFN = 8, 512
E2, I2, SHARED = 16, 176, 352
ROUTED = E2 * I2
D_INNER, STATE, DT_RANK = 256, 16, 64

COLS = {
    "k": dict(ident=P, mean=P, pairs=P, rot=P, qcos=LEN, kcos=LEN, qsin=LEN, ksin=LEN,
              heads8=16,
              floor=1, extra=1, seen=2, eps=1, one=1, back=1, before8=64, before16=256),
    "q": dict(m_bucket=384, m_local=384, m_causal=384, m_window=384),
    "a": dict(g1=1, c1=1, wqkv=384, bq=1, bk=1, bv=P, wo=P, bo=1, g2=1, c2=1, w1=512, b1=4, w2=512, b2=1),
    "f": dict(wqkv0=1536, qs0=1, ks0=1, wo0=512, g0=1, c0=1, w10=682, ba0=3, bg0=3, w20=384, b20=1,
              wqkv1=1536, qs1=1, ks1=1, wo1=512, g1=1, c1=1, w11=682, ba1=3, bg1=3, w21=384, b21=1),
    "m": dict(r1=1, r2=1, win=512, cw=8, cb=2, wx=192, wdt=256, bdt=2, alog=32, dskip=2, wout=256, router=8),
    "e": dict(wg=4096, wu=4096, wd=4096),
    "h": dict(wg=ROUTED + SHARED, wu=ROUTED + SHARED, wd=25 * P, expert=ROUTED),
    "g": dict(gate=E2, bias=E2),
    "c": dict(wq=P, wk=P, wv=P, wo=P, bq=1, bk=1, bv=P, bo=1),
    "d": dict(wq=1024, wk=1024, wv=1024, wo=1024, bq=8, bk=8, bv=1024, bo=1),
}


def starts(group):
    at, out = 0, {}
    for name, width in COLS[group].items():
        out[name] = at
        at += width
    return out, at


def span(signals):
    return range(signals[0].num, signals[-1].num + 1)


class Order:

    def __init__(self, eng, sem):
        self.eng, self.sem, self.n = eng, sem, 0

    def step(self, ins):
        self.n += 1
        ins.then_inc(self.sem, 1)
        self.eng.wait_ge(self.sem, self.n)


class Net:

    def __init__(self, nc, ctx):
        self.nc, self.ctx, self.sets, self.tensors = nc, ctx, {}, 0

    def sbuf(self, name, shape, dt=F32, ctx=None):
        self.tensors += 1
        return (ctx or self.ctx).enter_context(self.nc.sbuf_tensor(f"{name}_{self.tensors}", shape, dt))

    def psum(self, name, shape, ctx):
        self.tensors += 1
        return ctx.enter_context(self.nc.psum_tensor(f"{name}_{self.tensors}", shape, F32))

    def signals(self, kind, names):
        if kind not in self.sets:
            got = [self.ctx.enter_context(self.nc.semaphore(f"{kind}_{n}")) for n in names]
            nums = [s.num for s in got]
            assert nums == list(range(nums[0], nums[0] + len(nums))), nums
            self.sets[kind] = namedtuple(f"Signals_{kind}", names)(*got)
        return self.sets[kind]

    def w(self, group, name, a=0, b=None, rows=P):
        at, _ = starts(group)
        lo = at[name]
        hi = lo + (COLS[group][name] if b is None else b)
        return self.weights[group][0:rows, lo + a:hi]


def norm(net, tag, src, dst, root_mean_square=False, gain=None, bias=None, shift=False):
    nc = net.nc
    chunks = TOK // GROUP
    s = net.signals("norm", ["shifted", "mean_ready", "centred", "squared", "var_ready", "std_ready", "steps", "act_steps"])
    with ExitStack() as ctx:
        moved = net.sbuf("n_moved", [P, TOK], ctx=ctx) if shift else src
        centred = net.sbuf("n_centred", [P, TOK], ctx=ctx) if not root_mean_square else src
        squared = net.sbuf("n_squared", [P, TOK], ctx=ctx)
        std = net.sbuf("n_std", [P, TOK], ctx=ctx)
        mean_ps = net.psum("n_mean", [P, chunks, GROUP], ctx)
        var_ps = net.psum("n_var", [P, chunks, GROUP], ctx)
        ones = net.w("k", "mean")

        def cut(t, c):
            return t[:, c * GROUP:(c + 1) * GROUP]

        with nc.Block(no_gpsimd_drain=True) as block:
            @block.gpsimd
            def _(pool):
                if shift:
                    half = P // 2
                    by_seq = moved[half:P, :].rearrange("p (s t) -> p s t", s=SEQS)
                    src_seq = src[half:P, :].rearrange("p (s t) -> p s t", s=SEQS)
                    pool.tensor_copy(moved[0:half, :], src[0:half, :]).then_inc(s.shifted, 1)
                    pool.memset(by_seq[:, :, 0:1], 0.0).then_inc(s.shifted, 1)
                    pool.tensor_copy(by_seq[:, :, 1:LEN], src_seq[:, :, 0:LEN - 1]).then_inc(s.shifted, 1)

            @block.tensor
            def _(pe):
                if shift:
                    pe.wait_ge(s.shifted, 3)
                if not root_mean_square:
                    for c in range(chunks):
                        pe.matmul(mean_ps[:, c, :], ones, cut(moved, c), start=True, stop=True)\
                          .then_inc(s.mean_ready, 1)
                for c in range(chunks):
                    pe.wait_ge(s.squared, c + 1)
                    pe.matmul(var_ps[:, c, :], ones, cut(squared, c), start=True, stop=True)\
                      .then_inc(s.var_ready, 1)

            @block.scalar
            def _(act):
                order = Order(act, s.act_steps)
                nc.scalar.preload_act_table_set("natural_log_exp_and_others")
                for c in range(chunks):
                    if not root_mean_square:
                        act.wait_ge(s.centred, c + 1)
                    act.activation(cut(squared, c), cut(centred, c), ACT.Square).then_inc(s.squared, 1)
                for c in range(chunks):
                    act.wait_ge(s.var_ready, c + 1)
                    order.step(act.activation(cut(std, c), var_ps[:, c, :], ACT.Ln, bias=net.w("k", "eps")))
                    act.activation(cut(std, c), cut(std, c), ACT.Exp, scale=-0.5).then_inc(s.std_ready, 1)

            @block.vector
            def _(dve):
                if shift:
                    dve.wait_ge(s.shifted, 3)
                if not root_mean_square:
                    for c in range(chunks):
                        dve.wait_ge(s.mean_ready, c + 1)
                        dve.tensor_tensor(cut(centred, c), cut(moved, c), mean_ps[:, c, :], ALU.subtract)\
                           .then_inc(s.centred, 1)
                    dve.wait_ge(s.centred, chunks)
                order = Order(dve, s.steps)
                for c in range(chunks):
                    dve.wait_ge(s.std_ready, c + 1)
                    done = dve.tensor_tensor(cut(dst, c), cut(centred, c), cut(std, c), ALU.mult)
                    if gain is not None:
                        order.step(done)
                        if bias is None:
                            dve.tensor_scalar(cut(dst, c), cut(dst, c), gain, None, ALU.mult)
                        else:
                            dve.tensor_scalar(cut(dst, c), cut(dst, c), gain, bias, ALU.mult, ALU.add)
        nc.all_engine_barrier(sems_to_clear=span(s))


def mlp(net, src, dst, chunks, func, out_bias=None, also=None, shares=None):
    nc = net.nc
    s = net.signals("mlp", ["x_ready", "gate_ready", "up_ready", "act_done", "hidden_ready", "down_done", "steps"])
    n_chunks = len(chunks)
    gated = chunks[0]["up"] is not None
    numbers, matrices, last_use = [], [], {}
    for c, lot in enumerate(chunks):
        m = lot.get("share")
        if m is None:
            numbers.append(None)
            continue
        if lot["share_key"] not in last_use:
            matrices.append(m)
        last_use[lot["share_key"]] = c
        numbers.append(len(matrices) - 1)
    last_chunk = list(last_use.values())
    with ExitStack() as ctx:
        xin = net.sbuf("f_xin", [P, GROUP], ctx=ctx)
        acted = net.sbuf("f_acted", [P, 2, GROUP], ctx=ctx)
        shared = net.sbuf("f_shared", [P, 2, GROUP], ctx=ctx)
        hidden = net.sbuf("f_hidden", [P, 2, GROUP], ctx=ctx)
        total = net.sbuf("f_total", [P, GROUP], ctx=ctx)
        share_in = net.sbuf("f_share_in", [E2, GROUP], ctx=ctx)
        gate_ps = net.psum("f_gate", [P, 2, GROUP], ctx)
        up_ps = net.psum("f_up", [P, 2, GROUP], ctx)
        share_ps = net.psum("f_share", [P, 2, GROUP], ctx)
        out_ps = net.psum("f_out", [P, GROUP], ctx)
        n_share = shares.shape[0] if shares is not None else 0

        def down(pe, c):
            pe.wait_ge(s.hidden_ready, c + 1)
            rows = chunks[c]["rows"]
            pe.matmul(out_ps[:, :], chunks[c]["down"], hidden[0:rows, c % 2, :],
                      start=(c == 0), stop=(c == n_chunks - 1)).then_inc(s.down_done, 1)

        with nc.Fori(0, TOK // GROUP) as i:
            with nc.Block(no_gpsimd_drain=True) as block:
                @block.tensor
                def _(pe):
                    pe.wait_ge(s.x_ready, 1)
                    for c, lot in enumerate(chunks):
                        rows, b = lot["rows"], c % 2
                        if c >= 2:
                            pe.wait_ge(s.act_done if gated else s.hidden_ready, c - 1)
                        pe.matmul(gate_ps[0:rows, b, :], lot["gate"], xin[:, :], start=True, stop=True)\
                          .then_inc(s.gate_ready, 1)
                        if gated:
                            if c >= 2:
                                pe.wait_ge(s.hidden_ready, c - 1)
                            k = numbers[c]
                            if k is not None and (c == 0 or numbers[c - 1] != k):
                                if k >= 2:
                                    pe.wait_ge(s.hidden_ready, last_chunk[k - 2] + 1)
                                pe.matmul(share_ps[:, k % 2, :], matrices[k], share_in[0:n_share, :],
                                          start=True, stop=True)
                            pe.matmul(up_ps[0:rows, b, :], lot["up"], xin[:, :], start=True, stop=True)\
                              .then_inc(s.up_ready, 1)
                        if c >= 1:
                            down(pe, c - 1)
                    down(pe, n_chunks - 1)

                @block.scalar
                def _(act):
                    for c, lot in enumerate(chunks):
                        rows, b = lot["rows"], c % 2
                        act.wait_ge(s.gate_ready, c + 1)
                        bias = lot.get("gate_bias")
                        more = {} if bias is None else {"bias": bias}
                        if gated:
                            if c >= 2:
                                act.wait_ge(s.hidden_ready, c - 1)
                            act.activation(acted[0:rows, b, :], gate_ps[0:rows, b, :], func, **more)\
                               .then_inc(s.act_done, 1)
                        else:
                            if c >= 2:
                                act.wait_ge(s.down_done, c - 1)
                            act.activation(hidden[0:rows, b, :], gate_ps[0:rows, b, :], func, **more)\
                               .then_inc(s.hidden_ready, 1)

                @block.vector
                def _(dve):
                    order = Order(dve, s.steps)
                    if shares is not None:
                        order.step(dve.tensor_copy(share_in[0:n_share, :], shares[:, bass.ds(i * GROUP, GROUP)]))
                    dve.tensor_copy(xin[:, :], src[:, bass.ds(i * GROUP, GROUP)]).then_inc(s.x_ready, 1)
                    if gated:
                        for c, lot in enumerate(chunks):
                            rows, b = lot["rows"], c % 2
                            dve.wait_ge(s.act_done, c + 1)
                            dve.wait_ge(s.up_ready, c + 1)
                            left = acted[0:rows, b, :]
                            if numbers[c] is not None:
                                left = shared[0:rows, b, :]
                                order.step(dve.tensor_tensor(left, acted[0:rows, b, :],
                                                             share_ps[0:rows, numbers[c] % 2, :], ALU.mult))
                            if c >= 2:
                                dve.wait_ge(s.down_done, c - 1)
                            out = hidden[0:rows, b, :]
                            if lot.get("up_bias") is not None:
                                dve.scalar_tensor_tensor(out=out, in0=up_ps[0:rows, b, :], scalar=lot["up_bias"],
                                                         in1=left, op0=ALU.add, op1=ALU.mult)\
                                   .then_inc(s.hidden_ready, 1)
                            else:
                                dve.tensor_tensor(out, left, up_ps[0:rows, b, :], ALU.mult)\
                                   .then_inc(s.hidden_ready, 1)
                    dve.wait_ge(s.down_done, n_chunks)
                    here = dst[:, bass.ds(i * GROUP, GROUP)]
                    if out_bias is not None:
                        order.step(dve.tensor_scalar(total[:, :], out_ps[:, :], out_bias, None, ALU.add))
                    else:
                        order.step(dve.tensor_copy(total[:, :], out_ps[:, :]))
                    if also is not None:
                        order.step(dve.tensor_tensor(total[:, :], total[:, :],
                                                     also[:, bass.ds(i * GROUP, GROUP)], ALU.add))
                    dve.tensor_tensor(here, here, total[:, :], ALU.add)
            nc.all_engine_barrier(sems_to_clear=span(s))


def gate(net, src, shares, experts):
    nc = net.nc
    E, T = experts, TILES
    s = net.signals("gate", ["logits_ready", "scored", "steps", "chosen", "turned", "copied", "act_steps"])
    weights = net.w("m", "router") if E == N_EXP else net.w("g", "gate")
    with ExitStack() as ctx:
        x = net.sbuf("g_x", [P, T, E], ctx=ctx)
        y = net.sbuf("g_y", [P, T, E], ctx=ctx)
        rank = net.sbuf("g_rank", [P, T, E], ctx=ctx)
        more = net.sbuf("g_more", [P, T, E, E], ctx=ctx)
        same = net.sbuf("g_same", [P, T, E, E], ctx=ctx)
        row = net.sbuf("g_row", [P, T], ctx=ctx)
        z = net.sbuf("g_z", [P, T, E], ctx=ctx)
        pairs = net.sbuf("g_pairs", [P, T * 4, 6], ctx=ctx)
        groups = net.sbuf("g_groups", [P, T, 4], ctx=ctx)
        group_rank = net.sbuf("g_grank", [P, T, 4], ctx=ctx)
        logits = net.psum("g_logits", [P, T, E], ctx)
        turned = net.psum("g_turned", [E, TOK], ctx)

        def ranks(order, dve, v, out, n, before):
            big = more[:, :, :, :].rearrange("p t a b -> p t (a b)")[:, :, 0:n * n]\
                .rearrange("p t (a b) -> p t a b", a=n)
            eq = same[:, :, :, :].rearrange("p t a b -> p t (a b)")[:, :, 0:n * n]\
                .rearrange("p t (a b) -> p t a b", a=n)
            shape = [P, T, n, n]
            other = v.unsqueeze(2).to_broadcast(shape)
            own = v.unsqueeze(3).to_broadcast(shape)
            order.step(dve.tensor_tensor(big, other, own, ALU.is_gt))
            order.step(dve.tensor_tensor(eq, other, own, ALU.is_equal))
            order.step(dve.tensor_tensor(eq, eq, before.unsqueeze(1).to_broadcast(shape), ALU.mult))
            order.step(dve.tensor_tensor(big, big, eq, ALU.add))
            order.step(dve.tensor_reduce(out, big, AX, ALU.add))

        with nc.Block(no_gpsimd_drain=True) as block:
            @block.tensor
            def _(pe):
                for t in range(T):
                    last = pe.matmul(logits[:, t, :], src[:, t * P:(t + 1) * P], weights, start=True, stop=True)
                last.then_inc(s.logits_ready, 1)
                pe.wait_ge(s.chosen, 1)
                for t in range(T):
                    last = pe.transpose(turned[:, t * P:(t + 1) * P], x[:, t, :], net.w("k", "ident"))
                last.then_inc(s.turned, 1)

            @block.scalar
            def _(act):
                if E == N_EXP:
                    act.wait_ge(s.steps, 2)
                    act.activation(y[:, :, :], x[:, :, :], ACT.Exp).then_inc(s.scored, 1)
                else:
                    act.wait_ge(s.logits_ready, 1)
                    act.activation(y[:, :, :], logits[:, :, :], ACT.Sigmoid).then_inc(s.scored, 1)

            @block.vector
            def _(dve):
                order = Order(dve, s.steps)
                shape = [P, T, E]

                def over(v):
                    return v.unsqueeze(2).to_broadcast(shape)

                dve.wait_ge(s.logits_ready, 1)
                if E == N_EXP:
                    order.step(dve.tensor_reduce(row[:, :], logits[:, :, :], AX, ALU.max))
                    order.step(dve.tensor_tensor(x[:, :, :], logits[:, :, :], over(row[:, :]), ALU.subtract))
                    dve.wait_ge(s.scored, 1)
                    order.step(dve.tensor_reduce(row[:, :], y[:, :, :], AX, ALU.add))
                    order.step(dve.reciprocal(row[:, :], row[:, :]))
                    order.step(dve.tensor_tensor(y[:, :, :], y[:, :, :], over(row[:, :]), ALU.mult))
                    ranks(order, dve, y[:, :, :], rank[:, :, :], E,
                          net.w("k", "before8").rearrange("p (a b) -> p a b", a=E))
                    order.step(dve.tensor_scalar(rank[:, :, :], rank[:, :, :], 2.0, None, ALU.is_lt))
                    dve.tensor_tensor(x[:, :, :], y[:, :, :], rank[:, :, :], ALU.mult).then_inc(s.chosen, 1)
                else:
                    dve.wait_ge(s.scored, 1)
                    order.step(dve.tensor_tensor(z[:, :, :], y[:, :, :],
                                                 net.w("g", "bias").unsqueeze(1).to_broadcast(shape), ALU.add))
                    four = z[:, :, :].rearrange("p t (g e) -> p (t g) e", g=4)
                    order.step(dve.tensor_tensor(pairs[:, :, 0:3], four[:, :, 0:3], four[:, :, 1:4], ALU.add))
                    order.step(dve.tensor_tensor(pairs[:, :, 3:5], four[:, :, 0:2], four[:, :, 2:4], ALU.add))
                    order.step(dve.tensor_tensor(pairs[:, :, 5:6], four[:, :, 0:1], four[:, :, 3:4], ALU.add))
                    order.step(dve.tensor_reduce(groups[:, :, :].rearrange("p t g -> p (t g)"),
                                                 pairs[:, :, :], AX, ALU.max))
                    before4 = net.w("k", "before16").rearrange("p (a b) -> p a b", a=16)[:, 0:4, 0:4]
                    ranks(order, dve, groups[:, :, :], group_rank[:, :, :], 4, before4)
                    order.step(dve.tensor_scalar(group_rank[:, :, :], group_rank[:, :, :], 2.0, None, ALU.is_lt))
                    spread = group_rank[:, :, :].rearrange("p t g -> p (t g)").unsqueeze(2)\
                        .to_broadcast([P, T * 4, 4])
                    order.step(dve.tensor_tensor(four, four, spread, ALU.mult))
                    ranks(order, dve, z[:, :, :], rank[:, :, :], E,
                          net.w("k", "before16").rearrange("p (a b) -> p a b", a=16))
                    order.step(dve.tensor_scalar(rank[:, :, :], rank[:, :, :], 4.0, None, ALU.is_lt))
                    order.step(dve.tensor_tensor(y[:, :, :], y[:, :, :], rank[:, :, :], ALU.mult))
                    order.step(dve.tensor_reduce(row[:, :], y[:, :, :], AX, ALU.add))
                    order.step(dve.tensor_scalar(row[:, :], row[:, :], 1e-20, None, ALU.add))
                    order.step(dve.reciprocal(row[:, :], row[:, :]))
                    dve.tensor_tensor(x[:, :, :], y[:, :, :], over(row[:, :]), ALU.mult).then_inc(s.chosen, 1)
                dve.wait_ge(s.turned, 1)
                dve.tensor_copy(shares, turned[:, :])
        nc.all_engine_barrier(sems_to_clear=span(s))


def attention(net, kind, src, dst, mask, scale, wq, wk, wv, wo, bq=None, bk=None, bv=None, bo=None,
              q_gain=None, k_gain=None):
    nc = net.nc
    small = kind in ("bucket", "window")
    rotary = kind == "local"
    heads = {"bucket": A_HEADS, "window": A_HEADS, "local": F_HEADS, "causal": D_HEADS}[kind]
    dim = A_DIM if small else D_DIM
    width = heads * dim
    parts = width // P
    seqs = 2
    pairs = heads // 2
    units = seqs * pairs
    all_heads = 2 * units
    lag = 2 if rotary else 1
    lot = P // dim
    lots = all_heads // lot
    last_step = all_heads + 4
    v_w = min(width, GROUP)
    n_v = 2 * (width // v_w)
    segs = [(0, [0, 1], 0), (1, [1], 256)] if kind == "window" else [(0, [0], 0), (1, [0, 1], 128)]
    s = net.signals("attn", [
        "x_ready", "proj_ready", "proj_read", "side_ready", "side_read", "k_spread", "qk_done", "scores_ready",
        "max_ready", "probs_ready", "turned", "turned_read", "mixed", "out_scaled", "out_turned", "out_copied",
        "extra_ready", "raw_ready", "cos_ready", "sum_ready", "norm_ready", "vec_steps", "act_steps"])

    def projects(u):
        return not small or u % pairs == 0

    def projected(u):
        return u // pairs + 1 if small else u + 1

    def v_piece(u):
        return u % pairs if u % pairs < n_v else None

    def lot_at(h, after):
        g = (h - after - 3 + 1) // lot - 1
        return g if 0 <= g < lots and lot * (g + 1) - 1 + 3 + after == h else None

    def closes(g):
        return g // (lots // seqs) if g is not None and (g + 1) % (lots // seqs) == 0 else None

    def step_heads(t):
        return [h for h in (2 * (t - lag), 2 * (t - lag) + 1) if 0 <= h <= last_step]

    turns = lag + (last_step + 2) // 2
    uses = {}
    for t in range(turns):
        if t < units and v_piece(t) is not None:
            uses["v", t] = len(uses) + 1
        if rotary and 1 <= t <= units:
            uses["rot", t - 1] = len(uses) + 1
        for j, h in enumerate((2 * (t - lag), 2 * (t - lag) + 1)):
            if 0 <= h <= last_step and closes(lot_at(h, 2)) is not None:
                uses["out", closes(lot_at(h, 2))] = len(uses) + 1
            if j == 0 and rotary and 1 <= t <= units:
                uses["squares", t - 1] = len(uses) + 1

    with ExitStack() as ctx:
        xs = net.sbuf("t_x", [P, seqs, LEN], ctx=ctx)
        qk = net.sbuf("t_qk", [P, 3, 2, LEN], ctx=ctx)
        v_sb = net.sbuf("t_v", [P, seqs, 2, width], ctx=ctx)
        k_one = net.sbuf("t_kone", [P, 3, 2, LEN], ctx=ctx) if small else None
        probs = net.sbuf("t_probs", [P, 3, 384], ctx=ctx)
        turned = net.sbuf("t_turned", [P, 3, 384], ctx=ctx)
        neg_max = net.sbuf("t_negmax", [P, all_heads, 2], ctx=ctx)
        sums = net.sbuf("t_sums", [P, all_heads, 2], ctx=ctx)
        zero_key = net.sbuf("t_zero", [P, all_heads], ctx=ctx)
        o_sb = net.sbuf("t_o", [P, 2, 2, P], ctx=ctx)
        o_t = net.sbuf("t_ot", [P, seqs, parts, LEN], ctx=ctx)
        if rotary:
            raw = net.sbuf("t_raw", [P, 2, 2 * LEN], ctx=ctx)
            sq = net.sbuf("t_sq", [P, 2, 2 * LEN], ctx=ctx)
            cosd = net.sbuf("t_cos", [P, 2, 2 * LEN], ctx=ctx)
            sind = net.sbuf("t_sin", [P, 2, 2 * LEN], ctx=ctx)
            size = sq
        proj_ps = net.psum("t_pp", [P, 2, LEN], ctx)
        side_ps = net.psum("t_side", [P, 512], ctx)
        sc = net.psum("t_sc", [P, 2, 512], ctx)
        tp = net.psum("t_tp", [P, 2, 512], ctx)
        op = net.psum("t_op", [P, 2, 512], ctx)
        ident = net.w("k", "ident")

        def head_q(h, tile):
            u, j = h // 2, h % 2
            cut = slice(tile * P, (tile + 1) * P)
            if small:
                return qk[:, u // pairs, 0, cut]
            return qk[64 * j:64 * j + 64, u % 3, 0, cut]

        def head_k(h, tiles):
            u, j = h // 2, h % 2
            cut = slice(tiles[0] * P, (tiles[-1] + 1) * P)
            if small:
                return k_one[:, u % 3, j, cut]
            return qk[64 * j:64 * j + 64, u % 3, 1, cut]

        with nc.Fori(0, SEQS // seqs) as i:
            with nc.Block(no_gpsimd_drain=True) as block:
                @block.tensor
                def _(pe):
                    def side(key):
                        if uses[key] > 1:
                            pe.wait_ge(s.side_read, uses[key] - 1)

                    def project(u):
                        r, c = u // pairs, 0 if small else u % pairs
                        if projected(u) > 1:
                            pe.wait_ge(s.raw_ready if rotary else s.proj_read if small else s.qk_done,
                                       projected(u) - 1)
                        for n, wt in enumerate((wq, wk)):
                            last = pe.matmul(proj_ps[:, n, :], wt[:, c * P:(c + 1) * P], xs[:, r, :],
                                             start=True, stop=True)
                        last.then_inc(s.proj_ready, 1)

                    def project_v(u):
                        r, n = u // pairs, v_piece(u)
                        side(("v", u))
                        pe.matmul(side_ps[:, 0:v_w], xs[:, r, (n % 2) * P:(n % 2 + 1) * P],
                                  wv[:, (n // 2) * v_w:(n // 2 + 1) * v_w], start=True, stop=True)\
                          .then_inc(s.side_ready, 1)

                    def scores(h):
                        if small:
                            pe.wait_ge(s.k_spread, h // 2 + 1)
                        else:
                            pe.wait_ge(s.qk_done, h // 2 + 1)
                        if h >= 2:
                            pe.wait_ge(s.probs_ready, h - 1)
                        pe.matmul(sc[:, h % 2, 0:384], net.ident16[:, :], mask[:, :], start=True, stop=False)
                        for q, ks, at in segs:
                            last = pe.matmul(sc[:, h % 2, at:at + P * len(ks)], head_q(h, q), head_k(h, ks),
                                             start=False, stop=(q == 1))
                        last.then_inc(s.scores_ready, 1)

                    def turn(h):
                        pe.wait_ge(s.probs_ready, h + 1)
                        if h >= 2:
                            pe.wait_ge(s.turned_read, h - 1)
                        for n in range(3):
                            last = pe.transpose(tp[:, h % 2, n * P:(n + 1) * P],
                                                probs[:, h % 3, n * P:(n + 1) * P], ident)
                        last.then_inc(s.turned, 1)

                    def mix(h):
                        r, hr, g, j = h // heads, h % heads, h // lot, h % lot
                        pe.wait_ge(s.turned_read, h + 1)
                        piece = 2 * (hr * dim // v_w) + 1
                        pe.wait_ge(s.side_read, uses["v", r * pairs + piece])
                        if j == 0 and g >= 2:
                            pe.wait_ge(s.out_copied, g - 1)
                        for q, ks, at0 in segs:
                            for n, k in enumerate(ks):
                                at = at0 + P * n
                                last = pe.matmul(op[:, g % 2, q * P + j * dim:q * P + (j + 1) * dim],
                                                 turned[:, h % 3, at:at + P],
                                                 v_sb[:, r, k, hr * dim:(hr + 1) * dim],
                                                 start=(n == 0), stop=(n == len(ks) - 1))
                        last.then_inc(s.mixed, 1)

                    def turn_out(g):
                        pe.wait_ge(s.out_scaled, g + 1)
                        for q in range(2):
                            last = pe.transpose(op[:, g % 2, 256 + q * P:256 + (q + 1) * P], o_sb[:, g % 2, q, :],
                                                ident)
                        last.then_inc(s.out_turned, 1)

                    def project_out(r):
                        pe.wait_ge(s.out_copied, (r + 1) * lots // seqs)
                        side(("out", r))
                        for c in range(parts):
                            last = pe.matmul(side_ps[:, 0:LEN], wo[:, c * P:(c + 1) * P], o_t[:, r, c, :],
                                             start=(c == 0), stop=(c == parts - 1))
                        last.then_inc(s.side_ready, 1)

                    pe.wait_ge(s.x_ready, 1)
                    for t in range(turns):
                        if t < units:
                            if projects(t):
                                project(t)
                            if v_piece(t) is not None:
                                project_v(t)
                        if rotary and 1 <= t <= units:
                            u = t - 1
                            pe.wait_ge(s.raw_ready, u + 1)
                            side(("rot", u))
                            pe.matmul(side_ps[:, :], net.w("k", "rot"), raw[:, u % 2, :], start=True, stop=True)\
                              .then_inc(s.side_ready, 1)
                        for j, h in enumerate((2 * (t - lag), 2 * (t - lag) + 1)):
                            if 0 <= h <= last_step:
                                if h < all_heads:
                                    scores(h)
                                if 0 <= h - 2 < all_heads:
                                    turn(h - 2)
                                if 0 <= h - 3 < all_heads:
                                    mix(h - 3)
                                if lot_at(h, 1) is not None:
                                    turn_out(lot_at(h, 1))
                                if closes(lot_at(h, 2)) is not None:
                                    project_out(closes(lot_at(h, 2)))
                            if j == 0 and rotary and 1 <= t <= units:
                                side(("squares", u))
                                pe.matmul(side_ps[:, :], net.w("k", "pairs"), sq[:, u % 2, :],
                                          start=True, stop=True).then_inc(s.side_ready, 1)

                @block.scalar
                def _(act):
                    order = Order(act, s.act_steps)
                    nc.scalar.preload_act_table_set("natural_log_exp_and_others")
                    for t in range(turns):
                        if rotary and t < units:
                            u = t
                            act.wait_ge(s.proj_ready, u + 1)
                            if u >= 2:
                                act.wait_ge(s.side_read, uses["squares", u - 2])
                                act.wait_ge(s.cos_ready, u - 1)
                                act.wait_ge(s.qk_done, u - 1)
                            for n, gain in enumerate((q_gain, k_gain)):
                                act.activation(raw[:, u % 2, n * LEN:(n + 1) * LEN], proj_ps[:, n, :], ACT.Copy,
                                               scale=gain)
                            act.activation(sq[:, u % 2, :], proj_ps[:, :, :].rearrange("p a t -> p (a t)"),
                                           ACT.Square).then_inc(s.raw_ready, 1)
                        for j, h in enumerate((2 * (t - lag), 2 * (t - lag) + 1)):
                            if 0 <= h < all_heads:
                                act.wait_ge(s.max_ready, h + 1)
                                if h >= 3:
                                    act.wait_ge(s.turned, h - 2)
                                for n, (q, ks, at) in enumerate(segs):
                                    w = P * len(ks)
                                    last = act.activation(probs[:, h % 3, at:at + w], sc[:, h % 2, at:at + w],
                                                          ACT.Exp, bias=neg_max[:, h, n:n + 1],
                                                          accum_out=sums[:, h, n:n + 1])
                                last.then_inc(s.probs_ready, 1)
                                if kind == "bucket" and h % lot == lot - 1:
                                    act.activation(zero_key[:, h + 1 - lot:h + 1], neg_max[:, h + 1 - lot:h + 1, 0],
                                                   ACT.Exp).then_inc(s.extra_ready, 1)
                            if j == 0 and rotary and 1 <= t <= units:
                                u = t - 1
                                act.wait_ge(s.side_read, uses["squares", u])
                                order.step(act.activation(size[:, u % 2, :], size[:, u % 2, :], ACT.Ln,
                                                          scale=float(2 ** 20)))
                                act.activation(size[:, u % 2, :], size[:, u % 2, :], ACT.Exp, scale=-0.5,
                                               bias=net.w("k", "back")).then_inc(s.norm_ready, 1)

                @block.gpsimd
                def _(pool):
                    if rotary:
                        for t in range(units + 1):
                            if t < units:
                                pool.wait_ge(s.raw_ready, t + 1)
                                if t >= 2:
                                    pool.wait_ge(s.sum_ready, t - 1)
                                pool.tensor_tensor(cosd[:, t % 2, :], raw[:, t % 2, :],
                                                   net.w("k", "qcos", 0, 2 * LEN), ALU.mult).then_inc(s.cos_ready, 1)
                            if t >= 1:
                                u = t - 1
                                pool.wait_ge(s.side_read, uses["rot", u])
                                pool.wait_ge(s.cos_ready, u + 1)
                                pool.tensor_tensor(sind[:, u % 2, :], sind[:, u % 2, :], cosd[:, u % 2, :], ALU.add)\
                                    .then_inc(s.sum_ready, 1)
                    if small:
                        for u in range(units):
                            shape = [P, 2, LEN]
                            c = u % pairs
                            pool.wait_ge(s.proj_read, projected(u))
                            if u >= 3:
                                pool.wait_ge(s.scores_ready, 2 * (u - 3) + 2)
                            pool.tensor_tensor(k_one[:, u % 3, :, :],
                                               qk[:, u // pairs, 1, :].unsqueeze(1).to_broadcast(shape),
                                               net.w("k", "heads8", 2 * c, 2 * c + 2).unsqueeze(2)
                                               .to_broadcast(shape), ALU.mult).then_inc(s.k_spread, 1)

                @block.vector
                def _(dve):
                    order = Order(dve, s.vec_steps)

                    def read_projection(u):
                        c = 0 if small else u % pairs
                        slot = u // pairs if small else u % 3
                        dve.wait_ge(s.proj_ready, projected(u))
                        if not small and u >= 3:
                            dve.wait_ge(s.scores_ready, 2 * (u - 3) + 2)
                        dve.tensor_scalar(qk[:, slot, 0, :], proj_ps[:, 0, :], bq[:, c:c + 1], scale,
                                          ALU.add, ALU.mult)
                        dve.tensor_scalar(qk[:, slot, 1, :], proj_ps[:, 1, :], bk[:, c:c + 1], None, ALU.add)\
                           .then_inc(s.proj_read if small else s.qk_done, 1)

                    def read_v(u):
                        r, n = u // pairs, v_piece(u)
                        cut = slice((n // 2) * v_w, (n // 2 + 1) * v_w)
                        dve.wait_ge(s.side_ready, uses["v", u])
                        out = v_sb[:, r, n % 2, cut]
                        if bv is None:
                            dve.tensor_copy(out, side_ps[:, 0:v_w]).then_inc(s.side_read, 1)
                        else:
                            dve.tensor_tensor(out, side_ps[:, 0:v_w], bv[:, cut], ALU.add)\
                               .then_inc(s.side_read, 1)

                    def maxima(h):
                        dve.wait_ge(s.scores_ready, h + 1)
                        (q0, k0, a0), (q1, k1, a1) = segs
                        first = dve.tensor_reduce(neg_max[:, h, 0:1], sc[:, h % 2, a0:a0 + P * len(k0)], AX, ALU.max,
                                                  negate=True)
                        if kind == "bucket":
                            order.step(first)
                            dve.tensor_scalar(neg_max[:, h, 0:1], neg_max[:, h, 0:1], net.w("k", "floor"), None,
                                              ALU.min)
                        dve.tensor_reduce(neg_max[:, h, 1:2], sc[:, h % 2, a1:a1 + P * len(k1)], AX, ALU.max,
                                          negate=True).then_inc(s.max_ready, 1)

                    def copy_turned(h):
                        dve.wait_ge(s.turned, h + 1)
                        if h >= 3:
                            dve.wait_ge(s.mixed, h - 2)
                        dve.tensor_copy(turned[:, h % 3, :], tp[:, h % 2, 0:384]).then_inc(s.turned_read, 1)

                    def scale_out(g):
                        mine = sums[:, g * lot:(g + 1) * lot, :]
                        dve.wait_ge(s.mixed, (g + 1) * lot)
                        if kind == "bucket":
                            dve.wait_ge(s.extra_ready, g + 1)
                            order.step(dve.scalar_tensor_tensor(
                                out=mine[:, :, 0], in0=zero_key[:, g * lot:(g + 1) * lot], scalar=net.w("k", "extra"),
                                in1=mine[:, :, 0], op0=ALU.mult, op1=ALU.add))
                        order.step(dve.reciprocal(mine, mine))
                        if g >= 2:
                            dve.wait_ge(s.out_turned, g - 1)
                        shape = [P, 2, lot, dim]
                        part = op[:, g % 2, 0:2 * P].rearrange("p (q h d) -> p q h d", q=2, h=lot)
                        out = o_sb[:, g % 2, :, :].rearrange("p q (h d) -> p q h d", h=lot)
                        over = mine.rearrange("p h q -> p q h").unsqueeze(3).to_broadcast(shape)
                        done = dve.tensor_tensor(out, part, over, ALU.mult)
                        if kind == "window":
                            order.step(done)
                            done = dve.tensor_tensor(o_sb[:, g % 2, :, :], o_sb[:, g % 2, :, :],
                                                     net.w("k", "seen").unsqueeze(2).to_broadcast([P, 2, P]), ALU.mult)
                        done.then_inc(s.out_scaled, 1)

                    def copy_out(g):
                        dve.wait_ge(s.out_turned, g + 1)
                        r, c = g // (lots // seqs), g % (lots // seqs)
                        dve.tensor_copy(o_t[:, r, c, :], op[:, g % 2, 2 * P:4 * P]).then_inc(s.out_copied, 1)

                    def add_out(r):
                        dve.wait_ge(s.side_ready, uses["out", r])
                        to = dst[:, r * LEN:][:, bass.ds(i * (seqs * LEN), LEN)]
                        if bo is None:
                            dve.tensor_tensor(to, to, side_ps[:, 0:LEN], ALU.add).then_inc(s.side_read, 1)
                        else:
                            dve.scalar_tensor_tensor(out=to, in0=side_ps[:, 0:LEN], scalar=bo, in1=to,
                                                     op0=ALU.add, op1=ALU.add).then_inc(s.side_read, 1)

                    at = i * (seqs * LEN)
                    flat = xs[:, :, :].rearrange("p s t -> p (s t)")
                    if rotary:
                        dve.tensor_copy(flat[0:64, :], src[0:64, bass.ds(at, seqs * LEN)])
                        order.step(dve.tensor_copy(flat[64:P, 1:], src[64:P, bass.ds(at, seqs * LEN - 1)]))
                        dve.memset(xs[64:P, :, 0:1], 0.0).then_inc(s.x_ready, 1)
                    else:
                        dve.tensor_copy(flat, src[:, bass.ds(at, seqs * LEN)]).then_inc(s.x_ready, 1)
                    for t in range(turns):
                        if rotary and 0 <= t - 2 < units:
                            u = t - 2
                            dve.wait_ge(s.norm_ready, u + 1)
                            dve.wait_ge(s.sum_ready, u + 1)
                            if u >= 3:
                                dve.wait_ge(s.scores_ready, 2 * (u - 3) + 2)
                            dve.tensor_tensor(qk[:, u % 3, :, :].rearrange("p a t -> p (a t)"), sind[:, u % 2, :],
                                              size[:, u % 2, :], ALU.mult).then_inc(s.qk_done, 1)
                        if t < units:
                            if projects(t) and not rotary:
                                read_projection(t)
                            if v_piece(t) is not None:
                                read_v(t)
                        if rotary and 1 <= t <= units:
                            u = t - 1
                            dve.wait_ge(s.side_ready, uses["rot", u])
                            dve.tensor_tensor(sind[:, u % 2, :], side_ps[:, :], net.w("k", "qsin", 0, 2 * LEN),
                                              ALU.mult).then_inc(s.side_read, 1)
                        for j, h in enumerate((2 * (t - lag), 2 * (t - lag) + 1)):
                            if 0 <= h <= last_step:
                                if h < all_heads:
                                    maxima(h)
                                if 0 <= h - 2 < all_heads:
                                    copy_turned(h - 2)
                                if lot_at(h, 0) is not None:
                                    scale_out(lot_at(h, 0))
                                if lot_at(h, 1) is not None:
                                    copy_out(lot_at(h, 1))
                                if closes(lot_at(h, 2)) is not None:
                                    add_out(closes(lot_at(h, 2)))
                            if j == 0 and rotary and 1 <= t <= units:
                                dve.wait_ge(s.side_ready, uses["squares", u])
                                dve.tensor_scalar(size[:, u % 2, :], side_ps[:, :], 1e-24, None, ALU.max)\
                                   .then_inc(s.side_read, 1)
            nc.all_engine_barrier(sems_to_clear=span(s))


def selective_scan(net, src, dst):
    nc = net.nc
    s = net.signals("scan", [
        "rates_ready", "x_ready", "in_ready", "conv_done", "z_done", "x_acted", "low_ready", "low_copied",
        "high_ready", "split_done", "dt_ready", "dt_biased", "dt_steps", "delta_ready", "rows_ready", "driven",
        "decay_ready", "c_copied", "scanned", "hc_ready", "summed", "skipped", "gated", "out_ready", "steps"])
    C, R = D_INNER // P, 2
    T = R * LEN
    with ExitStack() as ctx:
        xi = net.sbuf("m_xi", [P, C, T], ctx=ctx)
        z = net.sbuf("m_z", [P, C, T], ctx=ctx)
        high = net.sbuf("m_high", [STATE, 2, T], F32R, ctx=ctx)
        rest = net.sbuf("m_rest", [STATE, 2, T], F32R, ctx=ctx)
        spread = net.sbuf("m_spread", [STATE, P], F32R, ctx=ctx)
        delta = net.sbuf("m_delta", [P, C, T], ctx=ctx)
        dx = net.sbuf("m_dx", [P, C, T], ctx=ctx)
        decay = net.sbuf("m_decay", [P, 2, C, R, LEN], ctx=ctx)
        drive = net.sbuf("m_drive", [P, 2, C * T], ctx=ctx)
        state = net.sbuf("m_state", [P, 2, C, T], ctx=ctx)
        c_sb = net.sbuf("m_c", [P, 2, T], ctx=ctx)
        hc = net.sbuf("m_hc", [P, 2, C, T], ctx=ctx)
        rates = net.sbuf("m_rates", [P, C * STATE], ctx=ctx)
        pad_w = LEN + 4
        padded = drive[:, :, :].rearrange("p b n -> p (b n)")[:, 0:C * R * pad_w]\
            .rearrange("p (c r t) -> p c r t", c=C, r=R)
        conv, soft = hc[:, 0, :, :], hc[:, 1, :, :]
        pre = dx
        y = state[:, 0, :, :]
        xs, low = state[:, 0, 0, :], state[0:DT_RANK, 1, 0, :]
        a_ps = net.psum("m_aps", [P, C, T], ctx)
        rows_ps = net.psum("m_rps", [P, 4, T], ctx)
        low_ps = net.psum("m_lps", [P, T], ctx)

        def by_seq(t, c):
            return t[:, c, :].rearrange("p (r t) -> p r t", r=R)

        with nc.Block(no_gpsimd_drain=True) as block:
            @block.scalar
            def _(act):
                act.activation(rates[:, :], net.w("m", "alog"), ACT.Exp).then_inc(s.rates_ready, 1)

            @block.vector
            def _(dve):
                dve.wait_ge(s.rates_ready, 1)
                dve.tensor_scalar(rates[:, :], rates[:, :], -1.0, None, ALU.mult)
                dve.memset(decay[:, :, :, :, 0:1].rearrange("p b c r o -> p (b c r) o"), 0.0)
                dve.tensor_copy(spread[:, :], net.w("k", "ident", rows=STATE))
        nc.all_engine_barrier(sems_to_clear=span(s))

        with nc.Fori(0, SEQS // R) as i:
            with nc.Block(no_gpsimd_drain=True) as block:
                @block.tensor
                def _(pe):
                    pe.wait_ge(s.x_ready, 1)
                    for n in range(2 * C):
                        to = a_ps[:, n, :] if n < C else rows_ps[:, n - C, :]
                        pe.matmul(to, net.w("m", "win", n * P, (n + 1) * P), xs, start=True, stop=True)\
                          .then_inc(s.in_ready, 1)
                    pe.wait_ge(s.x_acted, C)
                    wx = net.w("m", "wx").rearrange("p (c n) -> p c n", c=C)
                    for out, a, b in ((low_ps[0:DT_RANK, :], 0, DT_RANK),
                                      (rows_ps[0:STATE, 2, :], DT_RANK, DT_RANK + STATE),
                                      (rows_ps[0:STATE, 3, :], DT_RANK + STATE, DT_RANK + 2 * STATE)):
                        for c in range(C):
                            last = pe.matmul(out, wx[:, c, a:b], xi[:, c, :], start=(c == 0), stop=(c == C - 1))
                        last.then_inc(s.low_ready, 1)
                    pe.wait_ge(s.low_copied, 1)
                    for c in range(C):
                        pe.matmul(a_ps[:, c, :], net.w("m", "wdt", c * P, (c + 1) * P, rows=DT_RANK),
                                  low, start=True, stop=True).then_inc(s.dt_ready, 1)
                    pe.wait_ge(s.z_done, C)
                    pe.wait_ge(s.split_done, 2)
                    pe.wait_ge(s.dt_biased, C)

                    def add_up(n):
                        pe.wait_ge(s.hc_ready, n + 1)
                        for c in range(C):
                            last = pe.matmul(a_ps[:, c, :], net.w("k", "ident"), hc[:, n % 2, c, :],
                                             start=(n == 0), stop=(n == STATE - 1))
                        last.then_inc(s.summed, 1)

                    for n in range(STATE):
                        if n >= 2:
                            pe.wait_ge(s.driven, n - 1)
                            pe.wait_ge(s.c_copied, n - 1)
                        row = spread[:, n:n + 1].to_broadcast([STATE, P])
                        for m in range(2):
                            pe.matmul(rows_ps[:, 2 * (n % 2) + m, :], row, high[:, m, :], start=True, stop=False)
                            last = pe.matmul(rows_ps[:, 2 * (n % 2) + m, :], row, rest[:, m, :],
                                             start=False, stop=True)
                        last.then_inc(s.rows_ready, 1)
                        if n >= 3:
                            add_up(n - 3)
                    for n in range(STATE - 3, STATE):
                        add_up(n)
                    for c in range(C):
                        pe.wait_ge(s.gated, c + 1)
                        last = pe.matmul(low_ps[:, :], net.w("m", "wout", c * P, (c + 1) * P), y[:, c, :],
                                         start=(c == 0), stop=(c == C - 1))
                    last.then_inc(s.out_ready, 1)

                @block.scalar
                def _(act):
                    for c in range(C):
                        act.wait_ge(s.in_ready, C + c + 1)
                        act.activation(z[:, c, :], rows_ps[:, c, :], ACT.Silu).then_inc(s.z_done, 1)
                    for c in range(C):
                        act.wait_ge(s.conv_done, c + 1)
                        act.activation(xi[:, c, :], conv[:, c, :], ACT.Silu, bias=net.w("m", "cb", c, c + 1))\
                           .then_inc(s.x_acted, 1)
                    nc.scalar.preload_act_table_set("natural_log_exp_and_others")
                    for m in range(2):
                        act.wait_ge(s.low_ready, 2 + m)
                        act.activation(high[:, m, :], rows_ps[0:STATE, 2 + m, :], ACT.Copy)\
                           .then_inc(s.high_ready, 1)
                    order = Order(act, s.dt_steps)
                    act.wait_ge(s.dt_biased, C)
                    order.step(act.activation(soft, pre[:, :, :], ACT.Abs))
                    order.step(act.activation(soft, soft, ACT.Exp, scale=-1.0))
                    order.step(act.activation(soft, soft, ACT.Ln, bias=net.w("k", "one")))
                    act.wait_ge(s.delta_ready, 1)
                    for n in range(STATE):
                        if n >= 2:
                            act.wait_ge(s.scanned, n - 1)
                        for c in range(C):
                            last = act.activation(decay[:, n % 2, c, :, 1:LEN], by_seq(delta, c)[:, :, 1:LEN],
                                                  ACT.Exp, scale=rates[:, c * STATE + n:c * STATE + n + 1])
                        last.then_inc(s.decay_ready, 1)
                        act.wait_ge(s.rows_ready, n + 1)
                        if n >= 2:
                            act.wait_ge(s.hc_ready, n - 1)
                        act.activation(c_sb[:, n % 2, :], rows_ps[:, 2 * (n % 2) + 1, :], ACT.Copy)\
                           .then_inc(s.c_copied, 1)

                @block.gpsimd
                def _(pool):
                    for n in range(STATE):
                        b = n % 2
                        pool.wait_ge(s.scanned, n + 1)
                        pool.wait_ge(s.c_copied, n + 1)
                        if n >= 2:
                            pool.wait_ge(s.summed, n - 1)
                        pool.tensor_tensor(hc[:, b, :, :], state[:, b, :, :],
                                           c_sb[:, b, :].unsqueeze(1).to_broadcast([P, C, T]), ALU.mult)\
                            .then_inc(s.hc_ready, 1)
                    for c in range(C):
                        pool.wait_ge(s.skipped, c + 1)
                        pool.tensor_tensor(y[:, c, :], y[:, c, :], z[:, c, :], ALU.mult).then_inc(s.gated, 1)

                @block.vector
                def _(dve):
                    order = Order(dve, s.steps)
                    dve.tensor_copy(xs, src[:, bass.ds(i * T, T)]).then_inc(s.x_ready, 1)
                    dve.memset(padded[:, :, :, 0:3].rearrange("p c r t -> p (c r) t"), 0.0)
                    for c in range(C):
                        dve.wait_ge(s.in_ready, c + 1)
                        order.step(dve.tensor_copy(padded[:, c, :, 3:3 + LEN], by_seq(a_ps, c)))
                    for j in range(4):
                        for c in range(C):
                            tap = net.w("m", "cw", c * 4 + j, c * 4 + j + 1)
                            there, out = padded[:, c, :, j:j + LEN], by_seq(conv, c)
                            if j == 0:
                                ins = dve.tensor_scalar(out, there, tap, None, ALU.mult)
                            else:
                                ins = dve.scalar_tensor_tensor(out=out, in0=there, scalar=tap, in1=out,
                                                               op0=ALU.mult, op1=ALU.add)
                            if j == 3:
                                ins.then_inc(s.conv_done, 1)
                            elif c == C - 1:
                                order.step(ins)
                    dve.wait_ge(s.low_ready, 1)
                    dve.tensor_copy(low, low_ps[0:DT_RANK, :]).then_inc(s.low_copied, 1)
                    for m in range(2):
                        dve.wait_ge(s.high_ready, m + 1)
                        dve.tensor_tensor(rest[:, m, :], rows_ps[0:STATE, 2 + m, :],
                                          high[:, m, :].bitcast(F32), ALU.subtract).then_inc(s.split_done, 1)
                    for c in range(C):
                        dve.wait_ge(s.dt_ready, c + 1)
                        dve.tensor_scalar(pre[:, c, :], a_ps[:, c, :], net.w("m", "bdt", c, c + 1), None, ALU.add)\
                           .then_inc(s.dt_biased, 1)
                    dve.wait_ge(s.dt_biased, C)
                    dve.wait_ge(s.dt_steps, 3)
                    dve.scalar_tensor_tensor(out=delta[:, :, :], in0=pre[:, :, :], scalar=0.0, in1=soft,
                                             op0=ALU.max, op1=ALU.add).then_inc(s.delta_ready, 1)
                    dve.wait_ge(s.delta_ready, 1)
                    dve.wait_ge(s.x_acted, C)
                    order.step(dve.tensor_tensor(dx[:, :, :], delta[:, :, :], xi[:, :, :], ALU.mult))

                    def driven(n):
                        dve.wait_ge(s.rows_ready, n + 1)
                        dve.tensor_tensor(drive[:, n % 2, :].rearrange("p (c t) -> p c t", c=C), dx[:, :, :],
                                          rows_ps[:, 2 * (n % 2), :].unsqueeze(1).to_broadcast([P, C, T]), ALU.mult)\
                           .then_inc(s.driven, 1)

                    driven(0)
                    for n in range(STATE):
                        b = n % 2
                        if n >= 1:
                            dve.wait_ge(s.scanned, n)
                        if n + 1 < STATE:
                            driven(n + 1)
                        dve.wait_ge(s.driven, n + 1)
                        dve.wait_ge(s.decay_ready, n + 1)
                        if n >= 2:
                            dve.wait_ge(s.hc_ready, n - 1)
                        dve.tensor_tensor_scan(state[:, b, :, :].rearrange("p c t -> p (c t)"),
                                               decay[:, b, :, :, :].rearrange("p c r t -> p (c r t)"),
                                               drive[:, b, :], 0.0, ALU.mult, ALU.add).then_inc(s.scanned, 1)
                    dve.wait_ge(s.summed, STATE)
                    for c in range(C):
                        dve.scalar_tensor_tensor(out=y[:, c, :], in0=xi[:, c, :],
                                                 scalar=net.w("m", "dskip", c, c + 1), in1=a_ps[:, c, :],
                                                 op0=ALU.mult, op1=ALU.add).then_inc(s.skipped, 1)
                    dve.wait_ge(s.out_ready, 1)
                    to = dst[:, bass.ds(i * T, T)]
                    dve.tensor_tensor(to, to, low_ps[:, :], ALU.add)
            nc.all_engine_barrier(sems_to_clear=span(s))


def model(nc, x_in, blobs, out, stages):
    with ExitStack() as ctx:
        net = Net(nc, ctx)
        X = net.sbuf("X", [P, TOK])
        H = net.sbuf("H", [P, TOK])
        G = net.sbuf("G", [P, TOK])
        width = {g: starts(g)[1] for g in COLS}
        net.weights = {g: net.sbuf(f"w_{g}", [P, width[g]]) for g in COLS if g not in "ehq"}
        region = net.sbuf("w_experts", [P, max(width["e"], width["h"])])
        net.weights["e"] = net.weights["h"] = region
        net.ident16 = net.sbuf("ident16", [P, P], BF16)
        masks = {m: net.sbuf(f"mask_{m}", [P, 384], BF16) for m in ("m_bucket", "m_local", "m_causal", "m_window")}
        loaded = ctx.enter_context(nc.semaphore("loaded"))
        experts_loaded = ctx.enter_context(nc.semaphore("experts_loaded"))
        stored = ctx.enter_context(nc.semaphore("stored"))

        def load(sp, g, sem):
            sp.dma_start(net.weights[g][:, 0:width[g]], blobs[g]).then_inc(sem, 16)

        early = ["k", "a", "f"]
        late = ["m", "g", "c", "d"]
        with ExitStack() as first:
            net.weights["q"] = net.sbuf("w_q", [P, width["q"]], ctx=first)
            with nc.Block() as block:
                @block.sync
                def _(sp):
                    for g in ["q"] + early:
                        load(sp, g, loaded)
                    sp.dma_start(X[:, :], x_in).then_inc(loaded, 16)
                    for g in late:
                        load(sp, g, experts_loaded)
                    load(sp, "e" if "M" in stages else "h", experts_loaded)
                    sp.wait_ge(loaded, 16 * (2 + len(early)))

                @block.vector
                def _(dve):
                    dve.wait_ge(loaded, 16 * (2 + len(early)))
                    dve.tensor_copy(net.ident16[:, :], net.w("k", "ident"))
                    for m, t in masks.items():
                        dve.tensor_copy(t[:, :], net.w("q", m))

        def wait_experts(n):
            with nc.Block(no_gpsimd_drain=True) as block:
                @block.sync
                def _(sp):
                    sp.wait_ge(experts_loaded, n)

        def stage_a(here):
            norm(net, "a0", X, H)
            norm(net, "a1", H, G, gain=net.w("a", "g1"), bias=net.w("a", "c1"))
            w = net.w("a", "wqkv")
            attention(net, "bucket", G, H, masks["m_bucket"], A_DIM ** -0.5, w[:, 0:P], w[:, P:2 * P],
                      w[:, 2 * P:3 * P], net.w("a", "wo"), net.w("a", "bq"), net.w("a", "bk"),
                      net.w("a", "bv"), net.w("a", "bo"))
            norm(net, "a2", H, G, gain=net.w("a", "g2"), bias=net.w("a", "c2"))
            chunks = [dict(rows=P, gate=net.w("a", "w1", c * P, (c + 1) * P), up=None,
                           down=net.w("a", "w2", c * P, (c + 1) * P), gate_bias=net.w("a", "b1", c, c + 1))
                      for c in range(4)]
            mlp(net, G, X, chunks, ACT.Gelu, out_bias=net.w("a", "b2"), also=H)

        def stage_f(here):
            norm(net, "f0", X, H)
            for l in (0, 1):
                inner = F_HEADS * F_DIM
                w = net.w("f", f"wqkv{l}")
                attention(net, "local", H, H, masks["m_local"], None, w[:, 0:inner], w[:, inner:2 * inner],
                          w[:, 2 * inner:], net.w("f", f"wo{l}"), q_gain=net.w("f", f"qs{l}"),
                          k_gain=net.w("f", f"ks{l}"))
                norm(net, f"f{l}", H, G, gain=net.w("f", f"g{l}"), bias=net.w("f", f"c{l}"), shift=True)
                chunks = []
                for c in range(3):
                    rows = min(P, HID_F - c * P)
                    chunks.append(dict(
                        rows=rows, up=net.w("f", f"w1{l}", c * P, c * P + rows),
                        gate=net.w("f", f"w1{l}", HID_F + c * P, HID_F + c * P + rows),
                        down=net.w("f", f"w2{l}", c * P, (c + 1) * P, rows=rows),
                        up_bias=net.w("f", f"ba{l}", c, c + 1, rows=rows),
                        gate_bias=net.w("f", f"bg{l}", c, c + 1, rows=rows)))
                if l == 0:
                    mlp(net, G, H, chunks, ACT.Gelu, out_bias=net.w("f", "b20"))
                else:
                    mlp(net, G, X, chunks, ACT.Gelu, out_bias=net.w("f", "b21"), also=H)

        def stage_m(here):
            norm(net, "m0", X, H)
            norm(net, "m1", H, G, root_mean_square=True, gain=net.w("m", "r1"))
            selective_scan(net, G, H)
            norm(net, "m2", H, G, root_mean_square=True, gain=net.w("m", "r2"))
            shares = net.sbuf("shares", [E2, TOK], ctx=here)
            gate(net, G, shares[0:N_EXP, :], N_EXP)
            chunks = []
            for e in range(N_EXP):
                for c in range(FFN // P):
                    at = e * FFN + c * P
                    chunks.append(dict(rows=P, gate=net.w("e", "wg", at, at + P), up=net.w("e", "wu", at, at + P),
                                       down=net.w("e", "wd", at, at + P), share_key=e,
                                       share=net.w("k", "ident", e, e + 1, rows=N_EXP).to_broadcast([N_EXP, P])))
            mlp(net, G, X, chunks, ACT.Silu, also=H, shares=shares[0:N_EXP, :])

        def stage_c(here):
            norm(net, "c0", X, H)
            attention(net, "window", H, X, masks["m_window"], A_DIM ** -0.5, net.w("c", "wq"), net.w("c", "wk"),
                      net.w("c", "wv"), net.w("c", "wo"), net.w("c", "bq"), net.w("c", "bk"),
                      net.w("c", "bv"), net.w("c", "bo"))

        def stage_h(here):
            norm(net, "h0", X, H)
            shares = net.sbuf("shares", [E2, TOK], ctx=here)
            gate(net, H, shares[:, :], E2)
            chunks = []
            for c in range((ROUTED + SHARED + P - 1) // P):
                at = c * P
                rows = min(P, ROUTED + SHARED - at)
                lot = dict(rows=rows, gate=net.w("h", "wg", at, at + rows), up=net.w("h", "wu", at, at + rows),
                           down=net.w("h", "wd", at, at + P, rows=rows))
                if at < ROUTED:
                    lot.update(share_key=c, share=net.w("h", "expert", at, at + P, rows=E2))
                chunks.append(lot)
            mlp(net, H, X, chunks, ACT.Silu, shares=shares[:, :])

        def stage_d(here):
            norm(net, "d0", X, H)
            attention(net, "causal", H, X, masks["m_causal"], D_DIM ** -0.5, net.w("d", "wq"), net.w("d", "wk"),
                      net.w("d", "wv"), net.w("d", "wo"), net.w("d", "bq"), net.w("d", "bk"),
                      net.w("d", "bv"), net.w("d", "bo"))

        came = 16 * (len(late) + 1)
        for n, st in enumerate(stages):
            if n == min([stages.find(k) for k in "MCHD" if k in stages] or [99]):
                wait_experts(came)
            with ExitStack() as here:
                dict(A=stage_a, F=stage_f, M=stage_m, C=stage_c, H=stage_h, D=stage_d)[st](here)
            if st == "M":
                with nc.Block(no_gpsimd_drain=True) as block:
                    @block.sync
                    def _(sp):
                        load(sp, "h", experts_loaded)
                came += 16
                second = came
            if "M" in stages[:n + 1] and stages[n + 1:n + 2] == "H":
                wait_experts(second)

        with nc.Block() as block:
            @block.sync
            def _(sp):
                sp.dma_start(out, X[:, :]).then_inc(stored, 16)
                sp.wait_ge(stored, 16)



def _rows(a, n=P):
    a = np.asarray(a, np.float32)
    return np.concatenate([a, np.zeros((n - a.shape[0],) + a.shape[1:], np.float32)]) if a.shape[0] < n else a


def _col(b):
    b = np.asarray(b, np.float32).reshape(-1)
    n = -(-b.size // P)
    return np.ascontiguousarray(_rows(b, n * P).reshape(n, P).T)


def _stack(w):
    w = np.asarray(w, np.float32)
    k = -(-w.shape[0] // P)
    return np.ascontiguousarray(_rows(w, k * P).reshape(k, P, -1).transpose(1, 0, 2)).reshape(P, -1)


def _wide(b):
    return np.ascontiguousarray(np.broadcast_to(np.asarray(b, np.float32).reshape(1, -1), (P, np.size(b))))


def _constants():
    f = np.float32
    ident = np.eye(P, dtype=f)
    blocks = np.kron(np.eye(2, dtype=f), np.ones((64, 64), f))
    half = np.zeros((64, 64), f)
    for d in range(32):
        half[d + 32, d] = -1.0
        half[d, d + 32] = 1.0
    rot = np.kron(np.eye(2, dtype=f), half)
    idx = np.arange(0, F_DIM, 2, dtype=f)
    inv_freq = (f(1.0) / np.power(f(10000.0), idx / f(F_DIM))).astype(f)
    t = np.arange(LEN, dtype=f)
    freqs = (t[:, None] * inv_freq[None, :]).astype(f)
    base = ((idx + f(0.4 * F_DIM)) / f(1.4 * F_DIM)).astype(f)
    power = ((t - LEN // 2) / f(32.0)).astype(f)
    sc = np.power(base[None, :], power[:, None]).astype(f)
    cos, sin = np.cos(freqs).astype(f), np.sin(freqs).astype(f)

    def table(a):
        return np.ascontiguousarray(np.tile(np.concatenate([a, a], 1), (1, 2)).T.astype(f))

    qs = f(8.0)
    q = np.arange(P)[:, None]
    k = np.arange(P)[None, :]

    def lay(rule, window=False):
        segs = [(0, 0), (0, 1), (1, 1)] if window else [(0, 0), (1, 0), (1, 1)]
        return np.concatenate([np.where(rule(q + P * a, k + P * b), 0.0, MASKED) for a, b in segs], 1).astype(f)

    def win(i, j):
        first = (i >= 1) & (i <= 32) & (j >= 1) & (j <= 32)
        second = (i >= 129) & (i <= 160) & (j >= 129) & (j <= 160)
        return (i == 0) | first | second | ((i == j) & (i > 0))

    tok = np.arange(LEN)
    seen = ((tok <= 32) | ((tok >= 129) & (tok <= 160))).astype(f).reshape(2, P).T
    in_first = np.arange(P) < 64

    def before(n):
        return np.tile((np.arange(n)[None, :] < np.arange(n)[:, None]).astype(f).reshape(1, -1), (P, 1))

    masks = dict(m_bucket=lay(lambda i, j: (j <= i) & (j // 64 >= i // 64 - 1)),
                 m_local=lay(lambda i, j: (j <= i) & (i <= j + 64)),
                 m_causal=lay(lambda i, j: j <= i), m_window=lay(win, True))
    return masks, dict(
        ident=ident, mean=np.full((P, P), 1.0 / P, f), pairs=blocks, rot=rot,
        qcos=table(cos * sc * qs), qsin=table(sin * sc * qs), kcos=table(cos / sc), ksin=table(sin / sc),
        heads8=(np.arange(P)[:, None] // 8 == np.arange(16)[None, :]).astype(f),
        floor=np.where(in_first, 0.0, 3e38).astype(f)[:, None],
        extra=np.where(in_first, 64.0, 0.0).astype(f)[:, None],
        seen=seen, eps=np.full((P, 1), EPS, f), one=np.ones((P, 1), f), back=np.full((P, 1), 10 * np.log(2.0), f),
        before8=before(8), before16=before(16))


def _layout(v):
    masks, constants = _constants()
    out = {"k": constants, "q": masks}
    a = {n[len("L0_attn_a_"):]: x for n, x in v.items() if n.startswith("L0_attn_a_")}
    out["a"] = dict(g1=_col(a["ln1_g"]), c1=_col(a["ln1_b"]), wqkv=a["w_qkv"], bq=_col(a["b_qkv"][:P]),
                    bk=_col(a["b_qkv"][P:2 * P]), bv=_wide(a["b_qkv"][2 * P:]), wo=a["w_out"], bo=_col(a["b_out"]),
                    g2=_col(a["ln2_g"]), c2=_col(a["ln2_b"]), w1=a["w1"], b1=_col(a["b1"]), w2=_stack(a["w2"]),
                    b2=_col(a["b2"]))
    f = {n[len("L0_ffn_"):]: x for n, x in v.items() if n.startswith("L0_ffn_")}
    out["f"] = {}
    for l in (0, 1):
        twice = lambda g: _col(np.concatenate([g, g]))
        out["f"].update({
            f"wqkv{l}": f["wqkv"][l], f"qs{l}": twice(f["q_scale"][l]), f"ks{l}": twice(f["k_scale"][l]),
            f"wo{l}": _stack(f["wo"][l]), f"g{l}": _col(f["ln_g"][l]), f"c{l}": _col(f["ln_b"][l]),
            f"w1{l}": f["w1"][l], f"ba{l}": _col(f["b1"][l][:HID_F]), f"bg{l}": _col(f["b1"][l][HID_F:]),
            f"w2{l}": _stack(f["w2"][l]), f"b2{l}": _col(f["b2"][l])})
    m = {n[len("L0_attn_b_"):]: x for n, x in v.items() if n.startswith("L0_attn_b_")}
    out["m"] = dict(r1=_col(m["rms1_w"]), r2=_col(m["rms2_w"]), win=m["in_proj_w"],
                    cw=_stack(m["conv_w"].reshape(D_INNER, 4)), cb=_col(m["conv_b"]), wx=_stack(m["x_proj_w"]),
                    wdt=_rows(m["dt_proj_w"]), bdt=_col(m["dt_proj_b"]), alog=_stack(m["A_log"]),
                    dskip=_col(m["D_skip"]), wout=_stack(m["out_proj_w"]), router=m["router_w"])
    out["e"] = dict(wg=m["Wg"].transpose(1, 0, 2).reshape(P, -1), wu=m["Wu"].transpose(1, 0, 2).reshape(P, -1),
                    wd=_stack(m["Wd"].reshape(-1, P)))
    h = {n[len("L1_ffn_"):]: x for n, x in v.items() if n.startswith("L1_ffn_")}
    out["h"] = dict(
        wg=np.concatenate([h["gate_proj"].reshape(-1, P).T, h["shared_gate_w"].T], 1),
        wu=np.concatenate([h["up_proj"].reshape(-1, P).T, h["shared_up_w"].T], 1),
        wd=_stack(np.concatenate([h["down_proj"].transpose(0, 2, 1).reshape(-1, P), h["shared_down_w"].T], 0)),
        expert=_rows((np.arange(ROUTED)[None, :] // I2 == np.arange(E2)[:, None]).astype(np.float32)))
    out["g"] = dict(gate=h["gate_w"].T, bias=_wide(h["gate_bias"]))
    c = {n[len("L1_attn_a_"):]: x for n, x in v.items() if n.startswith("L1_attn_a_")}
    out["c"] = dict(wq=c["Wq"], wk=c["Wk"], wv=c["Wv"], wo=c["Wo"], bq=_col(c["bq"]), bk=_col(c["bk"]),
                    bv=_wide(c["bv"]), bo=_col(c["bo"]))
    d = {n[len("L1_attn_b_"):]: x for n, x in v.items() if n.startswith("L1_attn_b_")}
    flat = lambda w: w.transpose(1, 0, 2).reshape(P, -1)
    out["d"] = dict(wq=flat(d["W_Q"]), wk=flat(d["W_K"]), wv=flat(d["W_V"]),
                    wo=_stack(d["W_O"].reshape(-1, P)), bq=_col(d["b_Q"]), bk=_col(d["b_K"]), bv=_wide(d["b_V"]),
                    bo=_col(d["b_O"]))
    return out


def _arrays(inputs):
    v = {n: np.asarray(x) for n, x in inputs.items()}
    got = _layout(v)
    arrays = {"x_dram": np.ascontiguousarray(v["L0_attn_a_x"].reshape(TOK, P).T)}
    for g, parts in COLS.items():
        arrays[f"w_{g}_dram"] = np.ascontiguousarray(np.concatenate([got[g][n] for n in parts], 1))
        assert arrays[f"w_{g}_dram"].shape == (P, starts(g)[1]), g
    return arrays


STAGES = "AFMFCHDH"


def kernel(**inputs):
    import concourse.bacc as _bacc
    from concourse.bass_utils import run_bass_kernel_spmd as _launch

    arrays = _arrays(inputs)
    nc = _bacc.Bacc("TRN2", target_bir_lowering=False, num_devices=1)
    dram = {n: nc.dram_tensor(n, a.shape, F32, kind="ExternalInput").ap() for n, a in arrays.items()}
    out = nc.dram_tensor("out_dram", (P, TOK), F32, kind="ExternalOutput").ap()
    model(nc, dram["x_dram"], {g: dram[f"w_{g}_dram"] for g in COLS}, out, STAGES)
    r = _launch(nc, [arrays], core_ids=[0])
    return np.ascontiguousarray(r.results[0]["out_dram"].T).reshape(SEQS, LEN, P)
```

```python
from collections import namedtuple
from contextlib import ExitStack

import numpy as np
import concourse.bass as bass
from concourse import mybir

F32 = mybir.dt.float32
BF16 = mybir.dt.bfloat16
F32R = mybir.dt.float32r
ALU = mybir.AluOpType
ACT = mybir.ActivationFunctionType
AX = mybir.AxisListType.X

P = 128
SEQS, LEN = 8, 256
TOK = SEQS * LEN
GROUP = 512
TILES = TOK // P
EPS = 1e-5
MASKED = -1e30

A_HEADS, A_DIM = 16, 8
SEEN = [(0, 33), (129, 161)]
F_HEADS, F_DIM = 8, 64
D_HEADS, D_DIM = 16, 64
HID_F = 341
LOTS_F = -(-HID_F // P)
N_EXP, FFN = 8, 512
E2, I2, SHARED = 16, 176, 352
ROUTED = E2 * I2
LOTS2 = -(-(ROUTED + SHARED) // P)
D_INNER, STATE, DT_RANK = 256, 16, 64

COLS = {
    "k": dict(ident=P, mean=P, pairs=P, rot=P, qcos=LEN, kcos=LEN, qsin=LEN, ksin=LEN,
              heads8=16,
              floor=1, extra=1, eps=1, one=1, back=1, before16=256),
    "q": dict(m_bucket=320, m_local=320, m_causal=384, m_window=256),
    "a": dict(g1=1, c1=1, wqkv=384, bq=1, bk=1, bv=P, wo=P, bo=1, g2=1, c2=1, w=1024, b1=4, b2=1),
    "f": dict(wqkv0=1536, qs0=1, ks0=1, wo0=512, g0=1, c0=1, w0=3 * P * LOTS_F, ba0=3, bg0=3, b20=1,
              wqkv1=1536, qs1=1, ks1=1, wo1=512, g1=1, c1=1, w1=3 * P * LOTS_F, ba1=3, bg1=3, b21=1),
    "m": dict(r1=1, r2=1, win=512, cw=8, cb=2, wx=192, wdt=256, bdt=2, alog=32, dskip=2, wout=256, router=8),
    "e": dict(w=N_EXP * FFN * 3),
    "h": dict(w=LOTS2 * P * 3, expert=ROUTED),
    "g": dict(gate=E2, bias=E2),
    "c": dict(wq=P, wk=P, wv=P, wo=P, bq=1, bk=1, bv=P, bo=1),
    "d": dict(wq=1024, wk=1024, wv=1024, wo=1024, bq=8, bk=8, bv=1024, bo=1),
}


def starts(group):
    at, out = 0, {}
    for name, width in COLS[group].items():
        out[name] = at
        at += width
    return out, at


def span(signals):
    return range(signals[0].num, signals[-1].num + 1)


class Order:

    def __init__(self, eng, sem):
        self.eng, self.sem, self.n = eng, sem, 0

    def step(self, ins):
        self.n += 1
        ins.then_inc(self.sem, 1)
        self.eng.wait_ge(self.sem, self.n)


class Net:

    def __init__(self, nc, ctx):
        self.nc, self.ctx, self.sets, self.tensors = nc, ctx, {}, 0

    def sbuf(self, name, shape, dt=F32, ctx=None):
        self.tensors += 1
        return (ctx or self.ctx).enter_context(self.nc.sbuf_tensor(f"{name}_{self.tensors}", shape, dt))

    def psum(self, name, shape, ctx):
        self.tensors += 1
        return ctx.enter_context(self.nc.psum_tensor(f"{name}_{self.tensors}", shape, F32))

    def signals(self, kind, names):
        if kind not in self.sets:
            got = [self.ctx.enter_context(self.nc.semaphore(f"{kind}_{n}")) for n in names]
            nums = [s.num for s in got]
            assert nums == list(range(nums[0], nums[0] + len(nums))), nums
            self.sets[kind] = namedtuple(f"Signals_{kind}", names)(*got)
        return self.sets[kind]

    def w(self, group, name, a=0, b=None, rows=P):
        at, _ = starts(group)
        lo = at[name]
        hi = lo + (COLS[group][name] if b is None else b)
        return self.weights[group][0:rows, lo + a:hi]


def norm(net, tag, src, dst, root_mean_square=False, gain=None, bias=None, shift=False):
    nc = net.nc
    chunks = TOK // GROUP
    s = net.signals("norm", ["cleared", "kept", "shifted", "mean_ready", "centred", "squared", "var_ready", "std_ready",
                             "steps", "act_steps"])
    with ExitStack() as ctx:
        moved = net.sbuf("n_moved", [P, TOK], ctx=ctx) if shift else src
        centred = net.sbuf("n_centred", [P, TOK], ctx=ctx) if not root_mean_square else src
        squared = net.sbuf("n_squared", [P, TOK], ctx=ctx)
        std = net.sbuf("n_std", [P, TOK], ctx=ctx)
        mean_ps = net.psum("n_mean", [P, chunks, GROUP], ctx)
        var_ps = net.psum("n_var", [P, chunks, GROUP], ctx)
        ones = net.w("k", "mean")

        def cut(t, c):
            return t[:, c * GROUP:(c + 1) * GROUP]

        def by_seq(t, a, b):
            return t[P // 2:P, a:b].rearrange("p (s t) -> p s t", t=LEN)

        with nc.Block(no_gpsimd_drain=True) as block:
            @block.gpsimd
            def _(pool):
                if shift:
                    pool.memset(by_seq(moved, 0, TOK)[:, :, 0:1], 0.0).then_inc(s.cleared, 1)

            @block.tensor
            def _(pe):
                if shift:
                    pe.wait_ge(s.cleared, 1)
                if not root_mean_square:
                    for c in range(chunks):
                        if shift:
                            pe.wait_ge(s.shifted, c + 1)
                            pe.wait_ge(s.kept, c + 1)
                        pe.matmul(mean_ps[:, c, :], ones, cut(moved, c), start=True, stop=True)\
                          .then_inc(s.mean_ready, 1)
                for c in range(chunks):
                    pe.wait_ge(s.squared, c + 1)
                    pe.matmul(var_ps[:, c, :], ones, cut(squared, c), start=True, stop=True)\
                      .then_inc(s.var_ready, 1)

            @block.scalar
            def _(act):
                order = Order(act, s.act_steps)
                nc.scalar.preload_act_table_set("natural_log_exp_and_others")
                for c in range(chunks if shift else 0):
                    act.activation(by_seq(moved, c * GROUP, (c + 1) * GROUP)[:, :, 1:LEN],
                                   by_seq(src, c * GROUP, (c + 1) * GROUP)[:, :, 0:LEN - 1], ACT.Copy)\
                       .then_inc(s.shifted, 1)
                for c in range(chunks):
                    if not root_mean_square:
                        act.wait_ge(s.centred, c + 1)
                    act.activation(cut(squared, c), cut(centred, c), ACT.Square).then_inc(s.squared, 1)
                for c in range(chunks):
                    act.wait_ge(s.var_ready, c + 1)
                    order.step(act.activation(cut(std, c), var_ps[:, c, :], ACT.Ln, bias=net.w("k", "eps")))
                    act.activation(cut(std, c), cut(std, c), ACT.Exp, scale=-0.5).then_inc(s.std_ready, 1)

            @block.vector
            def _(dve):
                for c in range(chunks if shift else 0):
                    dve.tensor_copy(cut(moved, c)[0:P // 2, :], cut(src, c)[0:P // 2, :]).then_inc(s.kept, 1)
                if not root_mean_square:
                    for c in range(chunks):
                        dve.wait_ge(s.mean_ready, c + 1)
                        dve.tensor_tensor(cut(centred, c), cut(moved, c), mean_ps[:, c, :], ALU.subtract)\
                           .then_inc(s.centred, 1)
                    dve.wait_ge(s.centred, chunks)
                order = Order(dve, s.steps)
                for c in range(chunks):
                    dve.wait_ge(s.std_ready, c + 1)
                    done = dve.tensor_tensor(cut(dst, c), cut(centred, c), cut(std, c), ALU.mult)
                    if gain is not None:
                        order.step(done)
                        if bias is None:
                            dve.tensor_scalar(cut(dst, c), cut(dst, c), gain, None, ALU.mult)
                        else:
                            dve.tensor_scalar(cut(dst, c), cut(dst, c), gain, bias, ALU.mult, ALU.add)
        nc.all_engine_barrier(sems_to_clear=span(s))


def mixture(net, src, dst, weights, phases, share_high=None, share_rest=None, also=None, func=ACT.Silu,
            gated=True, gate_bias=None, up_bias=None, out_bias=None):
    nc = net.nc
    s = net.signals("exp", [
        "zeroed", "closed", "high_done", "rest_done", "w_high", "w_rest", "gate_ready", "up_ready", "share_ready",
        "acted",
        "weighted", "hidden", "hidden_high", "hidden_rest", "down_done", "added"])
    groups = TOK // GROUP
    W = (3 if gated else 2) * P
    n_exp = share_high.shape[0] if share_high is not None else 0
    most = max(lots for _, _, lots, _ in phases)
    with ExitStack() as ctx:
        x_high = net.sbuf("e_xh", [P, TOK], F32R, ctx=ctx)
        x_rest = net.sbuf("e_xr", [P, TOK], F32R, ctx=ctx)
        w_high = net.sbuf("e_wh", [P, 2, most, W], F32R, ctx=ctx)
        w_rest = net.sbuf("e_wr", [P, 2, most, W], F32R, ctx=ctx)
        spread = net.sbuf("e_spread", [n_exp, 2, P], F32R, ctx=ctx) if n_exp else None
        acted = net.sbuf("e_acted", [P, 2, GROUP], ctx=ctx)
        hidden = net.sbuf("e_hidden", [P, 2, GROUP], ctx=ctx)
        hid_high = net.sbuf("e_hh", [P, 3, GROUP], F32R, ctx=ctx)
        hid_rest = net.sbuf("e_hr", [P, 3, GROUP], F32R, ctx=ctx)
        zeros = net.sbuf("e_zeros", [P, P], F32R, ctx=ctx)
        gate_ps = net.psum("e_gate", [P, 2, GROUP], ctx)
        up_ps = net.psum("e_up", [P, GROUP], ctx)
        share_ps = net.psum("e_share", [P, GROUP], ctx)
        out_ps = net.psum("e_out", [P, groups, GROUP], ctx)

        def cut(t, g):
            return t[:, g * GROUP:(g + 1) * GROUP]

        def zero_sum(pe, start):
            for g in range(groups):
                if start:
                    pe.wait_ge(s.high_done, g + 1)
                last = pe.matmul(out_ps[:, g, :], zeros[:, :], cut(x_high, g), start=start, stop=not start)
            return last

        def three(pe, out, w, wr, x, xr, start, stop):
            pe.matmul(out, w, x, start=start, stop=False)
            pe.matmul(out, w, xr, start=False, stop=False)
            return pe.matmul(out, wr, x, start=False, stop=stop)

        def open_sums(pe):
            pe.wait_ge(s.zeroed, 1)
            zero_sum(pe, True)

        def split_high(act):
            for g in range(groups):
                act.activation(cut(x_high, g), cut(src, g), ACT.Copy).then_inc(s.high_done, 1)

        def split_rest(dve):
            dve.tensor_scalar(zeros[:, :], net.w("k", "ident"), 0.0, None, ALU.mult).then_inc(s.zeroed, 1)
            for g in range(groups):
                dve.wait_ge(s.high_done, g + 1)
                dve.tensor_tensor(cut(x_rest, g), cut(src, g), cut(x_high, g).bitcast(F32), ALU.subtract)\
                   .then_inc(s.rest_done, 1)

        def add_sums(dve):
            if also is not None:
                for g in range(groups):
                    dve.tensor_tensor(cut(dst, g), cut(dst, g), cut(also, g), ALU.add).then_inc(s.added, 1)
            dve.wait_ge(s.closed, 1)
            for g in range(groups):
                if also is not None:
                    dve.wait_ge(s.added, g + 1)
                if out_bias is None:
                    dve.tensor_tensor(cut(dst, g), cut(dst, g), out_ps[:, g, :], ALU.add)
                else:
                    dve.scalar_tensor_tensor(out=cut(dst, g), in0=out_ps[:, g, :], scalar=out_bias,
                                             in1=cut(dst, g), op0=ALU.add, op1=ALU.add)

        opened_within = phases[0][0] == 1
        closed_within = phases[-1][0] == 1
        if not opened_within:
            with nc.Block(no_gpsimd_drain=True) as block:
                @block.tensor
                def _(pe):
                    open_sums(pe)

                @block.scalar
                def _(act):
                    split_high(act)

                @block.vector
                def _(dve):
                    split_rest(dve)
            nc.all_engine_barrier(sems_to_clear=span(s))

        first_lot = 0
        for number, (turns, sets, lots, share_of) in enumerate(phases):
            opens = opened_within and number == 0
            closes = closed_within and number == len(phases) - 1
            units = [(e, g, k) for e in range(sets) for g in range(groups) for k in range(lots)]
            N = len(units)
            per_set = groups * lots

            def weights_of(i, e, first_lot=first_lot, turns=turns, sets=sets, lots=lots):
                w = weights[:, (first_lot + e * lots) * W:]
                if turns == 1:
                    return w[:, 0:lots * W]
                return w[:, bass.ds(i * (sets * lots * W), lots * W)]

            def turn(i):
                with nc.Block(no_gpsimd_drain=True) as block:
                    @block.tensor
                    def _(pe):
                        def down(n):
                            e, g, k = units[n]
                            pe.wait_ge(s.hidden_rest, n + 1)
                            b, h = e % 2, n % 3
                            three(pe, out_ps[:, g, :], w_high[:, b, k, W - P:], w_rest[:, b, k, W - P:],
                                  hid_high[:, h, :], hid_rest[:, h, :], False, False).then_inc(s.down_done, 1)

                        if opens:
                            open_sums(pe)
                        for n, (e, g, k) in enumerate(units):
                            b = e % 2
                            if n % per_set == 0:
                                pe.wait_ge(s.w_high, e + 1)
                                pe.wait_ge(s.w_rest, e + 1)
                            if opens and e == 0 and k == 0:
                                pe.wait_ge(s.rest_done, g + 1)
                            if n >= 2:
                                pe.wait_ge(s.acted if gated else s.hidden, n - 1)
                            three(pe, gate_ps[:, n % 2, :], w_high[:, b, k, 0:P], w_rest[:, b, k, 0:P],
                                  cut(x_high, g), cut(x_rest, g), True, True).then_inc(s.gate_ready, 1)
                            if n >= 3:
                                down(n - 3)
                            if share_of is not None and k == 0:
                                if n >= 1:
                                    pe.wait_ge(s.weighted, n)
                                pe.matmul(share_ps[:, :], spread[:, b, :], cut(share_high, g),
                                          start=True, stop=False)
                                pe.matmul(share_ps[:, :], spread[:, b, :], cut(share_rest, g),
                                          start=False, stop=True).then_inc(s.share_ready, 1)
                            if not gated:
                                continue
                            if n >= 1:
                                pe.wait_ge(s.hidden, n)
                            three(pe, up_ps[:, :], w_high[:, b, k, P:2 * P], w_rest[:, b, k, P:2 * P],
                                  cut(x_high, g), cut(x_rest, g), True, True).then_inc(s.up_ready, 1)
                        for n in range(max(0, N - 3), N):
                            down(n)
                        if closes:
                            zero_sum(pe, False).then_inc(s.closed, 1)

                    @block.scalar
                    def _(act):
                        def take_weights(e):
                            if e >= 2:
                                act.wait_ge(s.down_done, (e - 1) * per_set)
                            if share_of is not None:
                                act.activation(spread[:, e % 2, :], share_of(i, e), ACT.Copy)
                            act.activation(w_high[:, e % 2, 0:lots, :].rearrange("p k w -> p (k w)"),
                                           weights_of(i, e), ACT.Copy).then_inc(s.w_high, 1)

                        def high(n):
                            act.wait_ge(s.hidden, n + 1)
                            if n >= 3:
                                act.wait_ge(s.down_done, n - 2)
                            act.activation(hid_high[:, n % 3, :], hidden[:, n % 2, :], ACT.Copy)\
                               .then_inc(s.hidden_high, 1)

                        take_weights(0)
                        if opens:
                            split_high(act)
                        for n, (e, g, k) in enumerate(units):
                            act.wait_ge(s.gate_ready, n + 1)
                            if n >= 2:
                                act.wait_ge(s.hidden if gated else s.hidden_rest, n - 1)
                            out, done = (acted, s.acted) if gated else (hidden, s.hidden)
                            lot = e * lots + k
                            bias = {} if gate_bias is None else {"bias": gate_bias[:, lot:lot + 1]}
                            act.activation(out[:, n % 2, :], gate_ps[:, n % 2, :], func, **bias).then_inc(done, 1)
                            if not gated:
                                high(n)
                            elif n >= 1:
                                high(n - 1)
                            if n % per_set == 2 and e + 1 < sets:
                                take_weights(e + 1)
                        if gated:
                            high(N - 1)

                    @block.gpsimd
                    def _(pool):
                        def rest_weights(e):
                            pool.wait_ge(s.w_high, e + 1)
                            pool.tensor_tensor(w_rest[:, e % 2, 0:lots, :].rearrange("p k w -> p (k w)"),
                                               weights_of(i, e),
                                               w_high[:, e % 2, 0:lots, :].rearrange("p k w -> p (k w)").bitcast(F32),
                                               ALU.subtract).then_inc(s.w_rest, 1)

                        rest_weights(0)
                        for n, (e, g, k) in enumerate(units):
                            pool.wait_ge(s.hidden_high, n + 1)
                            pool.tensor_tensor(hid_rest[:, n % 3, :], hidden[:, n % 2, :],
                                               hid_high[:, n % 3, :].bitcast(F32), ALU.subtract)\
                                .then_inc(s.hidden_rest, 1)
                            if n % per_set == 1 and e + 1 < sets:
                                rest_weights(e + 1)

                    @block.vector
                    def _(dve):
                        if opens:
                            split_rest(dve)
                        for n, (e, g, k) in enumerate(units if gated else []):
                            dve.wait_ge(s.acted, n + 1)
                            if share_of is not None:
                                dve.wait_ge(s.share_ready, n // lots + 1)
                                dve.tensor_tensor(acted[:, n % 2, :], acted[:, n % 2, :], share_ps[:, :], ALU.mult)\
                                   .then_inc(s.weighted, 1)
                                dve.wait_ge(s.weighted, n + 1)
                            dve.wait_ge(s.up_ready, n + 1)
                            if n >= 2:
                                dve.wait_ge(s.hidden_rest, n - 1)
                            out, lot = hidden[:, n % 2, :], e * lots + k
                            if up_bias is None:
                                last = dve.tensor_tensor(out, acted[:, n % 2, :], up_ps[:, :], ALU.mult)
                            else:
                                last = dve.scalar_tensor_tensor(
                                    out=out, in0=up_ps[:, :], scalar=up_bias[:, lot:lot + 1],
                                    in1=acted[:, n % 2, :], op0=ALU.add, op1=ALU.mult)
                            last.then_inc(s.hidden, 1)
                        if closes:
                            add_sums(dve)
                nc.all_engine_barrier(sems_to_clear=span(s))

            if turns > 1:
                with nc.Fori(0, turns) as i:
                    turn(i)
            else:
                turn(0)
            first_lot += turns * sets * lots

        if not closed_within:
            with nc.Block(no_gpsimd_drain=True) as block:
                @block.tensor
                def _(pe):
                    zero_sum(pe, False).then_inc(s.closed, 1)

                @block.vector
                def _(dve):
                    add_sums(dve)
            nc.all_engine_barrier(sems_to_clear=span(s))


def gate(net, src, high, rest, experts):
    nc = net.nc
    E, T = experts, TILES
    s = net.signals("gate", ["logits_ready", "scored", "steps", "chosen", "turned", "copied"])
    weights = net.w("m", "router") if E == N_EXP else net.w("g", "gate")
    with ExitStack() as ctx:
        x = net.sbuf("g_x", [P, T, E], ctx=ctx)
        y = net.sbuf("g_y", [P, T, E], ctx=ctx)
        rank = net.sbuf("g_rank", [P, T, E], ctx=ctx)
        more = net.sbuf("g_more", [P, T, E, E], BF16, ctx=ctx)
        same = net.sbuf("g_same", [P, T, E, E], BF16, ctx=ctx)
        before = net.sbuf("g_before", [P, E, E], BF16, ctx=ctx)
        row = net.sbuf("g_row", [P, T], ctx=ctx)
        z = net.sbuf("g_z", [P, T, E], ctx=ctx)
        pairs = net.sbuf("g_pairs", [P, T * 4, 6], ctx=ctx)
        groups = net.sbuf("g_groups", [P, T, 4], ctx=ctx)
        group_rank = net.sbuf("g_grank", [P, T, 4], ctx=ctx)
        logits = net.psum("g_logits", [P, T, E], ctx)
        turned = net.psum("g_turned", [E, TOK], ctx)

        def ranks(order, dve, v, out, n):
            big = more[:, :, :, :].rearrange("p t a b -> p t (a b)")[:, :, 0:n * n]\
                .rearrange("p t (a b) -> p t a b", a=n)
            eq = same[:, :, :, :].rearrange("p t a b -> p t (a b)")[:, :, 0:n * n]\
                .rearrange("p t (a b) -> p t a b", a=n)
            shape = [P, T, n, n]
            other = v.unsqueeze(2).to_broadcast(shape)
            own = v.unsqueeze(3).to_broadcast(shape)
            order.step(dve.tensor_tensor(big, other, own, ALU.is_gt))
            order.step(dve.tensor_tensor(eq, other, own, ALU.is_equal))
            order.step(dve.tensor_tensor(eq, eq, before[:, 0:n, 0:n].unsqueeze(1).to_broadcast(shape), ALU.mult))
            order.step(dve.tensor_tensor(big, big, eq, ALU.add))
            order.step(dve.tensor_reduce(out, big, AX, ALU.add))

        with nc.Block(no_gpsimd_drain=True) as block:
            @block.tensor
            def _(pe):
                for t in range(T):
                    last = pe.matmul(logits[:, t, :], src[:, t * P:(t + 1) * P], weights, start=True, stop=True)
                last.then_inc(s.logits_ready, 1)
                pe.wait_ge(s.chosen, 1)
                for t in range(T):
                    last = pe.transpose(turned[:, t * P:(t + 1) * P], x[:, t, :], net.w("k", "ident"))
                last.then_inc(s.turned, 1)

            @block.scalar
            def _(act):
                if E == N_EXP:
                    act.wait_ge(s.steps, 3)
                    act.activation(y[:, :, :], x[:, :, :], ACT.Exp).then_inc(s.scored, 1)
                else:
                    act.wait_ge(s.logits_ready, 1)
                    act.activation(y[:, :, :], logits[:, :, :], ACT.Sigmoid).then_inc(s.scored, 1)
                act.wait_ge(s.turned, 1)
                act.activation(high[:, :], turned[:, :], ACT.Copy).then_inc(s.copied, 1)

            @block.vector
            def _(dve):
                order = Order(dve, s.steps)
                shape = [P, T, E]

                def over(v):
                    return v.unsqueeze(2).to_broadcast(shape)

                order.step(dve.tensor_copy(before[:, :, :], net.w("k", "before16").rearrange(
                    "p (a b) -> p a b", a=16)[:, 0:E, 0:E]))
                dve.wait_ge(s.logits_ready, 1)
                if E == N_EXP:
                    order.step(dve.tensor_reduce(row[:, :], logits[:, :, :], AX, ALU.max))
                    order.step(dve.tensor_tensor(x[:, :, :], logits[:, :, :], over(row[:, :]), ALU.subtract))
                    dve.wait_ge(s.scored, 1)
                    order.step(dve.tensor_reduce(row[:, :], y[:, :, :], AX, ALU.add))
                    order.step(dve.reciprocal(row[:, :], row[:, :]))
                    order.step(dve.tensor_tensor(y[:, :, :], y[:, :, :], over(row[:, :]), ALU.mult))
                    ranks(order, dve, y[:, :, :], rank[:, :, :], E)
                    order.step(dve.tensor_scalar(rank[:, :, :], rank[:, :, :], 2.0, None, ALU.is_lt))
                    dve.tensor_tensor(x[:, :, :], y[:, :, :], rank[:, :, :], ALU.mult).then_inc(s.chosen, 1)
                else:
                    dve.wait_ge(s.scored, 1)
                    order.step(dve.tensor_tensor(z[:, :, :], y[:, :, :],
                                                 net.w("g", "bias").unsqueeze(1).to_broadcast(shape), ALU.add))
                    four = z[:, :, :].rearrange("p t (g e) -> p (t g) e", g=4)
                    order.step(dve.tensor_tensor(pairs[:, :, 0:3], four[:, :, 0:3], four[:, :, 1:4], ALU.add))
                    order.step(dve.tensor_tensor(pairs[:, :, 3:5], four[:, :, 0:2], four[:, :, 2:4], ALU.add))
                    order.step(dve.tensor_tensor(pairs[:, :, 5:6], four[:, :, 0:1], four[:, :, 3:4], ALU.add))
                    order.step(dve.tensor_reduce(groups[:, :, :].rearrange("p t g -> p (t g)"),
                                                 pairs[:, :, :], AX, ALU.max))
                    ranks(order, dve, groups[:, :, :], group_rank[:, :, :], 4)
                    order.step(dve.tensor_scalar(group_rank[:, :, :], group_rank[:, :, :], 2.0, None, ALU.is_lt))
                    spread = group_rank[:, :, :].rearrange("p t g -> p (t g)").unsqueeze(2)\
                        .to_broadcast([P, T * 4, 4])
                    order.step(dve.tensor_tensor(four, four, spread, ALU.mult))
                    ranks(order, dve, z[:, :, :], rank[:, :, :], E)
                    order.step(dve.tensor_scalar(rank[:, :, :], rank[:, :, :], 4.0, None, ALU.is_lt))
                    order.step(dve.tensor_tensor(y[:, :, :], y[:, :, :], rank[:, :, :], ALU.mult))
                    order.step(dve.tensor_reduce(row[:, :], y[:, :, :], AX, ALU.add))
                    order.step(dve.tensor_scalar(row[:, :], row[:, :], 1e-20, None, ALU.add))
                    order.step(dve.reciprocal(row[:, :], row[:, :]))
                    dve.tensor_tensor(x[:, :, :], y[:, :, :], over(row[:, :]), ALU.mult).then_inc(s.chosen, 1)
                dve.wait_ge(s.copied, 1)
                dve.tensor_tensor(rest[:, :], turned[:, :], high[:, :].bitcast(F32), ALU.subtract)
        nc.all_engine_barrier(sems_to_clear=span(s))


def attention(net, kind, src, dst, mask, scale, wq, wk, wv, wo, bq=None, bk=None, bv=None, bo=None,
              q_gain=None, k_gain=None):
    nc = net.nc
    small = kind in ("bucket", "window")
    rotary = kind == "local"
    heads = {"bucket": A_HEADS, "window": A_HEADS, "local": F_HEADS, "causal": D_HEADS}[kind]
    dim = A_DIM if small else D_DIM
    width = heads * dim
    parts = width // P
    seqs = 4
    pairs = heads // 2
    units = seqs * pairs
    all_heads = 2 * units
    lag = 2 if rotary else 1
    lot = P // dim
    lots = all_heads // lot
    last_step = all_heads + 4
    v_w = min(width, GROUP)
    n_v = 2 * (width // v_w)
    near = P // 2 if kind in ("bucket", "local") else 0
    if kind == "window":
        segs = [(0, 0, LEN, 0)]
    else:
        segs = [(0, 0, P, 0), (1, near, LEN, P)]
    columns = sum(b - a for _, a, b, _ in segs)
    pieces = SEEN if kind == "window" else [(0, LEN)]
    rows = sum(b - a for a, b in pieces) if kind == "window" else P
    tiles = len(segs)
    blocks = sorted([(q, k, max(a - k * P, 0), at + max(k * P - a, 0))
                     for q, a, b, at in segs for k in range(a // P, b // P)], key=lambda block: block[2])
    whole = sum(block[2] == 0 for block in blocks)
    s = net.signals("attn", [
        "x_ready", "proj_ready", "proj_read", "side_ready", "side_read", "k_spread", "qk_done", "scores_ready",
        "max_ready", "probs_ready", "turned", "turned_read", "mixed", "out_scaled", "out_turned", "out_copied",
        "extra_ready", "raw_ready", "sq_ready", "raw_split", "sq_split", "cos_ready", "sum_ready",
        "norm_ready", "vec_steps", "act_steps"])

    def projects(u):
        return not small or u % pairs == 0

    def projected(u):
        return u // pairs + 1 if small else u + 1

    def v_piece(u):
        return u % pairs if u % pairs < n_v else None

    def lot_at(h, after):
        g = (h - after - 3 + 1) // lot - 1
        return g if 0 <= g < lots and lot * (g + 1) - 1 + 3 + after == h else None

    def closes(g):
        return g // (lots // seqs) if g is not None and (g + 1) % (lots // seqs) == 0 else None

    def step_heads(t):
        return [h for h in (2 * (t - lag), 2 * (t - lag) + 1) if 0 <= h <= last_step]

    turns = lag + (last_step + 2) // 2
    uses = {}
    for t in range(turns):
        if rotary and 1 <= t <= units:
            uses["rot", t - 1] = len(uses) + 1
        for j, h in enumerate((2 * (t - lag), 2 * (t - lag) + 1)):
            if 0 <= h <= last_step and closes(lot_at(h, 2)) is not None:
                uses["out", closes(lot_at(h, 2))] = len(uses) + 1
            if j == 0 and rotary and 1 <= t <= units:
                uses["squares", t - 1] = len(uses) + 1
        if t < units and v_piece(t) is not None:
            uses["v", t] = len(uses) + 1

    with ExitStack() as ctx:
        xs = net.sbuf("t_x", [P, seqs, LEN], ctx=ctx)
        qk = net.sbuf("t_qk", [P, 3, 2, LEN], ctx=ctx)
        v_sb = net.sbuf("t_v", [P, 2, 2, width], ctx=ctx)
        v_half = net.sbuf("t_vhalf", [near, 2, width], ctx=ctx) if near else None
        k_one = net.sbuf("t_kone", [P, 3, 2, LEN], ctx=ctx) if small else None
        probs = net.sbuf("t_probs", [P, 3, columns], ctx=ctx)
        turned = net.sbuf("t_turned", [P, 3, 384], ctx=ctx)
        neg_max = net.sbuf("t_negmax", [P, all_heads, 2], ctx=ctx)
        sums = net.sbuf("t_sums", [P, all_heads, 2], ctx=ctx)
        zero_key = net.sbuf("t_zero", [P, all_heads], ctx=ctx)
        o_sb = net.sbuf("t_o", [P, 2, 2, P], ctx=ctx)
        o_t = net.sbuf("t_ot", [P, 2, parts, LEN], ctx=ctx)
        if rotary:
            raw = net.sbuf("t_raw", [P, 2, 2 * LEN], ctx=ctx)
            raw_high = net.sbuf("t_raw_high", [P, 2, 2 * LEN], F32R, ctx=ctx)
            raw_rest = net.sbuf("t_raw_rest", [P, 2 * LEN], F32R, ctx=ctx)
            sq = net.sbuf("t_sq", [P, 2, 2 * LEN], ctx=ctx)
            sq_rest = net.sbuf("t_sq_rest", [P, 2 * LEN], F32R, ctx=ctx)
            sq_high = net.sbuf("t_sq_high", [P, 2, 2 * LEN], F32R, ctx=ctx)
            rot_and_pairs = net.sbuf("t_rot", [P, 2 * P], F32R, ctx=ctx)
            sind = net.sbuf("t_sin", [P, 2, 2 * LEN], ctx=ctx)
            cosd = raw
            size = sq
        proj_ps = net.psum("t_pp", [P, 2, LEN], ctx)
        side_ps = net.psum("t_side", [P, 512], ctx)
        sc = net.psum("t_sc", [P, 2, 512], ctx)
        tp = net.psum("t_tp", [P, 2, 512], ctx)
        op = net.psum("t_op", [P, 2, 512], ctx)
        ident = net.w("k", "ident")

        def head_q(h, tile):
            u, j = h // 2, h % 2
            cut = slice(tile * P, tile * P + rows)
            if small:
                return qk[:, u // pairs % 3, 0, cut]
            return qk[64 * j:64 * j + 64, u % 3, 0, cut]

        def head_k(h, cut):
            u, j = h // 2, h % 2
            if small:
                return k_one[:, u % 3, j, cut]
            return qk[64 * j:64 * j + 64, u % 3, 1, cut]

        with nc.Fori(0, SEQS // seqs) as i:
            with nc.Block(no_gpsimd_drain=True) as block:
                @block.tensor
                def _(pe):
                    def side(key):
                        if uses[key] > 1:
                            pe.wait_ge(s.side_read, uses[key] - 1)

                    def two(matrix, high, rest):
                        pe.matmul(side_ps[:, :], matrix, high, start=True, stop=False)
                        pe.matmul(side_ps[:, :], matrix, rest, start=False, stop=True).then_inc(s.side_ready, 1)

                    def project(u):
                        r, c = u // pairs, 0 if small else u % pairs
                        if projected(u) > 1:
                            pe.wait_ge(s.sq_ready if rotary else s.proj_read if small else s.qk_done,
                                       projected(u) - 1)
                        for n, wt in enumerate((wq, wk)):
                            last = pe.matmul(proj_ps[:, n, :], wt[:, c * P:(c + 1) * P], xs[:, r, :],
                                             start=True, stop=True)
                        last.then_inc(s.proj_ready, 1)

                    def project_v(u):
                        r, n = u // pairs, v_piece(u)
                        side(("v", u))
                        pe.matmul(side_ps[:, 0:v_w], xs[:, r, (n % 2) * P:(n % 2 + 1) * P],
                                  wv[:, (n // 2) * v_w:(n // 2 + 1) * v_w], start=True, stop=True)\
                          .then_inc(s.side_ready, 1)

                    def scores(h):
                        if small:
                            pe.wait_ge(s.k_spread, h // 2 + 1)
                        else:
                            pe.wait_ge(s.qk_done, h // 2 + 1)
                        if h >= 2:
                            pe.wait_ge(s.probs_ready, h - 1)
                        pe.matmul(sc[0:rows, h % 2, 0:columns], net.ident16[:, 0:rows], mask[:, 0:columns],
                                  start=True, stop=False)
                        for q, a, b, at in segs:
                            last = pe.matmul(sc[0:rows, h % 2, at:at + b - a], head_q(h, q), head_k(h, slice(a, b)),
                                             start=False, stop=(q == tiles - 1))
                        last.then_inc(s.scores_ready, 1)

                    def turn(h):
                        pe.wait_ge(s.probs_ready, h + 1)
                        if h >= 2:
                            pe.wait_ge(s.turned_read, h - 1)
                        for n, (q, k, first, at) in enumerate(blocks):
                            last = pe.transpose(tp[0:P - first, h % 2, n * rows:(n + 1) * rows],
                                                probs[0:rows, h % 3, at:at + P - first], ident[0:rows, 0:rows])
                        last.then_inc(s.turned, 1)

                    def mix(h):
                        r, hr, g, j = h // heads, h % heads, h // lot, h % lot
                        pe.wait_ge(s.turned_read, h + 1)
                        piece = 2 * (hr * dim // v_w) + 1
                        pe.wait_ge(s.side_read, uses["v", r * pairs + piece])
                        if j == 0 and g >= 2:
                            pe.wait_ge(s.out_copied, g - 1)
                        for q in range(tiles):
                            mine = [(n, k, first) for n, (of, k, first, _) in enumerate(blocks) if of == q]
                            for n, k, first in mine:
                                values = v_half[:, r % 2, :] if first else v_sb[:, r % 2, k, :]
                                last = pe.matmul(op[0:rows, g % 2, q * P + j * dim:q * P + (j + 1) * dim],
                                                 turned[0:P - first, h % 3, n * rows:(n + 1) * rows],
                                                 values[:, hr * dim:(hr + 1) * dim],
                                                 start=(n == mine[0][0]), stop=(n == mine[-1][0]))
                        last.then_inc(s.mixed, 1)

                    def turn_out(g):
                        pe.wait_ge(s.out_scaled, g + 1)
                        for q in range(tiles):
                            at = 2 * P + q * rows
                            last = pe.transpose(op[:, g % 2, at:at + rows], o_sb[0:rows, g % 2, q, :],
                                                ident[0:rows, 0:rows])
                        last.then_inc(s.out_turned, 1)

                    def project_out(r):
                        pe.wait_ge(s.out_copied, (r + 1) * lots // seqs)
                        side(("out", r))
                        for c in range(parts):
                            last = pe.matmul(side_ps[:, 0:tiles * rows], wo[:, c * P:(c + 1) * P],
                                             o_t[:, r % 2, c, 0:tiles * rows],
                                             start=(c == 0), stop=(c == parts - 1))
                        last.then_inc(s.side_ready, 1)

                    pe.wait_ge(s.x_ready, 1)
                    for t in range(turns):
                        if t < units:
                            if projects(t):
                                project(t)
                        if rotary and 1 <= t <= units:
                            u = t - 1
                            pe.wait_ge(s.raw_split, u + 1)
                            side(("rot", u))
                            two(rot_and_pairs[:, 0:P], raw_high[:, u % 2, :], raw_rest[:, :])
                        for j, h in enumerate((2 * (t - lag), 2 * (t - lag) + 1)):
                            if 0 <= h <= last_step:
                                if h < all_heads:
                                    scores(h)
                                if 0 <= h - 2 < all_heads:
                                    turn(h - 2)
                                if 0 <= h - 3 < all_heads:
                                    mix(h - 3)
                                if lot_at(h, 1) is not None:
                                    turn_out(lot_at(h, 1))
                                if closes(lot_at(h, 2)) is not None:
                                    project_out(closes(lot_at(h, 2)))
                            if j == 0 and rotary and 1 <= t <= units:
                                pe.wait_ge(s.sq_split, u + 1)
                                side(("squares", u))
                                two(rot_and_pairs[:, P:], sq_high[:, u % 2, :], sq_rest[:, :])
                        if t < units and v_piece(t) is not None:
                            project_v(t)

                @block.scalar
                def _(act):
                    order = Order(act, s.act_steps)
                    nc.scalar.preload_act_table_set("natural_log_exp_and_others")
                    for t in range(turns):
                        if rotary and t < units:
                            u = t
                            act.wait_ge(s.proj_ready, u + 1)
                            if u >= 2:
                                act.wait_ge(s.side_read, uses["squares", u - 2])
                                act.wait_ge(s.sum_ready, u - 1)
                                act.wait_ge(s.qk_done, u - 1)
                            for out in (raw, raw_high):
                                for n, gain in enumerate((q_gain, k_gain)):
                                    last = act.activation(out[:, u % 2, n * LEN:(n + 1) * LEN], proj_ps[:, n, :],
                                                          ACT.Copy, scale=gain)
                            last.then_inc(s.raw_ready, 1)
                            both = proj_ps[:, :, :].rearrange("p a t -> p (a t)")
                            act.activation(sq[:, u % 2, :], both, ACT.Square)
                            act.activation(sq_high[:, u % 2, :], both, ACT.Square).then_inc(s.sq_ready, 1)
                        for j, h in enumerate((2 * (t - lag), 2 * (t - lag) + 1)):
                            if 0 <= h < all_heads:
                                act.wait_ge(s.max_ready, h + 1)
                                if h >= 3:
                                    act.wait_ge(s.turned, h - 2)
                                for n, (q, a, b, at) in enumerate(segs):
                                    w = b - a
                                    last = act.activation(probs[0:rows, h % 3, at:at + w], sc[0:rows, h % 2, at:at + w],
                                                          ACT.Exp, bias=neg_max[0:rows, h, n:n + 1],
                                                          accum_out=sums[0:rows, h, n:n + 1])
                                last.then_inc(s.probs_ready, 1)
                                if kind == "bucket" and h % lot == lot - 1:
                                    act.activation(zero_key[:, h + 1 - lot:h + 1], neg_max[:, h + 1 - lot:h + 1, 0],
                                                   ACT.Exp).then_inc(s.extra_ready, 1)
                            if j == 0 and rotary and 1 <= t <= units:
                                u = t - 1
                                act.wait_ge(s.side_read, uses["squares", u])
                                order.step(act.activation(size[:, u % 2, :], size[:, u % 2, :], ACT.Ln,
                                                          scale=float(2 ** 20)))
                                act.activation(size[:, u % 2, :], size[:, u % 2, :], ACT.Exp, scale=-0.5,
                                               bias=net.w("k", "back")).then_inc(s.norm_ready, 1)

                @block.gpsimd
                def _(pool):
                    if rotary:
                        for t in range(units + 1):
                            if t >= 1:
                                u = t - 1
                                pool.wait_ge(s.side_read, uses["rot", u])
                                pool.wait_ge(s.cos_ready, u + 1)
                                pool.tensor_tensor(sind[:, u % 2, :], sind[:, u % 2, :], cosd[:, u % 2, :], ALU.add)\
                                    .then_inc(s.sum_ready, 1)
                            if t < units:
                                pool.wait_ge(s.raw_ready, t + 1)
                                pool.tensor_tensor(raw_rest[:, :], raw[:, t % 2, :],
                                                   raw_high[:, t % 2, :].bitcast(F32), ALU.subtract)\
                                    .then_inc(s.raw_split, 1)
                            if t < units:
                                pool.wait_ge(s.raw_split, t + 1)
                                pool.tensor_tensor(cosd[:, t % 2, :], raw[:, t % 2, :],
                                                   net.w("k", "qcos", 0, 2 * LEN), ALU.mult).then_inc(s.cos_ready, 1)
                                pool.wait_ge(s.sq_ready, t + 1)
                                if t >= 1:
                                    pool.wait_ge(s.side_read, uses["squares", t - 1])
                                pool.tensor_tensor(sq_rest[:, :], sq[:, t % 2, :],
                                                   sq_high[:, t % 2, :].bitcast(F32), ALU.subtract)\
                                    .then_inc(s.sq_split, 1)
                    if small:
                        for u in range(units):
                            shape = [P, 2, LEN]
                            c = u % pairs
                            pool.wait_ge(s.proj_read, projected(u))
                            if u >= 3:
                                pool.wait_ge(s.scores_ready, 2 * (u - 3) + 2)
                            pool.tensor_tensor(k_one[:, u % 3, :, :],
                                               qk[:, u // pairs % 3, 1, :].unsqueeze(1).to_broadcast(shape),
                                               net.w("k", "heads8", 2 * c, 2 * c + 2).unsqueeze(2)
                                               .to_broadcast(shape), ALU.mult).then_inc(s.k_spread, 1)

                @block.vector
                def _(dve):
                    order = Order(dve, s.vec_steps)

                    def read_projection(u):
                        c = 0 if small else u % pairs
                        slot = u // pairs % 3 if small else u % 3
                        dve.wait_ge(s.proj_ready, projected(u))
                        if small and u // pairs >= 3:
                            dve.wait_ge(s.scores_ready, (u // pairs - 2) * heads)
                        if not small and u >= 3:
                            dve.wait_ge(s.scores_ready, 2 * (u - 3) + 2)
                        at = 0
                        for a, b in pieces:
                            dve.tensor_scalar(qk[:, slot, 0, at:at + b - a], proj_ps[:, 0, a:b], bq[:, c:c + 1], scale,
                                              ALU.add, ALU.mult)
                            at += b - a
                        dve.tensor_scalar(qk[:, slot, 1, :], proj_ps[:, 1, :], bk[:, c:c + 1], None, ALU.add)\
                           .then_inc(s.proj_read if small else s.qk_done, 1)

                    def read_v(u):
                        r, n = u // pairs, v_piece(u)
                        cut = slice((n // 2) * v_w, (n // 2 + 1) * v_w)
                        dve.wait_ge(s.side_ready, uses["v", u])
                        if r >= 2:
                            dve.wait_ge(s.mixed, (r - 1) * heads)
                        outs = [(v_sb[:, r % 2, n % 2, cut], 0)]
                        if near and n % 2 == 0:
                            outs.append((v_half[:, r % 2, cut], near))
                        for out, first in outs:
                            if bv is None:
                                last = dve.tensor_copy(out, side_ps[first:P, 0:v_w])
                            else:
                                last = dve.tensor_tensor(out, side_ps[first:P, 0:v_w], bv[first:P, cut], ALU.add)
                        last.then_inc(s.side_read, 1)

                    def maxima(h):
                        dve.wait_ge(s.scores_ready, h + 1)
                        for n, (q, a, b, at) in enumerate(segs):
                            last = dve.tensor_reduce(neg_max[0:rows, h, n:n + 1], sc[0:rows, h % 2, at:at + b - a],
                                                     AX, ALU.max, negate=True)
                            if kind == "bucket" and q == 0:
                                order.step(last)
                                dve.tensor_scalar(neg_max[:, h, 0:1], neg_max[:, h, 0:1], net.w("k", "floor"), None,
                                                  ALU.min)
                        last.then_inc(s.max_ready, 1)

                    def copy_turned(h):
                        dve.wait_ge(s.turned, h + 1)
                        if h >= 3:
                            dve.wait_ge(s.mixed, h - 2)
                        last = dve.tensor_copy(turned[:, h % 3, 0:whole * rows], tp[:, h % 2, 0:whole * rows])
                        for n, (_, _, first, _) in enumerate(blocks[whole:], whole):
                            last = dve.tensor_copy(turned[0:P - first, h % 3, n * rows:(n + 1) * rows],
                                                   tp[0:P - first, h % 2, n * rows:(n + 1) * rows])
                        last.then_inc(s.turned_read, 1)

                    def scale_out(g):
                        mine = sums[0:rows, g * lot:(g + 1) * lot, 0:tiles]
                        dve.wait_ge(s.mixed, (g + 1) * lot)
                        if kind == "bucket":
                            dve.wait_ge(s.extra_ready, g + 1)
                            order.step(dve.scalar_tensor_tensor(
                                out=mine[:, :, 0], in0=zero_key[:, g * lot:(g + 1) * lot], scalar=net.w("k", "extra"),
                                in1=mine[:, :, 0], op0=ALU.mult, op1=ALU.add))
                        order.step(dve.reciprocal(mine, mine))
                        if g >= 2:
                            dve.wait_ge(s.out_turned, g - 1)
                        shape = [rows, tiles, lot, dim]
                        part = op[0:rows, g % 2, 0:tiles * P].rearrange("p (q h d) -> p q h d", q=tiles, h=lot)
                        out = o_sb[0:rows, g % 2, 0:tiles, :].rearrange("p q (h d) -> p q h d", h=lot)
                        over = mine.rearrange("p h q -> p q h").unsqueeze(3).to_broadcast(shape)
                        done = dve.tensor_tensor(out, part, over, ALU.mult)
                        done.then_inc(s.out_scaled, 1)

                    def copy_out(g):
                        dve.wait_ge(s.out_turned, g + 1)
                        r, c = g // (lots // seqs), g % (lots // seqs)
                        dve.tensor_copy(o_t[:, r % 2, c, 0:tiles * rows],
                                        op[:, g % 2, 2 * P:2 * P + tiles * rows]).then_inc(s.out_copied, 1)

                    def add_out(r):
                        dve.wait_ge(s.side_ready, uses["out", r])
                        at, before = 0, 0

                        def to(a, b):
                            return dst[:, r * LEN + a:][:, bass.ds(i * (seqs * LEN), b - a)]

                        for a, b in pieces:
                            if a > before:
                                dve.tensor_scalar(to(before, a), to(before, a), bo, None, ALU.add)
                            part = side_ps[:, at:at + b - a]
                            if bo is None:
                                last = dve.tensor_tensor(to(a, b), to(a, b), part, ALU.add)
                            else:
                                last = dve.scalar_tensor_tensor(out=to(a, b), in0=part, scalar=bo, in1=to(a, b),
                                                                op0=ALU.add, op1=ALU.add)
                            at, before = at + b - a, b
                        last.then_inc(s.side_read, 1)
                        if before < LEN:
                            dve.tensor_scalar(to(before, LEN), to(before, LEN), bo, None, ALU.add)

                    at = i * (seqs * LEN)
                    flat = xs[:, :, :].rearrange("p s t -> p (s t)")
                    if rotary:
                        dve.tensor_copy(rot_and_pairs[:, 0:P], net.w("k", "rot"))
                        dve.tensor_copy(rot_and_pairs[:, P:], net.w("k", "pairs"))
                        dve.tensor_copy(flat[0:64, :], src[0:64, bass.ds(at, seqs * LEN)])
                        order.step(dve.tensor_copy(flat[64:P, 1:], src[64:P, bass.ds(at, seqs * LEN - 1)]))
                        dve.memset(xs[64:P, :, 0:1], 0.0).then_inc(s.x_ready, 1)
                    else:
                        dve.tensor_copy(flat, src[:, bass.ds(at, seqs * LEN)]).then_inc(s.x_ready, 1)
                    for t in range(turns):
                        if rotary and 0 <= t - 2 < units:
                            u = t - 2
                            dve.wait_ge(s.norm_ready, u + 1)
                            dve.wait_ge(s.sum_ready, u + 1)
                            if u >= 3:
                                dve.wait_ge(s.scores_ready, 2 * (u - 3) + 2)
                            dve.tensor_tensor(qk[:, u % 3, :, :].rearrange("p a t -> p (a t)"), sind[:, u % 2, :],
                                              size[:, u % 2, :], ALU.mult).then_inc(s.qk_done, 1)
                        if t < units:
                            if projects(t) and not rotary:
                                read_projection(t)
                        if rotary and 1 <= t <= units:
                            u = t - 1
                            dve.wait_ge(s.side_ready, uses["rot", u])
                            dve.tensor_tensor(sind[:, u % 2, :], side_ps[:, :], net.w("k", "qsin", 0, 2 * LEN),
                                              ALU.mult).then_inc(s.side_read, 1)
                        for j, h in enumerate((2 * (t - lag), 2 * (t - lag) + 1)):
                            if 0 <= h <= last_step:
                                if h < all_heads:
                                    maxima(h)
                                if 0 <= h - 2 < all_heads:
                                    copy_turned(h - 2)
                                if lot_at(h, 0) is not None:
                                    scale_out(lot_at(h, 0))
                                if lot_at(h, 1) is not None:
                                    copy_out(lot_at(h, 1))
                                if closes(lot_at(h, 2)) is not None:
                                    add_out(closes(lot_at(h, 2)))
                            if j == 0 and rotary and 1 <= t <= units:
                                dve.wait_ge(s.side_ready, uses["squares", u])
                                dve.tensor_scalar(size[:, u % 2, :], side_ps[:, :], 1e-24, None, ALU.max)\
                                   .then_inc(s.side_read, 1)
                        if t < units and v_piece(t) is not None:
                            read_v(t)
            nc.all_engine_barrier(sems_to_clear=span(s))


def selective_scan(net, src, dst):
    nc = net.nc
    s = net.signals("scan", [
        "rates_ready", "x_ready", "in_ready", "conv_done", "z_done", "x_acted", "low_ready", "low_copied",
        "high_ready", "split_done", "dt_ready", "dt_biased", "dt_steps", "delta_ready", "rows_ready", "driven",
        "decay_ready", "c_copied", "scanned", "hc_ready", "summed", "skipped", "gated", "out_ready", "steps"])
    C, R = D_INNER // P, 2
    T = R * LEN
    with ExitStack() as ctx:
        xi = net.sbuf("m_xi", [P, C, T], ctx=ctx)
        z = net.sbuf("m_z", [P, C, T], ctx=ctx)
        high = net.sbuf("m_high", [STATE, 2, T], F32R, ctx=ctx)
        rest = net.sbuf("m_rest", [STATE, 2, T], F32R, ctx=ctx)
        spread = net.sbuf("m_spread", [STATE, P], F32R, ctx=ctx)
        delta = net.sbuf("m_delta", [P, C, T], ctx=ctx)
        dx = net.sbuf("m_dx", [P, C, T], ctx=ctx)
        decay = net.sbuf("m_decay", [P, 2, C, R, LEN], ctx=ctx)
        drive = net.sbuf("m_drive", [P, 2, C * T], ctx=ctx)
        state = net.sbuf("m_state", [P, 2, C, T], ctx=ctx)
        c_sb = net.sbuf("m_c", [P, 2, T], ctx=ctx)
        hc = net.sbuf("m_hc", [P, 2, C, T], ctx=ctx)
        rates = net.sbuf("m_rates", [P, C * STATE], ctx=ctx)
        pad_w = LEN + 4
        padded = drive[:, :, :].rearrange("p b n -> p (b n)")[:, 0:C * R * pad_w]\
            .rearrange("p (c r t) -> p c r t", c=C, r=R)
        conv, soft = hc[:, 0, :, :], hc[:, 1, :, :]
        pre = dx
        y = state[:, 0, :, :]
        xs, low = state[:, 0, 0, :], state[0:DT_RANK, 1, 0, :]
        a_ps = net.psum("m_aps", [P, C, T], ctx)
        rows_ps = net.psum("m_rps", [P, 4, T], ctx)
        low_ps = net.psum("m_lps", [P, T], ctx)

        def by_seq(t, c):
            return t[:, c, :].rearrange("p (r t) -> p r t", r=R)

        with nc.Block(no_gpsimd_drain=True) as block:
            @block.scalar
            def _(act):
                act.activation(rates[:, :], net.w("m", "alog"), ACT.Exp).then_inc(s.rates_ready, 1)

            @block.vector
            def _(dve):
                dve.wait_ge(s.rates_ready, 1)
                dve.tensor_scalar(rates[:, :], rates[:, :], -1.0, None, ALU.mult)
                dve.memset(decay[:, :, :, :, 0:1].rearrange("p b c r o -> p (b c r) o"), 0.0)
                dve.tensor_copy(spread[:, :], net.w("k", "ident", rows=STATE))
        nc.all_engine_barrier(sems_to_clear=span(s))

        with nc.Fori(0, SEQS // R) as i:
            with nc.Block(no_gpsimd_drain=True) as block:
                @block.tensor
                def _(pe):
                    pe.wait_ge(s.x_ready, 1)
                    for n in range(2 * C):
                        to = a_ps[:, n, :] if n < C else rows_ps[:, n - C, :]
                        pe.matmul(to, net.w("m", "win", n * P, (n + 1) * P), xs, start=True, stop=True)\
                          .then_inc(s.in_ready, 1)
                    pe.wait_ge(s.x_acted, C)
                    wx = net.w("m", "wx").rearrange("p (c n) -> p c n", c=C)
                    for out, a, b in ((low_ps[0:DT_RANK, :], 0, DT_RANK),
                                      (rows_ps[0:STATE, 2, :], DT_RANK, DT_RANK + STATE),
                                      (rows_ps[0:STATE, 3, :], DT_RANK + STATE, DT_RANK + 2 * STATE)):
                        for c in range(C):
                            last = pe.matmul(out, wx[:, c, a:b], xi[:, c, :], start=(c == 0), stop=(c == C - 1))
                        last.then_inc(s.low_ready, 1)
                    pe.wait_ge(s.low_copied, 1)
                    for c in range(C):
                        pe.matmul(a_ps[:, c, :], net.w("m", "wdt", c * P, (c + 1) * P, rows=DT_RANK),
                                  low, start=True, stop=True).then_inc(s.dt_ready, 1)
                    pe.wait_ge(s.z_done, C)
                    pe.wait_ge(s.split_done, 2)
                    pe.wait_ge(s.dt_biased, C)

                    def add_up(n):
                        pe.wait_ge(s.hc_ready, n + 1)
                        for c in range(C):
                            last = pe.matmul(a_ps[:, c, :], net.w("k", "ident"), hc[:, n % 2, c, :],
                                             start=(n == 0), stop=(n == STATE - 1))
                        last.then_inc(s.summed, 1)

                    for n in range(STATE):
                        if n >= 2:
                            pe.wait_ge(s.driven, n - 1)
                            pe.wait_ge(s.c_copied, n - 1)
                        row = spread[:, n:n + 1].to_broadcast([STATE, P])
                        for m in range(2):
                            pe.matmul(rows_ps[:, 2 * (n % 2) + m, :], row, high[:, m, :], start=True, stop=False)
                            last = pe.matmul(rows_ps[:, 2 * (n % 2) + m, :], row, rest[:, m, :],
                                             start=False, stop=True)
                        last.then_inc(s.rows_ready, 1)
                        if n >= 3:
                            add_up(n - 3)
                    for n in range(STATE - 3, STATE):
                        add_up(n)
                    for c in range(C):
                        pe.wait_ge(s.gated, c + 1)
                        last = pe.matmul(low_ps[:, :], net.w("m", "wout", c * P, (c + 1) * P), y[:, c, :],
                                         start=(c == 0), stop=(c == C - 1))
                    last.then_inc(s.out_ready, 1)

                @block.scalar
                def _(act):
                    for c in range(C):
                        act.wait_ge(s.in_ready, C + c + 1)
                        act.activation(z[:, c, :], rows_ps[:, c, :], ACT.Silu).then_inc(s.z_done, 1)
                    for c in range(C):
                        act.wait_ge(s.conv_done, c + 1)
                        act.activation(xi[:, c, :], conv[:, c, :], ACT.Silu, bias=net.w("m", "cb", c, c + 1))\
                           .then_inc(s.x_acted, 1)
                    nc.scalar.preload_act_table_set("natural_log_exp_and_others")
                    for m in range(2):
                        act.wait_ge(s.low_ready, 2 + m)
                        act.activation(high[:, m, :], rows_ps[0:STATE, 2 + m, :], ACT.Copy)\
                           .then_inc(s.high_ready, 1)
                    order = Order(act, s.dt_steps)
                    act.wait_ge(s.dt_biased, C)
                    order.step(act.activation(soft, pre[:, :, :], ACT.Abs))
                    order.step(act.activation(soft, soft, ACT.Exp, scale=-1.0))
                    order.step(act.activation(soft, soft, ACT.Ln, bias=net.w("k", "one")))
                    act.wait_ge(s.delta_ready, 1)
                    for n in range(STATE):
                        if n >= 2:
                            act.wait_ge(s.scanned, n - 1)
                        for c in range(C):
                            last = act.activation(decay[:, n % 2, c, :, 1:LEN], by_seq(delta, c)[:, :, 1:LEN],
                                                  ACT.Exp, scale=rates[:, c * STATE + n:c * STATE + n + 1])
                        last.then_inc(s.decay_ready, 1)
                        act.wait_ge(s.rows_ready, n + 1)
                        if n >= 2:
                            act.wait_ge(s.hc_ready, n - 1)
                        act.activation(c_sb[:, n % 2, :], rows_ps[:, 2 * (n % 2) + 1, :], ACT.Copy)\
                           .then_inc(s.c_copied, 1)

                @block.gpsimd
                def _(pool):
                    for n in range(STATE):
                        b = n % 2
                        pool.wait_ge(s.scanned, n + 1)
                        pool.wait_ge(s.c_copied, n + 1)
                        if n >= 2:
                            pool.wait_ge(s.summed, n - 1)
                        pool.tensor_tensor(hc[:, b, :, :], state[:, b, :, :],
                                           c_sb[:, b, :].unsqueeze(1).to_broadcast([P, C, T]), ALU.mult)\
                            .then_inc(s.hc_ready, 1)
                    for c in range(C):
                        pool.wait_ge(s.skipped, c + 1)
                        pool.tensor_tensor(y[:, c, :], y[:, c, :], z[:, c, :], ALU.mult).then_inc(s.gated, 1)

                @block.vector
                def _(dve):
                    order = Order(dve, s.steps)
                    dve.tensor_copy(xs, src[:, bass.ds(i * T, T)]).then_inc(s.x_ready, 1)
                    dve.memset(padded[:, :, :, 0:3].rearrange("p c r t -> p (c r) t"), 0.0)
                    for c in range(C):
                        dve.wait_ge(s.in_ready, c + 1)
                        order.step(dve.tensor_copy(padded[:, c, :, 3:3 + LEN], by_seq(a_ps, c)))
                    for j in range(4):
                        for c in range(C):
                            tap = net.w("m", "cw", c * 4 + j, c * 4 + j + 1)
                            there, out = padded[:, c, :, j:j + LEN], by_seq(conv, c)
                            if j == 0:
                                ins = dve.tensor_scalar(out, there, tap, None, ALU.mult)
                            else:
                                ins = dve.scalar_tensor_tensor(out=out, in0=there, scalar=tap, in1=out,
                                                               op0=ALU.mult, op1=ALU.add)
                            if j == 3:
                                ins.then_inc(s.conv_done, 1)
                            elif c == C - 1:
                                order.step(ins)
                    dve.wait_ge(s.low_ready, 1)
                    dve.tensor_copy(low, low_ps[0:DT_RANK, :]).then_inc(s.low_copied, 1)
                    for m in range(2):
                        dve.wait_ge(s.high_ready, m + 1)
                        dve.tensor_tensor(rest[:, m, :], rows_ps[0:STATE, 2 + m, :],
                                          high[:, m, :].bitcast(F32), ALU.subtract).then_inc(s.split_done, 1)
                    for c in range(C):
                        dve.wait_ge(s.dt_ready, c + 1)
                        dve.tensor_scalar(pre[:, c, :], a_ps[:, c, :], net.w("m", "bdt", c, c + 1), None, ALU.add)\
                           .then_inc(s.dt_biased, 1)
                    dve.wait_ge(s.dt_biased, C)
                    dve.wait_ge(s.dt_steps, 3)
                    dve.scalar_tensor_tensor(out=delta[:, :, :], in0=pre[:, :, :], scalar=0.0, in1=soft,
                                             op0=ALU.max, op1=ALU.add).then_inc(s.delta_ready, 1)
                    dve.wait_ge(s.delta_ready, 1)
                    dve.wait_ge(s.x_acted, C)
                    order.step(dve.tensor_tensor(dx[:, :, :], delta[:, :, :], xi[:, :, :], ALU.mult))

                    def driven(n):
                        dve.wait_ge(s.rows_ready, n + 1)
                        dve.tensor_tensor(drive[:, n % 2, :].rearrange("p (c t) -> p c t", c=C), dx[:, :, :],
                                          rows_ps[:, 2 * (n % 2), :].unsqueeze(1).to_broadcast([P, C, T]), ALU.mult)\
                           .then_inc(s.driven, 1)

                    driven(0)
                    for n in range(STATE):
                        b = n % 2
                        if n >= 1:
                            dve.wait_ge(s.scanned, n)
                        if n + 1 < STATE:
                            driven(n + 1)
                        dve.wait_ge(s.driven, n + 1)
                        dve.wait_ge(s.decay_ready, n + 1)
                        if n >= 2:
                            dve.wait_ge(s.hc_ready, n - 1)
                        dve.tensor_tensor_scan(state[:, b, :, :].rearrange("p c t -> p (c t)"),
                                               decay[:, b, :, :, :].rearrange("p c r t -> p (c r t)"),
                                               drive[:, b, :], 0.0, ALU.mult, ALU.add).then_inc(s.scanned, 1)
                    dve.wait_ge(s.summed, STATE)
                    for c in range(C):
                        dve.scalar_tensor_tensor(out=y[:, c, :], in0=xi[:, c, :],
                                                 scalar=net.w("m", "dskip", c, c + 1), in1=a_ps[:, c, :],
                                                 op0=ALU.mult, op1=ALU.add).then_inc(s.skipped, 1)
                    dve.wait_ge(s.out_ready, 1)
                    to = dst[:, bass.ds(i * T, T)]
                    dve.tensor_tensor(to, to, low_ps[:, :], ALU.add)
            nc.all_engine_barrier(sems_to_clear=span(s))


def model(nc, x_in, blobs, out, stages):
    with ExitStack() as ctx:
        net = Net(nc, ctx)
        X = net.sbuf("X", [P, TOK])
        H = net.sbuf("H", [P, TOK])
        G = net.sbuf("G", [P, TOK])
        width = {g: starts(g)[1] for g in COLS}
        net.weights = {g: net.sbuf(f"w_{g}", [P, width[g]]) for g in COLS if g not in "ehq"}
        region = net.sbuf("w_experts", [P, max(width["e"], width["h"])])
        net.weights["e"] = net.weights["h"] = region
        net.ident16 = net.sbuf("ident16", [P, P], BF16)
        masks = {m: net.sbuf(f"mask_{m}", [P, width], BF16) for m, width in COLS["q"].items()}
        loaded = ctx.enter_context(nc.semaphore("loaded"))
        early_loaded = ctx.enter_context(nc.semaphore("early_loaded"))
        experts_loaded = ctx.enter_context(nc.semaphore("experts_loaded"))
        stored = ctx.enter_context(nc.semaphore("stored"))

        def load(sp, g, sem):
            sp.dma_start(net.weights[g][:, 0:width[g]], blobs[g]).then_inc(sem, 16)

        early = ["q", "a", "f"]
        late = ["m", "g", "c", "d"]
        masks_in = ctx.enter_context(ExitStack())
        net.weights["q"] = net.sbuf("w_q", [P, width["q"]], ctx=masks_in)
        with nc.Block() as block:
            @block.sync
            def _(sp):
                load(sp, "k", loaded)
                sp.dma_start(X[:, :], x_in).then_inc(loaded, 16)
                for g in early:
                    load(sp, g, early_loaded)
                for g in late:
                    load(sp, g, experts_loaded)
                load(sp, "e" if "M" in stages else "h", experts_loaded)
                sp.wait_ge(loaded, 32)

            @block.vector
            def _(dve):
                dve.wait_ge(loaded, 32)
                dve.tensor_copy(net.ident16[:, :], net.w("k", "ident"))

        def first_ready():
            with nc.Block(no_gpsimd_drain=True) as block:
                @block.vector
                def _(dve):
                    dve.wait_ge(early_loaded, 16 * len(early))
                    for m, t in masks.items():
                        dve.tensor_copy(t[:, :], net.w("q", m))
            nc.all_engine_barrier()
            masks_in.close()

        def wait_experts(n):
            with nc.Block(no_gpsimd_drain=True) as block:
                @block.sync
                def _(sp):
                    sp.wait_ge(experts_loaded, n)

        def stage_a(here):
            norm(net, "a1", H, G, gain=net.w("a", "g1"), bias=net.w("a", "c1"))
            w = net.w("a", "wqkv")
            attention(net, "bucket", G, H, masks["m_bucket"], A_DIM ** -0.5, w[:, 0:P], w[:, P:2 * P],
                      w[:, 2 * P:3 * P], net.w("a", "wo"), net.w("a", "bq"), net.w("a", "bk"),
                      net.w("a", "bv"), net.w("a", "bo"))
            norm(net, "a2", H, G, gain=net.w("a", "g2"), bias=net.w("a", "c2"))
            mixture(net, G, X, net.w("a", "w"), [(1, 4, 1, None)], also=H, func=ACT.Gelu, gated=False,
                    gate_bias=net.w("a", "b1"), out_bias=net.w("a", "b2"))

        def stage_f(here):
            for l in (0, 1):
                inner = F_HEADS * F_DIM
                w = net.w("f", f"wqkv{l}")
                attention(net, "local", H, H, masks["m_local"], None, w[:, 0:inner], w[:, inner:2 * inner],
                          w[:, 2 * inner:], net.w("f", f"wo{l}"), q_gain=net.w("f", f"qs{l}"),
                          k_gain=net.w("f", f"ks{l}"))
                norm(net, f"f{l}", H, G, gain=net.w("f", f"g{l}"), bias=net.w("f", f"c{l}"), shift=True)
                more = dict(func=ACT.Gelu, gate_bias=net.w("f", f"bg{l}"), up_bias=net.w("f", f"ba{l}"),
                            out_bias=net.w("f", f"b2{l}"))
                if l == 0:
                    mixture(net, G, H, net.w("f", "w0"), [(1, LOTS_F, 1, None)], **more)
                else:
                    mixture(net, G, X, net.w("f", "w1"), [(1, LOTS_F, 1, None)], also=H, **more)

        def stage_m(here):
            norm(net, "m1", H, G, root_mean_square=True, gain=net.w("m", "r1"))
            selective_scan(net, G, H)
            norm(net, "m2", H, G, root_mean_square=True, gain=net.w("m", "r2"))
            high = net.sbuf("share_high", [N_EXP, TOK], F32R, ctx=here)
            rest = net.sbuf("share_rest", [N_EXP, TOK], F32R, ctx=here)
            gate(net, G, high, rest, N_EXP)
            taken = 2
            halves = FFN // P // 2

            def column(i, e):
                row = net.w("k", "ident", rows=N_EXP)[:, e // halves:][:, bass.ds(i * taken, 1)]
                return row.to_broadcast([N_EXP, P])

            mixture(net, G, X, net.w("e", "w"), [(N_EXP // taken, taken * halves, 2, column)], high, rest, also=H)

        def stage_c(here):
            attention(net, "window", H, X, masks["m_window"], A_DIM ** -0.5, net.w("c", "wq"), net.w("c", "wk"),
                      net.w("c", "wv"), net.w("c", "wo"), net.w("c", "bq"), net.w("c", "bk"),
                      net.w("c", "bv"), net.w("c", "bo"))

        def stage_h(here):
            high = net.sbuf("share_high", [E2, TOK], F32R, ctx=here)
            rest = net.sbuf("share_rest", [E2, TOK], F32R, ctx=here)
            gate(net, H, high, rest, E2)
            routed = ROUTED // P
            turns = 2

            def columns(i, e):
                return net.w("h", "expert", rows=E2)[:, e * P:][:, bass.ds(i * (routed // turns * P), P)]

            mixture(net, H, X, net.w("h", "w"), [(turns, routed // turns, 1, columns), (1, LOTS2 - routed, 1, None)],
                    high, rest)

        def stage_d(here):
            attention(net, "causal", H, X, masks["m_causal"], D_DIM ** -0.5, net.w("d", "wq"), net.w("d", "wk"),
                      net.w("d", "wv"), net.w("d", "wo"), net.w("d", "bq"), net.w("d", "bk"),
                      net.w("d", "bv"), net.w("d", "bo"))

        came = 16 * (len(late) + 1)
        for n, st in enumerate(stages):
            norm(net, f"{st}{n}", X, H)
            if n == 0:
                first_ready()
            if n == min([stages.find(k) for k in "MCHD" if k in stages] or [99]):
                wait_experts(came)
            with ExitStack() as here:
                dict(A=stage_a, F=stage_f, M=stage_m, C=stage_c, H=stage_h, D=stage_d)[st](here)
            if st == "M":
                with nc.Block(no_gpsimd_drain=True) as block:
                    @block.sync
                    def _(sp):
                        load(sp, "h", experts_loaded)
                came += 16
                second = came
            if "M" in stages[:n + 1] and stages[n + 1:n + 2] == "H":
                wait_experts(second)

        with nc.Block() as block:
            @block.sync
            def _(sp):
                sp.dma_start(out, X[:, :]).then_inc(stored, 16)
                sp.wait_ge(stored, 16)



def _rows(a, n=P):
    a = np.asarray(a, np.float32)
    return np.concatenate([a, np.zeros((n - a.shape[0],) + a.shape[1:], np.float32)]) if a.shape[0] < n else a


def _col(b):
    b = np.asarray(b, np.float32).reshape(-1)
    n = -(-b.size // P)
    return np.ascontiguousarray(_rows(b, n * P).reshape(n, P).T)


def _stack(w):
    w = np.asarray(w, np.float32)
    k = -(-w.shape[0] // P)
    return np.ascontiguousarray(_rows(w, k * P).reshape(k, P, -1).transpose(1, 0, 2)).reshape(P, -1)


def _lots(gate, up, down):
    n = -(-gate.shape[1] // P)
    parts = [_rows(w.T, n * P).T.reshape(P, n, P) for w in (gate, up) if w is not None]
    parts.append(_rows(down, n * P).reshape(n, P, P).transpose(1, 0, 2))
    return np.ascontiguousarray(np.stack(parts, 2)).reshape(P, -1)


def _wide(b):
    return np.ascontiguousarray(np.broadcast_to(np.asarray(b, np.float32).reshape(1, -1), (P, np.size(b))))


def _constants():
    f = np.float32
    ident = np.eye(P, dtype=f)
    blocks = np.kron(np.eye(2, dtype=f), np.ones((64, 64), f))
    half = np.zeros((64, 64), f)
    for d in range(32):
        half[d + 32, d] = -1.0
        half[d, d + 32] = 1.0
    rot = np.kron(np.eye(2, dtype=f), half)
    idx = np.arange(0, F_DIM, 2, dtype=f)
    inv_freq = (f(1.0) / np.power(f(10000.0), idx / f(F_DIM))).astype(f)
    t = np.arange(LEN, dtype=f)
    freqs = (t[:, None] * inv_freq[None, :]).astype(f)
    base = ((idx + f(0.4 * F_DIM)) / f(1.4 * F_DIM)).astype(f)
    power = ((t - LEN // 2) / f(32.0)).astype(f)
    sc = np.power(base[None, :], power[:, None]).astype(f)
    cos, sin = np.cos(freqs).astype(f), np.sin(freqs).astype(f)

    def table(a):
        return np.ascontiguousarray(np.tile(np.concatenate([a, a], 1), (1, 2)).T.astype(f))

    qs = f(8.0)
    q = np.arange(P)[:, None]
    k = np.arange(P)[None, :]

    def lay(rule, near=P // 2):
        first = np.where(rule(q, k), 0.0, MASKED)
        second = np.where(rule(q + P, np.arange(near, LEN)[None, :]), 0.0, MASKED)
        return np.concatenate([first, second], 1).astype(f)

    def win(i, j):
        first = (i >= 1) & (i <= 32) & (j >= 1) & (j <= 32)
        second = (i >= 129) & (i <= 160) & (j >= 129) & (j <= 160)
        return (i == 0) | first | second

    tok = np.concatenate([np.arange(a, b) for a, b in SEEN])
    m_window = np.full((P, LEN), MASKED, f)
    m_window[:len(tok), :LEN] = np.where(win(tok[:, None], np.arange(LEN)[None, :]), 0.0, MASKED)
    in_first = np.arange(P) < 64

    def before(n):
        return np.tile((np.arange(n)[None, :] < np.arange(n)[:, None]).astype(f).reshape(1, -1), (P, 1))

    masks = dict(m_bucket=lay(lambda i, j: (j <= i) & (j // 64 >= i // 64 - 1)),
                 m_local=lay(lambda i, j: (j <= i) & (i <= j + 64)),
                 m_causal=lay(lambda i, j: j <= i, 0), m_window=m_window)
    return masks, dict(
        ident=ident, mean=np.full((P, P), 1.0 / P, f), pairs=blocks, rot=rot,
        qcos=table(cos * sc * qs), qsin=table(sin * sc * qs), kcos=table(cos / sc), ksin=table(sin / sc),
        heads8=(np.arange(P)[:, None] // 8 == np.arange(16)[None, :]).astype(f),
        floor=np.where(in_first, 0.0, 3e38).astype(f)[:, None],
        extra=np.where(in_first, 64.0, 0.0).astype(f)[:, None],
        eps=np.full((P, 1), EPS, f), one=np.ones((P, 1), f), back=np.full((P, 1), 10 * np.log(2.0), f),
        before16=before(16))


def _layout(v):
    masks, constants = _constants()
    out = {"k": constants, "q": masks}
    a = {n[len("L0_attn_a_"):]: x for n, x in v.items() if n.startswith("L0_attn_a_")}
    out["a"] = dict(g1=_col(a["ln1_g"]), c1=_col(a["ln1_b"]), wqkv=a["w_qkv"], bq=_col(a["b_qkv"][:P]),
                    bk=_col(a["b_qkv"][P:2 * P]), bv=_wide(a["b_qkv"][2 * P:]), wo=a["w_out"], bo=_col(a["b_out"]),
                    g2=_col(a["ln2_g"]), c2=_col(a["ln2_b"]), w=_lots(a["w1"], None, a["w2"]), b1=_col(a["b1"]),
                    b2=_col(a["b2"]))
    f = {n[len("L0_ffn_"):]: x for n, x in v.items() if n.startswith("L0_ffn_")}
    out["f"] = {}
    for l in (0, 1):
        twice = lambda g: _col(np.concatenate([g, g]))
        out["f"].update({
            f"wqkv{l}": f["wqkv"][l], f"qs{l}": twice(f["q_scale"][l]), f"ks{l}": twice(f["k_scale"][l]),
            f"wo{l}": _stack(f["wo"][l]), f"g{l}": _col(f["ln_g"][l]), f"c{l}": _col(f["ln_b"][l]),
            f"w{l}": _lots(f["w1"][l][:, HID_F:], f["w1"][l][:, :HID_F], f["w2"][l]),
            f"ba{l}": _col(f["b1"][l][:HID_F]), f"bg{l}": _col(f["b1"][l][HID_F:]),
            f"b2{l}": _col(f["b2"][l])})
    m = {n[len("L0_attn_b_"):]: x for n, x in v.items() if n.startswith("L0_attn_b_")}
    out["m"] = dict(r1=_col(m["rms1_w"]), r2=_col(m["rms2_w"]), win=m["in_proj_w"],
                    cw=_stack(m["conv_w"].reshape(D_INNER, 4)), cb=_col(m["conv_b"]), wx=_stack(m["x_proj_w"]),
                    wdt=_rows(m["dt_proj_w"]), bdt=_col(m["dt_proj_b"]), alog=_stack(m["A_log"]),
                    dskip=_col(m["D_skip"]), wout=_stack(m["out_proj_w"]), router=m["router_w"])
    out["e"] = dict(w=_lots(m["Wg"].transpose(1, 0, 2).reshape(P, -1), m["Wu"].transpose(1, 0, 2).reshape(P, -1),
                            m["Wd"].reshape(-1, P)))
    h = {n[len("L1_ffn_"):]: x for n, x in v.items() if n.startswith("L1_ffn_")}
    out["h"] = dict(
        w=_lots(np.concatenate([h["gate_proj"].reshape(-1, P).T, h["shared_gate_w"].T], 1),
                np.concatenate([h["up_proj"].reshape(-1, P).T, h["shared_up_w"].T], 1),
                np.concatenate([h["down_proj"].transpose(0, 2, 1).reshape(-1, P), h["shared_down_w"].T], 0)),
        expert=_rows((np.arange(ROUTED)[None, :] // I2 == np.arange(E2)[:, None]).astype(np.float32)))
    out["g"] = dict(gate=h["gate_w"].T, bias=_wide(h["gate_bias"]))
    c = {n[len("L1_attn_a_"):]: x for n, x in v.items() if n.startswith("L1_attn_a_")}
    out["c"] = dict(wq=c["Wq"], wk=c["Wk"], wv=c["Wv"], wo=c["Wo"], bq=_col(c["bq"]), bk=_col(c["bk"]),
                    bv=_wide(c["bv"]), bo=_col(c["bo"]))
    d = {n[len("L1_attn_b_"):]: x for n, x in v.items() if n.startswith("L1_attn_b_")}
    flat = lambda w: w.transpose(1, 0, 2).reshape(P, -1)
    out["d"] = dict(wq=flat(d["W_Q"]), wk=flat(d["W_K"]), wv=flat(d["W_V"]),
                    wo=_stack(d["W_O"].reshape(-1, P)), bq=_col(d["b_Q"]), bk=_col(d["b_K"]), bv=_wide(d["b_V"]),
                    bo=_col(d["b_O"]))
    return out


def _arrays(inputs):
    v = {n: np.asarray(x) for n, x in inputs.items()}
    got = _layout(v)
    arrays = {"x_dram": np.ascontiguousarray(v["L0_attn_a_x"].reshape(TOK, P).T)}
    for g, parts in COLS.items():
        arrays[f"w_{g}_dram"] = np.ascontiguousarray(np.concatenate([got[g][n] for n in parts], 1))
        assert arrays[f"w_{g}_dram"].shape == (P, starts(g)[1]), g
    return arrays


STAGES = "AFMFCHDH"


def kernel(**inputs):
    import concourse.bacc as _bacc
    from concourse.bass_utils import run_bass_kernel_spmd as _launch

    arrays = _arrays(inputs)
    nc = _bacc.Bacc("TRN2", target_bir_lowering=False, num_devices=1)
    dram = {n: nc.dram_tensor(n, a.shape, F32, kind="ExternalInput").ap() for n, a in arrays.items()}
    out = nc.dram_tensor("out_dram", (P, TOK), F32, kind="ExternalOutput").ap()
    model(nc, dram["x_dram"], {g: dram[f"w_{g}_dram"] for g in COLS}, out, STAGES)
    r = _launch(nc, [arrays], core_ids=[0])
    return np.ascontiguousarray(r.results[0]["out_dram"].T).reshape(SEQS, LEN, P)
```
